# Optimizing a Trainium2 kernel written in Bass

```python
import numpy as np
import jax
import jax.numpy as jnp

def _softmax(x, axis=-1):
    return jax.nn.softmax(x, axis=axis)

def _gelu(x):
    return jax.nn.gelu(x, approximate=True)

def _silu(x):
    return jax.nn.silu(x)

def _sigmoid(x):
    return jax.nn.sigmoid(x)

def _layernorm(x, axis=-1, eps=1e-05):
    m = jnp.mean(x, axis=axis, keepdims=True)
    v = jnp.var(x, axis=axis, keepdims=True)
    return (x - m) / jnp.sqrt(v + eps)

def _scatter_add(tgt, idx, src, axis=0):
    return tgt.at[idx].add(src)

def _segment_sum(src, seg, n):
    return jax.ops.segment_sum(src, seg, n)
kernel_name = 'mk_gps_d2_gnn_r8_c72fd4'

def setup_inputs(seed: int=0):
    np.random.seed(seed)
    _w = jnp.asarray

    def _rec_inputs():
        import jax
        import jax.numpy as jnp
        _gk = jax.random.key(seed)
        x = -0.0003713 + 1 * jax.random.normal(jax.random.fold_in(_gk, 1), (6250, 256), jnp.float32)
        _s = jax.random.randint(jax.random.fold_in(_gk, 2), (100000,), 0, 6250, jnp.int32)
        _d = jax.random.randint(jax.random.fold_in(_gk, 3), (100000,), 0, 6250, jnp.int32)
        _loop = jnp.arange(6250, dtype=jnp.int32)
        src = jnp.concatenate([_s, _d, _loop])
        dst = jnp.concatenate([_d, _s, _loop])
        _o = jnp.argsort(dst, stable=True)
        src = src[_o]
        dst = dst[_o]
        return (x, src, dst)
    x, src, dst = _rec_inputs()

    def _L0_gnn_setup():
        import jax, jax.numpy as jnp
        import numpy as np
        N, E, H, D = (6250, 100000, 4, 64)
        IN_DIM = H * D
        NEG_SLOPE = 0.2
        key = jax.random.key(seed)
        k = jax.random.split(key, 7)
        h = jax.random.normal(k[0], (N, IN_DIM), dtype=jnp.float32)
        W = jax.random.normal(k[1], (IN_DIM, H * D), dtype=jnp.float32) * (1.0 / np.sqrt(IN_DIM))
        attn_l = jax.random.normal(k[2], (H, D), dtype=jnp.float32) * 0.1
        attn_r = jax.random.normal(k[3], (H, D), dtype=jnp.float32) * 0.1
        bias = jnp.zeros((H * D,), dtype=jnp.float32)
        src = jax.random.randint(k[4], (E,), 0, N, dtype=jnp.int32)
        dst = jax.random.randint(k[5], (E,), 0, N, dtype=jnp.int32)
        return {'h': h, 'W': W, 'attn_l': attn_l, 'attn_r': attn_r, 'bias': bias, 'src': src, 'dst': dst}
    _L0_gnn_all = _L0_gnn_setup()
    _L0_gnn_in = {k: v for k, v in _L0_gnn_all.items() if k in ('W', 'attn_l', 'attn_r', 'bias')}
    del _L0_gnn_all

    def _L0_mix_setup():
        import math
        import jax, jax.numpy as jnp
        import numpy as np
        EPS_DIV = 1e-07
        EPS_NORM = 1e-12

        def _l2_normalize(x, axis):
            n = jnp.sqrt(jnp.sum(x * x, axis=axis, keepdims=True))
            return x / jnp.maximum(n, EPS_NORM)
        key = jax.random.key(seed)
        ks = jax.random.split(key, 5)
        b, N, C = (8, 512, 256)
        x = jax.random.normal(ks[0], (b, N, C), dtype=jnp.float32)
        W_qkv = jax.random.normal(ks[1], (C, 3 * C), dtype=jnp.float32) * (1.0 / math.sqrt(C))
        b_qkv = jax.random.normal(ks[2], (3 * C,), dtype=jnp.float32) * 0.02
        W_out = jax.random.normal(ks[3], (C, C), dtype=jnp.float32) * (1.0 / math.sqrt(C))
        b_out = jax.random.normal(ks[4], (C,), dtype=jnp.float32) * 0.02
        return {'x': x, 'W_qkv': W_qkv, 'b_qkv': b_qkv, 'W_out': W_out, 'b_out': b_out}
    _L0_mix_all = _L0_mix_setup()
    _L0_mix_in = {k: v for k, v in _L0_mix_all.items() if k in ('W_qkv', 'b_qkv', 'W_out', 'b_out')}
    del _L0_mix_all

    def _L0_ffn_setup():
        import jax, jax.numpy as jnp
        import numpy as np
        E, D, H, TOP_K = (6, 256, 256, 2)
        ROUTER_H = D // 2
        key = jax.random.key(seed)
        ks = jax.random.split(key, 12)
        s = 1.0 / np.sqrt(D)
        sh = 1.0 / np.sqrt(H)
        sr = 1.0 / np.sqrt(ROUTER_H)
        return {'features': jax.random.normal(ks[0], (8, 512, D), dtype=jnp.float32), 'router_w1': jax.random.uniform(ks[1], (D, ROUTER_H), jnp.float32, -s, s), 'router_b1': jnp.zeros((ROUTER_H,), jnp.float32), 'router_w2': jax.random.uniform(ks[2], (ROUTER_H, E), jnp.float32, -sr, sr), 'router_b2': jnp.zeros((E,), jnp.float32), 'expert_w1': jax.random.uniform(ks[3], (E, D, H), jnp.float32, -s, s), 'expert_b1': jnp.zeros((E, H), jnp.float32), 'expert_w2': jax.random.uniform(ks[4], (E, H, H), jnp.float32, -sh, sh), 'expert_b2': jnp.zeros((E, H), jnp.float32), 'expert_w3': jax.random.uniform(ks[5], (E, H, D), jnp.float32, -sh, sh), 'expert_b3': jnp.zeros((E, D), jnp.float32)}
    _L0_ffn_all = _L0_ffn_setup()
    _L0_ffn_in = {k: v for k, v in _L0_ffn_all.items() if k in ('router_w1', 'router_b1', 'router_w2', 'router_b2', 'expert_w1', 'expert_b1', 'expert_w2', 'expert_b2', 'expert_w3', 'expert_b3')}
    del _L0_ffn_all

    def _L1_gnn_setup():
        import jax, jax.numpy as jnp
        import numpy as np
        N, E = (6250, 100000)
        IN, H, C = (256, 8, 32)
        NEG_SLOPE = 0.2
        EPS = 1e-05
        key = jax.random.key(seed)
        ks = jax.random.split(key, 6)
        x = jax.random.normal(ks[0], (N, IN), jnp.float32)
        edge_index = jax.random.randint(ks[1], (2, E), 0, N, dtype=jnp.int32)
        W = jax.random.normal(ks[2], (IN, H * C), jnp.float32) / np.sqrt(IN).astype(np.float32)
        att_src = jax.random.normal(ks[3], (H, C), jnp.float32) * 0.1
        att_dst = jax.random.normal(ks[4], (H, C), jnp.float32) * 0.1
        bias = jnp.zeros((H * C,), jnp.float32)
        gamma = jnp.ones((H * C,), jnp.float32)
        beta = jnp.zeros((H * C,), jnp.float32)
        return {'x': x, 'edge_index': edge_index, 'W': W, 'att_src': att_src, 'att_dst': att_dst, 'bias': bias, 'gamma': gamma, 'beta': beta}
    _L1_gnn_all = _L1_gnn_setup()
    _L1_gnn_in = {k: v for k, v in _L1_gnn_all.items() if k in ('W', 'att_src', 'att_dst', 'bias', 'gamma', 'beta')}
    del _L1_gnn_all

    def _L1_mix_setup():
        import jax, jax.numpy as jnp
        import numpy as np
        HEADS = 8
        DIM_HEAD = 32
        SCALE = DIM_HEAD ** (-0.5)
        EPS = 1e-05

        def _layernorm_gamma(x, gamma):
            mu = jnp.mean(x, axis=-1, keepdims=True)
            var = jnp.var(x, axis=-1, keepdims=True)
            return (x - mu) * jax.lax.rsqrt(var + EPS) * gamma
        key = jax.random.key(seed)
        k1, k2, k3 = jax.random.split(key, 3)
        B, N, D = (8, 2048, 256)
        hidden = HEADS * DIM_HEAD
        x = jax.random.normal(k1, (B, N, D), dtype=jnp.float32)
        Wqkv = jax.random.normal(k2, (D, 3 * hidden), dtype=jnp.float32) * D ** (-0.5)
        Wout = jax.random.normal(k3, (hidden, D), dtype=jnp.float32) * hidden ** (-0.5)
        gamma = jnp.ones((D,), dtype=jnp.float32)
        return {'x': x, 'Wqkv': Wqkv, 'Wout': Wout, 'gamma': gamma}
    _L1_mix_all = _L1_mix_setup()
    _L1_mix_in = {k: v for k, v in _L1_mix_all.items() if k in ('Wqkv', 'Wout', 'gamma')}
    del _L1_mix_all

    def _L1_ffn_setup():
        import jax, jax.numpy as jnp
        import numpy as np
        B, S, D = (8, 512, 256)
        H = 4 * D
        CAPACITY = 0.5
        key = jax.random.key(seed)
        ks = jax.random.split(key, 6)
        x = jax.random.normal(ks[0], (B, S, D), dtype=jnp.float32)
        attention_mask = jnp.zeros((B, 1, 1, S), dtype=jnp.float32)
        wr = jax.random.normal(ks[1], (D, 1), dtype=jnp.float32) * 0.02
        br = jnp.zeros((1,), dtype=jnp.float32)
        w1 = jax.random.normal(ks[2], (D, H), dtype=jnp.float32) * 0.02
        b1 = jnp.zeros((H,), dtype=jnp.float32)
        w2 = jax.random.normal(ks[3], (H, D), dtype=jnp.float32) * 0.02
        b2 = jnp.zeros((D,), dtype=jnp.float32)
        return {'x': x, 'attention_mask': attention_mask, 'wr': wr, 'br': br, 'w1': w1, 'b1': b1, 'w2': w2, 'b2': b2}
    _L1_ffn_all = _L1_ffn_setup()
    _L1_ffn_in = {k: v for k, v in _L1_ffn_all.items() if k in ('attention_mask', 'wr', 'br', 'w1', 'b1', 'w2', 'b2')}
    del _L1_ffn_all
    return {'x': x, 'src': src, 'dst': dst, 'L0_gnn_W': _L0_gnn_in['W'], 'L0_gnn_attn_l': _L0_gnn_in['attn_l'], 'L0_gnn_attn_r': _L0_gnn_in['attn_r'], 'L0_gnn_bias': _L0_gnn_in['bias'], 'L0_mix_W_qkv': _L0_mix_in['W_qkv'], 'L0_mix_b_qkv': _L0_mix_in['b_qkv'], 'L0_mix_W_out': _L0_mix_in['W_out'], 'L0_mix_b_out': _L0_mix_in['b_out'], 'L0_ffn_router_w1': _L0_ffn_in['router_w1'], 'L0_ffn_router_b1': _L0_ffn_in['router_b1'], 'L0_ffn_router_w2': _L0_ffn_in['router_w2'], 'L0_ffn_router_b2': _L0_ffn_in['router_b2'], 'L0_ffn_expert_w1': _L0_ffn_in['expert_w1'], 'L0_ffn_expert_b1': _L0_ffn_in['expert_b1'], 'L0_ffn_expert_w2': _L0_ffn_in['expert_w2'], 'L0_ffn_expert_b2': _L0_ffn_in['expert_b2'], 'L0_ffn_expert_w3': _L0_ffn_in['expert_w3'], 'L0_ffn_expert_b3': _L0_ffn_in['expert_b3'], 'L1_gnn_W': _L1_gnn_in['W'], 'L1_gnn_att_src': _L1_gnn_in['att_src'], 'L1_gnn_att_dst': _L1_gnn_in['att_dst'], 'L1_gnn_bias': _L1_gnn_in['bias'], 'L1_gnn_gamma': _L1_gnn_in['gamma'], 'L1_gnn_beta': _L1_gnn_in['beta'], 'L1_mix_Wqkv': _L1_mix_in['Wqkv'], 'L1_mix_Wout': _L1_mix_in['Wout'], 'L1_mix_gamma': _L1_mix_in['gamma'], 'L1_ffn_attention_mask': _L1_ffn_in['attention_mask'], 'L1_ffn_wr': _L1_ffn_in['wr'], 'L1_ffn_br': _L1_ffn_in['br'], 'L1_ffn_w1': _L1_ffn_in['w1'], 'L1_ffn_b1': _L1_ffn_in['b1'], 'L1_ffn_w2': _L1_ffn_in['w2'], 'L1_ffn_b2': _L1_ffn_in['b2']}

def reference(x, src, dst, L0_gnn_W, L0_gnn_attn_l, L0_gnn_attn_r, L0_gnn_bias, L0_mix_W_qkv, L0_mix_b_qkv, L0_mix_W_out, L0_mix_b_out, L0_ffn_router_w1, L0_ffn_router_b1, L0_ffn_router_w2, L0_ffn_router_b2, L0_ffn_expert_w1, L0_ffn_expert_b1, L0_ffn_expert_w2, L0_ffn_expert_b2, L0_ffn_expert_w3, L0_ffn_expert_b3, L1_gnn_W, L1_gnn_att_src, L1_gnn_att_dst, L1_gnn_bias, L1_gnn_gamma, L1_gnn_beta, L1_mix_Wqkv, L1_mix_Wout, L1_mix_gamma, L1_ffn_attention_mask, L1_ffn_wr, L1_ffn_br, L1_ffn_w1, L1_ffn_b1, L1_ffn_w2, L1_ffn_b2):
    import jax
    import jax.numpy as jnp

    def _L0_gnn_ref(h, W, attn_l, attn_r, bias, src, dst):
        import jax, jax.numpy as jnp
        import numpy as np
        N, E, H, D = (6250, 100000, 4, 64)
        IN_DIM = H * D
        NEG_SLOPE = 0.2
        feat = (h @ W).reshape(N, H, D)
        el = jnp.einsum('nhd,hd->nh', feat, attn_l)
        er = jnp.einsum('nhd,hd->nh', feat, attn_r)
        e = jax.nn.leaky_relu(el[src] + er[dst], NEG_SLOPE)
        emax = jax.ops.segment_max(e, dst, num_segments=N)
        ex = jnp.exp(e - emax[dst])
        denom = jax.ops.segment_sum(ex, dst, num_segments=N)
        alpha = ex / denom[dst]
        msg = feat[src] * alpha[..., None]
        rst = jax.ops.segment_sum(msg, dst, num_segments=N)
        rst = rst + bias.reshape(1, H, D)
        out = jax.nn.elu(rst.reshape(N, H * D))
        return h + out

    def _L0_mix_ref(x, W_qkv, b_qkv, W_out, b_out):
        import math
        import jax, jax.numpy as jnp
        import numpy as np
        EPS_DIV = 1e-07
        EPS_NORM = 1e-12

        def _l2_normalize(x, axis):
            n = jnp.sqrt(jnp.sum(x * x, axis=axis, keepdims=True))
            return x / jnp.maximum(n, EPS_NORM)
        b, N, C = x.shape
        qkv = x @ W_qkv + b_qkv
        q, k, v = jnp.split(qkv, 3, axis=2)
        q = q - jnp.mean(q, axis=2, keepdims=True)
        k = k - jnp.mean(k, axis=2, keepdims=True)
        q2 = q * q
        k2 = k * k
        q2s = jnp.sum(q2, axis=2, keepdims=True)
        k2s = jnp.sum(k2, axis=2, keepdims=True)
        k2 = _l2_normalize(k2 / (k2s + EPS_DIV), axis=-2)
        q2 = _l2_normalize(q2 / (q2s + EPS_DIV), axis=-1)
        kv = jnp.einsum('bnc,bnd->bcd', k2, v)
        t2 = jnp.einsum('bnc,bcd->bnd', q2, kv) / math.sqrt(N)
        attn = v + t2
        return attn @ W_out + b_out

    def _L0_ffn_ref(features, router_w1, router_b1, router_w2, router_b2, expert_w1, expert_b1, expert_w2, expert_b2, expert_w3, expert_b3):
        import jax, jax.numpy as jnp
        import numpy as np
        E, D, H, TOP_K = (6, 256, 256, 2)
        ROUTER_H = D // 2
        rh = jax.nn.relu(features @ router_w1 + router_b1)
        expert_logits = jax.nn.softmax(rh @ router_w2 + router_b2, axis=-1)
        top_w, top_i = jax.lax.top_k(expert_logits, TOP_K)
        routing_weights = jax.nn.softmax(top_w, axis=-1)
        h1 = jax.nn.relu(jnp.einsum('bsd,edh->bseh', features, expert_w1) + expert_b1)
        h2 = jax.nn.relu(jnp.einsum('bseh,ehf->bsef', h1, expert_w2) + expert_b2)
        expert_out = jnp.einsum('bsef,efo->bseo', h2, expert_w3) + expert_b3
        sel = jnp.take_along_axis(expert_out, top_i[:, :, :, None], axis=2)
        combined = jnp.sum(sel * routing_weights[..., None], axis=2)
        return combined

    def _L1_gnn_ref(x, edge_index, W, att_src, att_dst, bias, gamma, beta):
        import jax, jax.numpy as jnp
        import numpy as np
        N, E = (6250, 100000)
        IN, H, C = (256, 8, 32)
        NEG_SLOPE = 0.2
        EPS = 1e-05
        n = x.shape[0]
        xl = (x @ W).reshape(n, H, C)
        a_src = jnp.einsum('nhc,hc->nh', xl, att_src)
        a_dst = jnp.einsum('nhc,hc->nh', xl, att_dst)
        loops = jnp.arange(n, dtype=edge_index.dtype)
        src = jnp.concatenate([edge_index[0], loops])
        dst = jnp.concatenate([edge_index[1], loops])
        logits = jax.nn.leaky_relu(a_src[src] + a_dst[dst], NEG_SLOPE)
        seg_max = jax.ops.segment_max(logits, dst, num_segments=n)
        ex = jnp.exp(logits - seg_max[dst])
        denom = jax.ops.segment_sum(ex, dst, num_segments=n)
        alpha = ex / denom[dst]
        msgs = xl[src] * alpha[:, :, None]
        out = jax.ops.segment_sum(msgs, dst, num_segments=n).reshape(n, H * C) + bias
        mu = jnp.mean(out, axis=-1, keepdims=True)
        var = jnp.var(out, axis=-1, keepdims=True)
        return (out - mu) / jnp.sqrt(var + EPS) * gamma + beta

    def _L1_mix_ref(x, Wqkv, Wout, gamma):
        import jax, jax.numpy as jnp
        import numpy as np
        HEADS = 8
        DIM_HEAD = 32
        SCALE = DIM_HEAD ** (-0.5)
        EPS = 1e-05

        def _layernorm_gamma(x, gamma):
            mu = jnp.mean(x, axis=-1, keepdims=True)
            var = jnp.var(x, axis=-1, keepdims=True)
            return (x - mu) * jax.lax.rsqrt(var + EPS) * gamma
        B, N, D = x.shape
        qkv = x @ Wqkv
        q, k, v = jnp.split(qkv, 3, axis=-1)

        def to_heads(t):
            return t.reshape(B, N, HEADS, DIM_HEAD).transpose(0, 2, 1, 3)
        q, k, v = map(to_heads, (q, k, v))
        q = jax.nn.softmax(q, axis=-1) * SCALE
        k = jax.nn.softmax(k, axis=2)
        context = jnp.einsum('bhnd,bhne->bhde', k, v)
        out = jnp.einsum('bhde,bhnd->bhne', context, q)
        out = out.transpose(0, 2, 1, 3).reshape(B, N, HEADS * DIM_HEAD)
        out = out @ Wout
        return _layernorm_gamma(out, gamma)

    def _L1_ffn_ref(x, attention_mask, wr, br, w1, b1, w2, b2):
        import jax, jax.numpy as jnp
        import numpy as np
        B, S, D = (8, 512, 256)
        H = 4 * D
        CAPACITY = 0.5
        b, s, d = x.shape
        weights = (jnp.einsum('bsd,do->bso', x, wr) + br)[..., 0]
        k = max(1, int(CAPACITY * s))
        kk = k - 1 if k > 1 else 1
        _, idx = jax.lax.top_k(weights, k)
        sel_idx = idx[:, :kk]
        sel = jnp.take_along_axis(x, sel_idx[:, :, None], axis=1)
        h = jax.nn.gelu(jnp.einsum('bkd,dh->bkh', sel, w1) + b1)
        y = jnp.einsum('bkh,hd->bkd', h, w2) + b2
        w_sel = jnp.take_along_axis(weights, sel_idx, axis=1)
        y = y * w_sel[..., None]
        batch_idx = jnp.arange(b)[:, None]
        processed = jnp.zeros_like(x).at[batch_idx, sel_idx].set(y)
        return processed + x
    edge_index = jnp.stack([src, dst])
    xn = _layernorm(x, axis=-1)
    x = x + _L0_gnn_ref(xn, L0_gnn_W, L0_gnn_attn_l, L0_gnn_attn_r, L0_gnn_bias, src, dst) + _L0_mix_ref(xn[None], L0_mix_W_qkv, L0_mix_b_qkv, L0_mix_W_out, L0_mix_b_out)[0]
    x = x + _L0_ffn_ref(_layernorm(x, axis=-1)[None], L0_ffn_router_w1, L0_ffn_router_b1, L0_ffn_router_w2, L0_ffn_router_b2, L0_ffn_expert_w1, L0_ffn_expert_b1, L0_ffn_expert_w2, L0_ffn_expert_b2, L0_ffn_expert_w3, L0_ffn_expert_b3)[0]
    xn = _layernorm(x, axis=-1)
    x = x + _L1_gnn_ref(xn, edge_index, L1_gnn_W, L1_gnn_att_src, L1_gnn_att_dst, L1_gnn_bias, L1_gnn_gamma, L1_gnn_beta) + _L1_mix_ref(xn[None], L1_mix_Wqkv, L1_mix_Wout, L1_mix_gamma)[0]
    x = x + _L1_ffn_ref(_layernorm(x, axis=-1)[None], L1_ffn_attention_mask, L1_ffn_wr, L1_ffn_br, L1_ffn_w1, L1_ffn_b1, L1_ffn_w2, L1_ffn_b2)[0]
    return x

_drawn_inputs = setup_inputs


def setup_inputs(seed=0):
    import zlib

    import numpy as np

    out = dict(_drawn_inputs(seed))
    spreads = {'L0_gnn_bias': (0.0, 0.1),
     'L0_ffn_router_b1': (0.0, 0.473),
     'L0_ffn_router_b2': (0.0, 0.1),
     'L0_ffn_expert_b1': (0.0, 0.8),
     'L0_ffn_expert_b2': (0.0, 0.1),
     'L0_ffn_expert_b3': (0.0, 0.1),
     'L1_gnn_bias': (0.0, 0.1),
     'L1_gnn_gamma': (1.0, 0.2),
     'L1_gnn_beta': (0.0, 0.1),
     'L1_mix_gamma': (1.0, 0.2),
     'L1_ffn_b1': (0.0, 0.8),
     'L1_ffn_b2': (0.0, 0.8)}
    factors = {'L0_gnn_attn_r': 3.506,
     'L0_ffn_expert_w1': 2.7,
     'L1_ffn_wr': 7.925,
     'L1_ffn_w1': 8.0,
     'L1_ffn_w2': 8.0}
    for name, (base, spread) in spreads.items():
        noise = np.random.default_rng([zlib.crc32(name.encode()), seed]).standard_normal(out[name].shape)
        drawn = base * np.exp(spread * noise) if base else spread * noise
        out[name] = jnp.asarray(drawn.astype(out[name].dtype))
    for name, factor in factors.items():
        out[name] = (out[name] * factor).astype(out[name].dtype)
    return out
```

```python
from contextlib import ExitStack

import concourse.bass as bass
from concourse import mybir

F32 = mybir.dt.float32
I32 = mybir.dt.int32
ALU = mybir.AluOpType
ACT = mybir.ActivationFunctionType
AX = mybir.AxisListType

P = 128
N = 6250
D = 256
DC = D // P
NT = -(-N // P)
TB = 7
NBLK = NT // TB
NPAD = NT * P
HALF = TB * P // 2
E = 206250
G = 16
ME = G * P
NM = -(-E // ME)
NSTEP = NM + NT
NSTEP += NSTEP % 2
NTA = NT + 1
BIG = 1e30
NEG_SLOPE = 0.2
LN_EPS = 1e-5
N_EXP = 6
TOPK_KEEP = 3124

assert NT == TB * NBLK and HALF <= 512 and NM % 2 == 1

CONST = {}
_at = 0
for _name, _width in (("ident", P), ("ones", P), ("iota", P), ("valid", NT), ("negpad", NT),
                      ("blockmask", P), ("steps", NSTEP), ("macros", NM), ("below", P), ("index", NT),
                      ("head4", DC * 4), ("head8", DC * 8), ("earlier", 36), ("eps", 1)):
    CONST[_name] = (_at, _at + _width)
    _at += _width
CONST_W = _at


class Link:

    def __init__(self, eng, sem):
        self.eng, self.sem, self.before, self.n, self.i, self.per = eng, sem, 0, 0, None, 0

    def loop(self, i, per):
        self.before, self.n, self.i, self.per = self.before + self.n, 0, i, per

    def leave(self, rounds):
        assert self.n == self.per, f"the loop's body has {self.n} links"
        self.before, self.n, self.i = self.before + rounds * self.per, 0, None

    def __call__(self, ins):
        ins.then_inc(self.sem, 1)
        self.n += 1
        value = self.before + self.n
        self.eng.wait_ge(self.sem, value if self.i is None else self.i * self.per + value)


class Stage:

    def __init__(self, nc, name):
        self.nc, self.name, self.stack, self.sems = nc, name, ExitStack(), []

    def __enter__(self):
        return self

    def sb(self, name, shape, dt=F32):
        return self.stack.enter_context(self.nc.sbuf_tensor(f"{self.name}_{name}", shape, dt))

    def banks(self, name, n):
        return [self.stack.enter_context(self.nc.psum_tensor(f"{self.name}_{name}{i}", [P, 512], F32))
                for i in range(n)]

    def sem(self, name):
        self.sems.append(self.nc.alloc_semaphore(f"{self.name}_{name}"))
        return self.sems[-1]

    def __exit__(self, *exc):
        if exc[0] is None:
            self.nc.clear_and_free_semaphores(self.sems)
            self.nc.all_engine_barrier()
            self.stack.close()
        return False


def col(keep, name):
    a, b = CONST[name]
    return keep["const"][:, a:b]


def blocks(dram):
    return dram.rearrange("(b j p) c -> b p j c", p=P, j=TB)


def cast(ap, n):
    return ap.unsqueeze(2).to_broadcast([ap.shape[0], ap.shape[1], n])


def block_of(dram, i):
    return blocks(dram)[bass.ds(i, 1), :, :, :].rearrange("b p j c -> p (b j) c")


def row_moments(nc, link, x, stats, mv, passed):
    for j in range(TB):
        last = nc.vector.bn_stats(stats[:, j, :], x[:, j, :])
    link(last)
    nc.vector.sem_inc(passed, 1)
    for j in range(TB):
        last = nc.vector.bn_aggr(mv[:, j, :], stats[:, j, :])
    return last


def schedule_stage(nc, keep, io):
    with Stage(nc, "sched") as st:
        ends_row = st.sb("ends_row", [P, NM], I32)
        ends_col = st.sb("ends_col", [P, 1], I32)
        tile_row = st.sb("tile_row", [P, NM], I32)
        tile_col = st.sb("tile_col", [P, 1], I32)
        key_row = st.sb("key_row", [P, NM])
        key_col = st.sb("key_col", [P, 1])
        after = st.sb("after", [P, NSTEP])
        psum = st.banks("macro", 1)[0]
        loaded, chain, compared, summed = (st.sem(n) for n in ("loaded", "chain", "compared", "summed"))
        with nc.Block() as block:
            @block.sync
            def _(sp):
                sp.dma_start(keep["const"][:], io["const"]).then_inc(loaded, 16)
                sp.dma_start(ends_row[:], io["ends_row"]).then_inc(loaded, 16)
                sp.dma_start(ends_col[:], io["ends_col"]).then_inc(loaded, 16)
                sp.wait_ge(loaded, 48)

            @block.vector
            def _(dve):
                link = Link(dve, chain)
                link(nc.vector.memset(keep["right"][:], 0.0))
                dve.wait_ge(loaded, 48)
                nc.vector.tensor_copy(keep["iota_b"][:], col(keep, "iota"))
                nc.vector.tensor_single_scalar(tile_row[:], ends_row[:], 7, ALU.logical_shift_right)
                link(nc.vector.tensor_single_scalar(tile_col[:], ends_col[:], 7, ALU.logical_shift_right))
                nc.vector.tensor_tensor(key_row[:], tile_row[:], col(keep, "macros"), ALU.add)
                link(nc.vector.tensor_tensor(key_col[:], tile_col[:], col(keep, "index")[:, 0:1], ALU.add))
                nc.vector.tensor_copy(keep["last_step"][:], key_row[:])
                nc.vector.tensor_scalar(after[:], col(keep, "steps"), key_col[:, 0:1], None,
                                        ALU.is_gt).then_inc(compared, 1)
                dve.wait_ge(summed, 1)
                nc.vector.tensor_copy(keep["macro_of"][:], psum[:, 0:NSTEP])
                link(nc.vector.tensor_tensor(keep["node0"][:], col(keep, "steps"), psum[:, 0:NSTEP], ALU.subtract))
                link(nc.vector.tensor_copy(keep["tile_of"][:], keep["node0"][:]))
                link(nc.vector.tensor_scalar(keep["node0"][:], keep["node0"][:], float(P), None, ALU.mult))

            @block.tensor
            def _(pe):
                pe.wait_ge(compared, 1)
                nc.tensor.matmul(psum[:, 0:NSTEP], col(keep, "ones"), after[:], start=True, stop=True)\
                    .then_inc(summed, 1)


def pre_stage(nc, keep, io, layer):
    H = 4 if layer == 0 else 8
    ROW = D + H
    L = f"l{layer}_"
    first = layer == 0
    src, table = io["x0" if first else "x2"], io[f"table{layer}"]
    with Stage(nc, f"pre{layer}") as st:
        x = st.sb("x", [P, TB, D])
        xn = st.sb("xn", [P, TB, D])
        stats = st.sb("stats", [P, TB, 6])
        mv = st.sb("mv", [P, TB, 2])
        std = st.sb("std", [P, TB])
        rstd = st.sb("rstd", [P, TB])
        w_gat = st.sb("w_gat", [P, DC, D + 2 * H])
        w_gat_t = st.sb("w_gat_t", [P, DC, D])
        attn = st.sb("attn", [P, DC, 2])
        attn_heads = st.sb("attn_heads", [P, DC, 2, H])
        w_qkv = st.sb("w_qkv", [P, DC, 3 * D])
        xt = st.sb("xt", [P, 2, DC, P])
        row = st.sb("row", [P, TB, ROW])
        q = st.sb("q", [P, TB, D])
        k = st.sb("k", [P, TB, D])
        v = st.sb("v", [P, TB, D])
        rights = st.sb("rights", [P, TB, H])
        if first:
            mean = st.sb("mean", [P, DC, 2])
            bias = st.sb("bias", [P, 3 * D])
            bias_mean = st.sb("bias_mean", [P, 2])
            q2 = st.sb("q2", [P, TB, D])
            k2 = st.sb("k2", [P, TB, D])
            junk = st.sb("junk", [P, D])
            k_square = st.sb("k_square", [P, TB, D])
            sums = st.sb("sums", [P, 3, TB])
            q_root = st.sb("q_root", [P, TB])
            scale = st.sb("scale", [P, 2, TB])
            zeros = st.sb("zeros", [P, 512])
            kv_t = st.sb("kv_t", [P, DC, D])
            w_out = st.sb("w_out", [P, DC, D])
            col_norm = st.sb("col_norm", [P, DC])
            norm_root = st.sb("norm_root", [P, DC])
        else:
            q_max = st.sb("q_max", [P, TB, H])
            q_sum = st.sb("q_sum", [P, TB, H])
            block_max = st.sb("block_max", [P, D])
            run_max = st.sb("run_max", [P, D])
            col_max = st.sb("col_max", [P, DC])
            diag = st.sb("diag", [P, DC, P])
        ps_xt = st.banks("ps_xt", 2)
        ps_qk = st.banks("ps_qk", 2)
        ps_gv = st.banks("ps_gv", 1)[0]
        ps_lr = st.banks("ps_lr", 1)[0]
        ps_kv = st.banks("ps_kv", 1)[0]
        ps_norm = st.banks("ps_norm", 1)[0]
        S = {n: st.sem(n) for n in (
            "weights_in x_in passed chain act_chain moments_ready std_ready xn_ready xt_made xt_copied projected row_ready "
            "qkv_ready squares_ready q_root_ready stored out_free q_ready k_ready k_square_ready kv_done "
            "w_t_made w_t_copied heads_ready wa_made weights_ready kv_copied kw_made norm_root_ready zeros_ready "
            "q_shifted q_exp max_ready max_t_made diag_ready max_row_made v_ready").split()}
        n_weights = 6 if first else 4
        ident = col(keep, "ident")
        eps = col(keep, "eps")
        with nc.Block() as block:
            @block.sync
            def _(sp):
                sp.dma_start(w_gat_t[:], io[L + "w_gat"]).then_inc(S["weights_in"], 16)
                sp.dma_start(attn[:], io[L + "attn"]).then_inc(S["weights_in"], 16)
                sp.dma_start(w_gat[:, :, 0:D], io[L + "w_gat"]).then_inc(S["weights_in"], 16)
                sp.dma_start(w_qkv[:], io[L + "w_qkv"]).then_inc(S["weights_in"], 16)
                if first:
                    sp.dma_start(bias[:], io["l0_b_qkv"]).then_inc(S["weights_in"], 16)
                    sp.dma_start(w_out[:], io["l0_w_out"]).then_inc(S["weights_in"], 16)
                sp.sem_inc(S["out_free"], 1)
                with sp.Fori(0, NBLK) as i:
                    sp.dma_start(x[:], block_of(src, i)).then_inc(S["x_in"], 16)
                    sp.wait_ge(S["row_ready"], (i + 1) * TB)
                    sp.dma_start(block_of(table, i), row[:]).then_inc(S["stored"], 16)
                    sp.wait_ge(S["q_ready"], i + 1)
                    sp.dma_start(block_of(io["q"], i), (q2 if first else q)[:]).then_inc(S["stored"], 16)
                    if first:
                        sp.wait_ge(S["v_ready"], i + 1)
                    sp.dma_start(block_of(io["v"], i), v[:]).then_inc(S["stored"], 16)
                    if first:
                        sp.dma_start(block_of(io["xn"], i), xn[:]).then_inc(S["stored"], 16)
                    else:
                        sp.dma_start(block_of(io["k"], i), k[:]).then_inc(S["stored"], 16)
                    sp.wait_ge(S["stored"], (i + 1) * 64)
                    sp.sem_inc(S["out_free"], 1)

            @block.vector
            def _(dve):
                link = Link(dve, S["chain"])
                dve.wait_ge(S["weights_in"], 16 * n_weights)
                heads = col(keep, f"head{H}").rearrange("p (k h) -> p k h", k=DC)
                for side in range(2):
                    last = nc.vector.tensor_tensor(attn_heads[:, :, side, :], heads, cast(attn[:, :, side], H), ALU.mult)
                last.then_inc(S["heads_ready"], 1)
                if first:
                    for a in range(2):
                        nc.vector.tensor_reduce(mean[:, :, a], w_qkv[:, :, a * D:(a + 1) * D], AX.X, ALU.add)
                        last = nc.vector.tensor_reduce(bias_mean[:, a:a + 1], bias[:, a * D:(a + 1) * D], AX.X, ALU.add)
                    link(last)
                    nc.vector.tensor_scalar(mean[:], mean[:], 1.0 / D, None, ALU.mult)
                    link(nc.vector.tensor_scalar(bias_mean[:], bias_mean[:], 1.0 / D, None, ALU.mult))
                    for a in range(2):
                        nc.vector.tensor_tensor(w_qkv[:, :, a * D:(a + 1) * D], w_qkv[:, :, a * D:(a + 1) * D],
                                                cast(mean[:, :, a], D), ALU.subtract)
                        nc.vector.tensor_scalar(bias[:, a * D:(a + 1) * D], bias[:, a * D:(a + 1) * D],
                                                bias_mean[:, a:a + 1], None, ALU.subtract)
                    nc.vector.memset(zeros[:], 0.0).then_inc(S["zeros_ready"], 1)
                else:
                    nc.vector.memset(run_max[:], -BIG).then_inc(S["zeros_ready"], 1)
                dve.wait_ge(S["zeros_ready"], 1)
                dve.wait_ge(S["wa_made"], 1)
                nc.vector.tensor_copy(w_gat[:, :, D:D + 2 * H],
                                      ps_lr[:, 0:DC * 2 * H].rearrange("p (k h) -> p k h", k=DC))\
                    .then_inc(S["weights_ready"], 1)
                with dve.Fori(0, NBLK) as i:
                    link.loop(i, 7 if first else 7)
                    dve.wait_ge(S["x_in"], (i + 1) * 16)
                    row_moments(nc, link, x, stats, mv, S["passed"]).then_inc(S["moments_ready"], 1)
                    dve.wait_ge(S["std_ready"], i + 1)
                    link(nc.vector.reciprocal(rstd[:], std[:]))
                    dve.wait_ge(S["out_free"], i + 1)
                    for j in range(TB):
                        nc.vector.tensor_scalar(xn[:, j, :], x[:, j, :], mv[:, j, 0:1], rstd[:, j:j + 1],
                                                ALU.subtract, ALU.mult).then_inc(S["xn_ready"], 1)
                    for j in range(TB):
                        t1 = i * TB + j + 1
                        dve.wait_ge(S["projected"], t1)
                        if first:
                            nc.vector.tensor_tensor(q[:, j, :], ps_qk[j % 2][:, 0:D], bias[:, 0:D], ALU.add)
                            nc.vector.tensor_tensor(k[:, j, :], ps_qk[j % 2][:, D:2 * D], bias[:, D:2 * D],
                                                    ALU.add).then_inc(S["qkv_ready"], 1)
                        else:
                            nc.vector.tensor_scalar(k[:, j, :], ps_qk[j % 2][:, D:2 * D],
                                                    keep["negpad"][:, bass.ds(i * TB + j, 1)], None, ALU.add)
                            nc.vector.tensor_copy(q[:, j, :], ps_qk[j % 2][:, 0:D]).then_inc(S["qkv_ready"], 1)
                    dve.wait_ge(S["qkv_ready"], (i + 1) * TB)
                    dve.wait_ge(S["row_ready"], (i + 1) * TB)
                    nc.vector.tensor_scalar(keep["right"][:, bass.ds(i * TB, TB), 0:H], rights[:], 1.0, None, ALU.mult)
                    if first:
                        nc.vector.tensor_tensor(v[:], v[:], bias[:, 2 * D:3 * D].unsqueeze(1).to_broadcast([P, TB, D]),
                                                ALU.add).then_inc(S["v_ready"], 1)
                    else:
                        here = bass.ds(i * TB, TB)
                        nc.vector.tensor_scalar(keep["acc"][:, here, 0:D], row[:, :, 0:D], 1.0, None, ALU.mult)
                        nc.vector.tensor_scalar(keep["acc"][:, here, D:ROW], row[:, :, D:ROW], 0.0, 1.0, ALU.mult, ALU.add)
                        nc.vector.tensor_scalar(keep["left_max"][:, here, 0:H], row[:, :, D:ROW], 1.0, None, ALU.mult)
                    if first:
                        dve.wait_ge(S["squares_ready"], i + 1)
                        dve.wait_ge(S["q_root_ready"], i + 1)
                        link(nc.vector.tensor_scalar(sums[:, 0:2, :], sums[:, 0:2, :], 1e-7, None, ALU.add))
                        link(nc.vector.reciprocal(scale[:], sums[:, 0:2, :]))
                        nc.vector.tensor_tensor(scale[:, 1, :], scale[:, 1, :], keep["valid"][:, bass.ds(i * TB, TB)],
                                                ALU.mult)
                        link(nc.vector.tensor_tensor(q_root[:], q_root[:], scale[:, 0, :], ALU.mult))
                        link(nc.vector.tensor_scalar(q_root[:], q_root[:], 1e-12, None, ALU.max))
                        link(nc.vector.reciprocal(q_root[:], q_root[:]))
                        nc.vector.tensor_tensor(k2[:], k2[:], cast(scale[:, 1, :], D), ALU.mult).then_inc(S["k_ready"], 1)
                        dve.wait_ge(S["k_ready"], i + 1)
                        for j in range(TB):
                            last = nc.vector.tensor_scalar(q2[:, j, :], q2[:, j, :], scale[:, 0, j:j + 1],
                                                           q_root[:, j:j + 1], ALU.mult, ALU.mult)
                        last.then_inc(S["q_ready"], 1)
                    else:
                        qh = q[:].rearrange("p j (h d) -> p (j h) d", h=H)
                        m, s = (a[:].rearrange("p j h -> p (j h)") for a in (q_max, q_sum))
                        link(nc.vector.tensor_reduce(m, qh, AX.X, ALU.max))
                        nc.vector.tensor_tensor(qh, qh, cast(m, D // H), ALU.subtract).then_inc(S["q_shifted"], 1)
                        link(nc.vector.tensor_reduce(block_max[:], k[:].rearrange("p j c -> p c j"), AX.X, ALU.max))
                        link(nc.vector.tensor_tensor(run_max[:], run_max[:], block_max[:], ALU.max))
                        dve.wait_ge(S["q_exp"], i + 1)
                        link(nc.vector.tensor_reduce(s, qh, AX.X, ALU.add))
                        link(nc.vector.reciprocal(s, s))
                        nc.vector.tensor_tensor(qh, qh, cast(s, D // H), ALU.mult).then_inc(S["q_ready"], 1)
                link.leave(NBLK)
                if first:
                    dve.wait_ge(S["kv_done"], 1)
                    nc.vector.tensor_copy(kv_t[:].rearrange("p k c -> p (k c)"), ps_kv[:]).then_inc(S["kv_copied"], 1)
                    dve.wait_ge(S["norm_root_ready"], 1)
                    link(nc.vector.tensor_scalar(norm_root[:], norm_root[:], 1e-12, float(N) ** 0.5, ALU.max, ALU.mult))
                    link(nc.vector.reciprocal(col_norm[:], norm_root[:]))
                    dve.wait_ge(S["kw_made"], 1)
                    for c in range(DC):
                        last = nc.vector.tensor_scalar(keep["kw"][:, c, :], ps_qk[0][:, c * D:(c + 1) * D],
                                                       col_norm[:, c:c + 1], None, ALU.mult)
                    link(last)
                else:
                    nc.vector.tensor_copy(block_max[:], run_max[:]).then_inc(S["max_ready"], 1)
                    dve.wait_ge(S["max_t_made"], 1)
                    link(nc.vector.tensor_reduce(col_max[:], ps_kv[:, 0:D].rearrange("p (k n) -> p k n", k=DC), AX.X, ALU.max))
                    for c in range(DC):
                        last = nc.vector.tensor_scalar(diag[:, c, :], ident, col_max[:, c:c + 1], None, ALU.mult)
                    last.then_inc(S["diag_ready"], 1)
                    dve.wait_ge(S["max_row_made"], 1)
                    link(nc.vector.tensor_copy(keep["k_max"][:], ps_norm[:, 0:D]))

            @block.scalar
            def _(act):
                act.wait_ge(S["w_t_made"], 1)
                nc.scalar.activation(w_gat_t[:].rearrange("p k n -> p (k n)"), ps_kv[:], ACT.Copy).then_inc(S["w_t_copied"], 1)
                with act.Fori(0, NBLK) as i:
                    act.wait_ge(S["moments_ready"], i + 1)
                    nc.scalar.activation(std[:], mv[:, :, 1], ACT.Sqrt, bias=eps).then_inc(S["std_ready"], 1)
                    for j in range(TB):
                        t1 = i * TB + j + 1
                        act.wait_ge(S["xt_made"], t1)
                        nc.scalar.activation(xt[:, j % 2].rearrange("p k n -> p (k n)"), ps_xt[j % 2][:, 0:D], ACT.Copy)\
                            .then_inc(S["xt_copied"], 1)
                        act.wait_ge(S["projected"], t1)
                        nc.scalar.activation(v[:, j, :], ps_gv[:, D:2 * D], ACT.Copy)
                        nc.scalar.activation(row[:, j, 0:D], ps_gv[:, 0:D], ACT.Copy)
                        nc.scalar.activation(rights[:, j, :], ps_lr[:, H:2 * H], ACT.Copy)
                        nc.scalar.activation(row[:, j, D:ROW], ps_lr[:, 0:H], ACT.Copy).then_inc(S["row_ready"], 1)
                        if first:
                            act.wait_ge(S["qkv_ready"], t1)
                            nc.scalar.activation(k2[:, j, :], k[:, j, :], ACT.Square, accum_out=sums[:, 1, j:j + 1])
                            nc.scalar.activation(q2[:, j, :], q[:, j, :], ACT.Square,
                                                 accum_out=sums[:, 0, j:j + 1]).then_inc(S["act_chain"], 1)
                            act.wait_ge(S["act_chain"], t1)
                            last = nc.scalar.activation(junk[:], q2[:, j, :], ACT.Square, accum_out=sums[:, 2, j:j + 1])
                    if first:
                        last.then_inc(S["squares_ready"], 1)
                        act.wait_ge(S["squares_ready"], i + 1)
                        nc.scalar.activation(q_root[:], sums[:, 2, :], ACT.Sqrt).then_inc(S["q_root_ready"], 1)
                        act.wait_ge(S["k_ready"], i + 1)
                        nc.scalar.activation(k_square[:], k2[:], ACT.Square).then_inc(S["k_square_ready"], 1)
                    else:
                        act.wait_ge(S["q_shifted"], i + 1)
                        nc.scalar.activation(q[:], q[:], ACT.Exp).then_inc(S["q_exp"], 1)
                if first:
                    act.wait_ge(S["kv_done"], 1)
                    nc.scalar.activation(norm_root[:], ps_norm[:, 0:DC], ACT.Sqrt).then_inc(S["norm_root_ready"], 1)

            @block.tensor
            def _(pe):
                pe.wait_ge(S["weights_in"], 16 * n_weights)
                for k_ in range(DC):
                    for n_ in range(DC):
                        last = nc.tensor.transpose(ps_kv[:, n_ * D + k_ * P:n_ * D + (k_ + 1) * P],
                                                   w_gat[:, k_, n_ * P:(n_ + 1) * P], ident)
                last.then_inc(S["w_t_made"], 1)
                pe.wait_ge(S["w_t_copied"], 1)
                pe.wait_ge(S["heads_ready"], 1)
                for k_ in range(DC):
                    for n_ in range(DC):
                        last = nc.tensor.matmul(ps_lr[:, k_ * 2 * H:(k_ + 1) * 2 * H],
                                                w_gat_t[:, n_, k_ * P:(k_ + 1) * P],
                                                attn_heads[:, n_].rearrange("p a h -> p (a h)"),
                                                start=n_ == 0, stop=n_ == DC - 1)
                last.then_inc(S["wa_made"], 1)
                pe.wait_ge(S["weights_ready"], 1)
                if first:
                    nc.tensor.matmul(ps_kv[:], zeros[:, 0:P], zeros[:], start=True, stop=False, skip_group_check=True)
                    nc.tensor.matmul(ps_norm[:, 0:DC], zeros[:, 0:P], zeros[:, 0:DC], start=True, stop=False,
                                     skip_group_check=True)

                def transposes(i, j):
                    pe.wait_ge(S["xn_ready"], i * TB + j + 1)
                    for c in range(DC):
                        last = nc.tensor.transpose(ps_xt[j % 2][:, c * P:(c + 1) * P], xn[:, j, c * P:(c + 1) * P], ident)
                    last.then_inc(S["xt_made"], 1)

                with pe.Fori(0, NBLK) as i:
                    transposes(i, 0)
                    for j in range(TB):
                        if j + 1 < TB:
                            transposes(i, j + 1)
                        pe.wait_ge(S["xt_copied"], i * TB + j + 1)
                        if j >= 2:
                            pe.wait_ge(S["qkv_ready"], i * TB + j - 1)
                        for c in range(DC):
                            a, o = xt[:, j % 2, c], dict(start=c == 0, stop=c == DC - 1)
                            nc.tensor.matmul(ps_qk[j % 2][:], a, w_qkv[:, c, 0:2 * D], **o)
                        if j:
                            pe.wait_ge(S["row_ready"], i * TB + j)
                        for c in range(DC):
                            a, o = xt[:, j % 2, c], dict(start=c == 0, stop=c == DC - 1)
                            nc.tensor.matmul(ps_gv[:, 0:D], a, w_gat[:, c, 0:D], **o)
                        for c in range(DC):
                            a, o = xt[:, j % 2, c], dict(start=c == 0, stop=c == DC - 1)
                            nc.tensor.matmul(ps_gv[:, D:2 * D], a, w_qkv[:, c, 2 * D:3 * D], **o)
                        for c in range(DC):
                            a, o = xt[:, j % 2, c], dict(start=c == 0, stop=c == DC - 1)
                            last = nc.tensor.matmul(ps_lr[:, 0:2 * H], a, w_gat[:, c, D:D + 2 * H], **o)
                        last.then_inc(S["projected"], 1)
                    if first:
                        pe.wait_ge(S["k_ready"], i + 1)
                        for j in range(TB):
                            for c in range(DC):
                                nc.tensor.matmul(ps_kv[:, c * D:(c + 1) * D], v[:, j, c * P:(c + 1) * P], k2[:, j, :],
                                                 start=False, stop=False, skip_group_check=True)
                        pe.wait_ge(S["k_square_ready"], i + 1)
                        for j in range(TB):
                            for c in range(DC):
                                last = nc.tensor.matmul(ps_norm[:, c:c + 1], k_square[:, j, c * P:(c + 1) * P],
                                                        col(keep, "ones")[:, 0:1], start=False, stop=False,
                                                        skip_group_check=True)
                if first:
                    nc.tensor.matmul(ps_norm[:, 0:DC], zeros[:, 0:P], zeros[:, 0:DC], start=False, stop=True,
                                     skip_group_check=True)
                    nc.tensor.matmul(ps_kv[:], zeros[:, 0:P], zeros[:], start=False, stop=True,
                                     skip_group_check=True).then_inc(S["kv_done"], 1)
                    pe.wait_ge(S["kv_copied"], 1)
                    for c in range(DC):
                        for d in range(DC):
                            last = nc.tensor.matmul(ps_qk[0][:, c * D:(c + 1) * D], kv_t[:, d, c * P:(c + 1) * P],
                                                    w_out[:, d, :], start=d == 0, stop=d == DC - 1)
                    last.then_inc(S["kw_made"], 1)
                else:
                    pe.wait_ge(S["max_ready"], 1)
                    for c in range(DC):
                        last = nc.tensor.transpose(ps_kv[:, c * P:(c + 1) * P], block_max[:, c * P:(c + 1) * P], ident)
                    last.then_inc(S["max_t_made"], 1)
                    pe.wait_ge(S["diag_ready"], 1)
                    for c in range(DC):
                        last = nc.tensor.matmul(ps_norm[:, c * P:(c + 1) * P], col(keep, "ones"), diag[:, c],
                                                start=True, stop=True)
                    last.then_inc(S["max_row_made"], 1)


def edge_stage(nc, keep, io, layer):
    H = 4 if layer == 0 else 8
    ROW = D + H
    GH = G * H
    BF16 = mybir.dt.bfloat16
    NROWS = 3
    table = io[f"table{layer}"]
    acc, left_max, right = keep["acc"], keep["left_max"], keep["right"]
    with Stage(nc, f"edge{layer}") as st:
        dst = st.sb("dst", [P, NM * G])
        srcs = st.sb("srcs", [P, NM * G], I32)
        index = st.sb("index", [P, NROWS, G], I32)
        rows = st.sb("rows", [P, NROWS, G * ROW])
        local = st.sb("local", [P, G])
        onehot = st.sb("onehot", [P, 2, G, P])
        onehot_b = st.sb("onehot_b", [P, G, P], BF16)
        onehot_t = st.sb("onehot_t", [P, G, P])
        flat = st.sb("flat", [P, 2, G, H])
        dst_t = st.sb("dst_t", [P, P])
        border = st.sb("border", [P, P + 1])
        reset = st.sb("reset", [P, P])
        running = st.sb("running", [P, P])
        at_last = st.sb("at_last", [P, P])
        values = st.sb("values", [P, G, 2, H])
        absent = st.sb("absent", [P, G, H])
        new_max = st.sb("new_max", [P, H])
        z = st.sb("z", [P, 2, H])
        shifts = st.sb("shifts", [P, 2, H])
        node_side = st.sb("node_side", [P, 2, H])
        fade = st.sb("fade", [P, H])
        logit = st.sb("logit", [P, G, H])
        weighted = st.sb("weighted", [P, 2, G, ROW])
        ident_b = st.sb("ident_b", [P, P], BF16)
        ps_t = st.banks("ps_t", 1)[0]
        ps_o = [st.stack.enter_context(nc.psum_tensor(f"{st.name}_ps_o{n}", [P, 1024], BF16)) for n in range(2)]
        ps_b = st.banks("ps_b", 1)[0]
        ps_m = st.banks("ps_m", 1)[0]
        ps_e = st.banks("ps_e", 1)[0]
        ps_acc = st.banks("ps_acc", 2)
        S = {n: st.sem(n) for n in (
            "edges_in passed chain prepared index_ready tick gather0 gather1 gather2 macro_ready onehot_b_ready onehot_ready flat_ready "
            "ident_ready t_made dst_t_ready at_last_ready back_made values_ready onehot_t_made onehot_t_copied locals_made "
            "node_side_ready fade_ready expanded logit_ready exp_ready rows_weighted summed").split()}
        ident = col(keep, "ident")
        gather = [S[f"gather{n}"] for n in range(NROWS)]
        dst_int = weighted[:].rearrange("p a g r -> p (a g r)")[:, 0:NM * G].bitcast(I32)
        with nc.Block() as block:
            @block.sync
            def _(sp):
                sp.dma_start(srcs[:], io["src"]).then_inc(S["edges_in"], 16)
                sp.dma_start(dst_int, io["dst"]).then_inc(S["edges_in"], 16)
                sp.wait_ge(S["edges_in"], 32)

            @block.gpsimd
            def _(pool):
                pool.wait_ge(S["edges_in"], 32)

                def issue(m, buf, release):
                    if release:
                        last = pool.value_load(keep["last_step"][0:1, bass.ds(m - NROWS, 1)], min_val=0, max_val=NSTEP)
                        pool.wait_ge(S["rows_weighted"], last * 4 + 4)
                        pool.sem_inc(S["tick"], 1)
                    nc.gpsimd.tensor_copy(index[:, buf, :], srcs[:, bass.ds(m * G, G)]).then_inc(S["index_ready"], 1)
                    pool.wait_ge(S["index_ready"], m + 1)
                    pool.sem_inc(S["tick"], 1)
                    for c in range(G):
                        pool.indirect_dma_start(
                            out=rows[:, buf, c * ROW:(c + 1) * ROW], out_offset=None, in_=table,
                            in_offset=bass.IndirectOffsetOnAxis(ap=index[:, buf, c:c + 1], axis=0)
                        ).then_inc(gather[buf], 16)

                def confirm(turn, buf):
                    pool.wait_ge(gather[buf], (turn + 1) * (16 * G))
                    pool.sem_inc(S["macro_ready"], 1)

                for m in range(NROWS):
                    issue(m, m, False)
                    if m:
                        confirm(0, m - 1)
                with pool.Fori(1, NM // NROWS) as i:
                    for buf in range(NROWS):
                        issue(i * NROWS + buf, buf, True)
                        if buf:
                            confirm(i, buf - 1)
                        else:
                            confirm(i - 1, NROWS - 1)
                for m in range(NM // NROWS * NROWS, NM):
                    issue(m, m % NROWS, True)
                    confirm((m - 1) // NROWS, (m - 1) % NROWS)
                confirm((NM - 1) // NROWS, (NM - 1) % NROWS)

            @block.vector
            def _(dve):
                link = Link(dve, S["chain"])
                one = lambda a: a.rearrange("p a h -> p (a h)")

                def macro(s):
                    return dve.value_load(keep["macro_of"][0:1, bass.ds(s, 1)], min_val=0, max_val=NM - 1)

                def got(m):
                    return rows[:, bass.ds(m % NROWS, 1), :].rearrange("p a (g r) -> p (a g) r", r=ROW)

                def tile(s, m):
                    return nc.s_assert_within(s - m, 0, NTA - 1, skip_runtime_bounds_check_because=
                                              "a step's macro is the number of macros whose last step is before it")

                def sums_of(s, m):
                    return one(acc[:, bass.ds(tile(s, m), 1), :])

                def spread(s, m):
                    link(nc.vector.tensor_scalar(local[:], dst[:, bass.ds(m * G, G)], keep["node0"][:, bass.ds(s, 1)],
                                                 None, ALU.subtract))
                    nc.vector.tensor_copy(flat[:, 1], cast(local[:], H))
                    dve.wait_ge(S["macro_ready"], m + 1)
                    nc.vector.tensor_scalar(flat[:, 0], got(m)[:, :, D:ROW], 1.0, None, ALU.mult).then_inc(S["flat_ready"], 1)
                    nc.vector.tensor_tensor(onehot_b[:], col(keep, "iota").unsqueeze(1).to_broadcast([P, G, P]),
                                            cast(local[:], P), ALU.is_equal).then_inc(S["onehot_b_ready"], 1)

                def local_maxima(s):
                    dve.wait_ge(S["dst_t_ready"], s + 1)
                    link(nc.vector.tensor_tensor(border[0:GH, 1:P], dst_t[0:GH, 1:P], dst_t[0:GH, 0:P - 1], ALU.not_equal))
                    link(nc.vector.tensor_scalar(reset[0:GH], border[0:GH, 0:P], -BIG, None, ALU.mult))
                    link(nc.vector.tensor_tensor_scan(running[0:GH], reset[0:GH], ps_t[0:GH, 0:P], -BIG, ALU.add, ALU.max))
                    nc.vector.tensor_tensor(at_last[0:GH], running[0:GH], border[0:GH, 1:P + 1], ALU.mult)\
                        .then_inc(S["at_last_ready"], 1)

                def maxima(s, m):
                    t = tile(s, m)
                    er, old_max = one(right[:, bass.ds(t, 1), 0:H]), one(left_max[:, bass.ds(t, 1), 0:H])
                    dve.wait_ge(S["locals_made"], s + 1)
                    loc = ps_m[:, 0:2 * GH].rearrange("p (g a h) -> p g a h", g=G, a=2)
                    link(nc.vector.tensor_scalar(absent[:], loc[:, :, 1, :], BIG, BIG, ALU.mult, ALU.subtract))
                    link(nc.vector.tensor_tensor(absent[:], absent[:], loc[:, :, 0, :], ALU.add))
                    link(nc.vector.tensor_reduce(new_max[:], absent[:].rearrange("p g h -> p h g"), AX.X, ALU.max))
                    nc.vector.tensor_tensor(z[:, 0], old_max, er, ALU.add)
                    link(nc.vector.tensor_tensor(new_max[:], new_max[:], old_max, ALU.max))
                    nc.vector.tensor_scalar(old_max, new_max[:], 1.0, None, ALU.mult)
                    link(nc.vector.tensor_tensor(z[:, 1], new_max[:], er, ALU.add))
                    nc.vector.tensor_scalar(node_side[:, 0], er, 1.0, None, ALU.mult)
                    nc.vector.scalar_tensor_tensor(node_side[:, 1], z[:, 1], NEG_SLOPE, z[:, 1], ALU.mult, ALU.max)\
                        .then_inc(S["node_side_ready"], 1)
                    link(nc.vector.scalar_tensor_tensor(shifts[:], z[:], NEG_SLOPE, z[:], ALU.mult, ALU.max))
                    nc.vector.tensor_tensor(fade[:], shifts[:, 0], shifts[:, 1], ALU.subtract).then_inc(S["prepared"], 1)

                def logits(s):
                    dve.wait_ge(S["expanded"], s + 1)
                    node = ps_e[:, 0:2 * GH].rearrange("p (g a h) -> p g a h", g=G, a=2)
                    link(nc.vector.tensor_tensor(logit[:], node[:, :, 0, :], flat[:, 0], ALU.add))
                    link(nc.vector.scalar_tensor_tensor(logit[:], logit[:], NEG_SLOPE, logit[:], ALU.mult, ALU.max))
                    link(nc.vector.tensor_tensor(logit[:], logit[:], node[:, :, 1, :], ALU.subtract))
                    nc.vector.tensor_scalar(logit[:], logit[:], 0.0, None, ALU.min).then_inc(S["logit_ready"], 1)

                def let_fade(s, m):
                    mine = sums_of(s, m)
                    dve.wait_ge(S["fade_ready"], s + 1)
                    nc.vector.tensor_tensor(mine[:, 0:D].rearrange("p (h d) -> p h d", h=H),
                                            mine[:, 0:D].rearrange("p (h d) -> p h d", h=H), cast(fade[:], D // H), ALU.mult)
                    link(nc.vector.tensor_tensor(mine[:, D:ROW], mine[:, D:ROW], fade[:], ALU.mult))
                    dve.wait_ge(S["exp_ready"], s + 1)
                    dve.sem_inc(S["passed"], 1)

                def weigh(s, m, par, part):
                    a, b = part * G // 4, (part + 1) * G // 4
                    nc.vector.tensor_tensor(weighted[:, par, a:b, 0:D].rearrange("p g (h d) -> p g h d", h=H),
                                            got(m)[:, a:b, 0:D].rearrange("p g (h d) -> p g h d", h=H),
                                            weighted[:, par, a:b, D:ROW].unsqueeze(3).to_broadcast([P, G // 4, H, D // H]),
                                            ALU.mult).then_inc(S["rows_weighted"], 1)

                def add(s, m, par):
                    mine = sums_of(s, m)
                    dve.wait_ge(S["summed"], s + 1)
                    link(nc.vector.tensor_tensor(mine[:, 0:ROW], mine[:, 0:ROW], ps_acc[par][:, 0:ROW], ALU.add))

                def round_of(s, par, before, now, after):
                    spread(s + 1, after)
                    if before is not None:
                        add(s - 1, before, 1 - par)
                    let_fade(s, now)
                    weigh(s, now, par, 0)
                    local_maxima(s + 1)
                    weigh(s, now, par, 1)
                    weigh(s, now, par, 2)
                    maxima(s + 1, after)
                    weigh(s, now, par, 3)
                    logits(s + 1)

                dve.wait_ge(S["edges_in"], 32)
                nc.vector.tensor_copy(dst[:], dst_int)
                nc.vector.tensor_copy(ident_b[:], ident).then_inc(S["ident_ready"], 1)
                first_tile = 0 if layer == 0 else NT
                nc.vector.memset(acc[:, first_tile:NTA, :], 0.0)
                nc.vector.memset(left_max[:, first_tile:NTA, :], -BIG)
                link(nc.vector.memset(border[:], 1.0))
                dve.sem_inc(S["passed"], 1)
                m0 = macro(0)
                spread(0, m0)
                local_maxima(0)
                maxima(0, m0)
                logits(0)
                round_of(0, 0, None, m0, macro(1))
                with dve.Fori(0, (NSTEP - 2) // 2) as i:
                    link.loop(i, 30)
                    m0, m1, m2, m3 = (macro(i * 2 + n) for n in range(4))
                    round_of(i * 2 + 1, 1, m0, m1, m2)
                    round_of(i * 2 + 2, 0, m1, m2, m3)
                link.leave((NSTEP - 2) // 2)
                m0, m1 = macro(NSTEP - 2), macro(NSTEP - 1)
                add(NSTEP - 2, m0, 0)
                let_fade(NSTEP - 1, m1)
                for part in range(4):
                    weigh(NSTEP - 1, m1, 1, part)
                add(NSTEP - 1, m1, 1)

            @block.scalar
            def _(act):
                def front(s, par, again):
                    def transposed(k):
                        act.wait_ge(S["onehot_t_made"], s * 2 + k + 1)
                        nc.scalar.activation(onehot_t[:, 8 * k:8 * k + 8, :].rearrange("p g n -> p (g n)"), ps_o[k][:],
                                             ACT.Copy).then_inc(S["onehot_t_copied"], 1)

                    act.wait_ge(S["t_made"], s + 1)
                    nc.scalar.activation(dst_t[0:GH], ps_t[0:GH, P:2 * P], ACT.Copy).then_inc(S["dst_t_ready"], 1)
                    if again:
                        act.wait_ge(S["summed"], s - 1)
                    act.wait_ge(S["onehot_b_ready"], s + 1)
                    nc.scalar.activation(onehot[:, par], onehot_b[:], ACT.Copy).then_inc(S["onehot_ready"], 1)
                    transposed(0)
                    act.wait_ge(S["back_made"], s + 1)
                    nc.scalar.activation(values[:].rearrange("p g a h -> p a g h"),
                                         ps_b[:, 0:2 * GH].rearrange("p (a g h) -> p a g h", a=2, g=G),
                                         ACT.Copy).then_inc(S["values_ready"], 1)
                    transposed(1)
                    act.wait_ge(S["prepared"], s + 1)
                    nc.scalar.activation(fade[:], fade[:], ACT.Exp).then_inc(S["fade_ready"], 1)
                    act.wait_ge(S["logit_ready"], s + 1)
                    nc.scalar.activation(weighted[:, par, :, D:ROW], logit[:], ACT.Exp).then_inc(S["exp_ready"], 1)

                front(0, 0, False)
                front(1, 1, False)
                with act.Fori(1, NSTEP // 2) as i:
                    for par in range(2):
                        front(i * 2 + par, par, True)

            @block.tensor
            def _(pe):
                def transposes(s):
                    pe.wait_ge(S["flat_ready"], s + 1)
                    pe.sem_inc(S["passed"], 1)
                    for a in range(2):
                        last = nc.tensor.transpose(ps_t[0:GH, a * P:(a + 1) * P],
                                                   flat[:, a].rearrange("p g h -> p (g h)"), ident)
                    last.then_inc(S["t_made"], 1)
                    pe.wait_ge(S["onehot_b_ready"], s + 1)
                    for k in range(2):
                        for c in range(8):
                            last = nc.tensor.transpose(ps_o[k][:, c * P:(c + 1) * P], onehot_b[:, 8 * k + c, :], ident_b[:])
                        last.then_inc(S["onehot_t_made"], 1)

                def back(s):
                    pe.wait_ge(S["at_last_ready"], s + 1)
                    pe.sem_inc(S["passed"], 1)
                    nc.tensor.transpose(ps_b[:, 0:GH], at_last[0:GH], ident[0:GH, 0:GH])
                    nc.tensor.transpose(ps_b[:, GH:2 * GH], border[0:GH, 1:P + 1], ident[0:GH, 0:GH])\
                        .then_inc(S["back_made"], 1)

                def locals_of(s, par):
                    pe.wait_ge(S["onehot_ready"], s + 1)
                    pe.wait_ge(S["values_ready"], s + 1)
                    for c in range(G):
                        last = nc.tensor.matmul(ps_m[:, c * 2 * H:(c + 1) * 2 * H], onehot[:, par, c, :],
                                                values[:, c].rearrange("p a h -> p (a h)"), start=True, stop=True)
                    last.then_inc(S["locals_made"], 1)

                def expand(s):
                    pe.wait_ge(S["node_side_ready"], s + 1)
                    pe.wait_ge(S["onehot_t_copied"], (s + 1) * 2)
                    for c in range(G):
                        last = nc.tensor.matmul(ps_e[:, c * 2 * H:(c + 1) * 2 * H], onehot_t[:, c, :],
                                                node_side[:].rearrange("p a h -> p (a h)"), start=True, stop=True)
                    last.then_inc(S["expanded"], 1)

                def sum_up(s, par, chunks):
                    for c in chunks:
                        if c % (G // 4) == 0:
                            pe.wait_ge(S["rows_weighted"], s * 4 + c // (G // 4) + 1)
                        last = nc.tensor.matmul(ps_acc[par][:, 0:ROW], onehot[:, par, c, :], weighted[:, par, c, :],
                                                start=c == 0, stop=c == G - 1)
                    if c == G - 1:
                        last.then_inc(S["summed"], 1)

                def both(front, back_step, par):
                    transposes(front)
                    sum_up(back_step, par, range(0, 4))
                    back(front)
                    sum_up(back_step, par, range(4, 8))
                    locals_of(front, 1 - par)
                    sum_up(back_step, par, range(8, 12))
                    expand(front)
                    sum_up(back_step, par, range(12, G))

                pe.wait_ge(S["ident_ready"], 1)
                transposes(0)
                back(0)
                locals_of(0, 0)
                expand(0)
                both(1, 0, 0)
                with pe.Fori(0, (NSTEP - 2) // 2) as i:
                    for par in (1, 0):
                        s = i * 2 + (2 - par)
                        both(s + 1, s, par)
                sum_up(NSTEP - 1, 1, range(G))


def moe_stage(nc, keep, io):
    H, ROW = 4, D + 4
    acc = keep["acc"]
    with Stage(nc, "moe") as st:
        x = st.sb("x", [P, TB, D])
        xn = st.sb("xn", [P, TB, D])
        v = st.sb("v", [P, TB, D])
        q2 = st.sb("q2", [P, TB, D])
        elu = st.sb("elu", [P, TB, D])
        stats = st.sb("stats", [P, TB, 6])
        mv = st.sb("mv", [P, TB, 2])
        std = st.sb("std", [P, TB])
        rstd = st.sb("rstd", [P, TB])
        den = st.sb("den", [P, TB, H])
        vq_t = st.sb("vq_t", [P, 2 * DC, P])
        w_out = st.sb("w_out", [P, DC, D])
        b_out = st.sb("b_out", [P, D])
        gat_bias = st.sb("gat_bias", [P, D])
        r_w1 = st.sb("r_w1", [P, DC, P])
        r_b1 = st.sb("r_b1", [P, 1])
        r_w2 = st.sb("r_w2", [P, N_EXP])
        r_b2 = st.sb("r_b2", [P, N_EXP])
        w1 = st.sb("w1", [P, N_EXP, DC, D])
        b1 = st.sb("b1", [P, N_EXP, DC])
        w2 = st.sb("w2", [P, N_EXP, DC, D])
        b2 = st.sb("b2", [P, N_EXP, DC])
        w3 = st.sb("w3", [P, N_EXP, DC, D])
        b3 = st.sb("b3", [N_EXP, D])
        xt = st.sb("xt", [P, DC, TB * P])
        h1 = st.sb("h1", [P, DC, TB * P])
        h2 = st.sb("h2", [P, DC, TB * P])
        rh = h1
        prob = st.sb("prob", [P, TB, N_EXP])
        e_max = st.sb("e_max", [P, TB])
        e_sum = st.sb("e_sum", [P, TB])
        rank = st.sb("rank", [P, TB, N_EXP])
        greater = st.sb("greater", [P, TB, 36])
        equal = st.sb("equal", [P, TB, 36])
        gate = st.sb("gate", [P, TB, N_EXP])
        gate_t = st.sb("gate_t", [N_EXP, TB * P])
        ps_a = st.banks("ps_a", 2)
        ps_h = st.banks("ps_h", 4)
        ps_o = st.banks("ps_o", 2)
        S = {n: st.sem(n) for n in (
            "weights_in inputs_in passed passed_sp chain acc_read elu_ready vq_made vq_copied mixed mix_added moments_ready std_ready "
            "xn_ready xt_made xt_copied rh_made rh_ready logits_made gates_shifted probs_exp top_shifted top_exp gate_ready "
            "gate_t_made gate_t_copied up1_made h1_ready up2_made h2_ready down_made down_added stored "
            "neg_ready").split()}
        ident, eps = col(keep, "ident"), col(keep, "eps")
        W = [(w_out, "l0_w_out"), (b_out, "l0_b_out"), (gat_bias, "l0_gat_bias"), (r_w1, "r_w1"), (r_b1, "r_b1"),
             (r_w2, "r_w2"), (r_b2, "r_b2"), (w1, "e_w1"), (b1, "e_b1"), (w2, "e_w2"), (b2, "e_b2"), (w3, "e_w3"),
             (b3, "e_b3")]
        with nc.Block() as block:
            @block.sync
            def _(sp):
                for tile, name in W:
                    sp.dma_start(tile[:], io[name]).then_inc(S["weights_in"], 16)
                with sp.Fori(0, NBLK) as i:
                    for tile, name in ((x, "x0"), (xn, "xn"), (v, "v"), (q2, "q")):
                        sp.dma_start(tile[:], block_of(io[name], i)).then_inc(S["inputs_in"], 16)
                    sp.wait_ge(S["down_added"], (i + 1) * (TB * (N_EXP + 1)))
                    sp.dma_start(block_of(io["x2"], i), x[:]).then_inc(S["stored"], 16)
                    sp.wait_ge(S["stored"], (i + 1) * 16)
                    sp.sem_inc(S["passed_sp"], 1)
                sp.wait_ge(S["weights_in"], 16 * len(W))

            @block.vector
            def _(dve):
                link = Link(dve, S["chain"])
                dve.wait_ge(S["weights_in"], 16 * len(W))
                with dve.Fori(0, NBLK) as i:
                    link.loop(i, 23)
                    mine = acc[:, bass.ds(i * TB, TB), :]
                    link(nc.vector.tensor_scalar(den[:], mine[:, :, D:ROW], 1e-30, None, ALU.max))
                    link(nc.vector.reciprocal(den[:], den[:]))
                    for h in range(H):
                        last = nc.vector.tensor_tensor(elu[:, :, h * 64:(h + 1) * 64], mine[:, :, h * 64:(h + 1) * 64],
                                                       cast(den[:, :, h], 64), ALU.mult)
                    link(last)
                    link(nc.vector.tensor_tensor(elu[:], elu[:], gat_bias[:].unsqueeze(1).to_broadcast([P, TB, D]), ALU.add))
                    dve.wait_ge(S["inputs_in"], (i + 1) * 64)
                    link(nc.vector.tensor_tensor(x[:], x[:], xn[:], ALU.add))
                    link(nc.vector.scalar_tensor_tensor(x[:], elu[:], 0.0, x[:], ALU.max, ALU.add))
                    nc.vector.tensor_scalar(elu[:], elu[:], 0.0, None, ALU.min).then_inc(S["neg_ready"], 1)
                    link(nc.vector.tensor_tensor(x[:], x[:], b_out[:].unsqueeze(1).to_broadcast([P, TB, D]), ALU.add))
                    dve.wait_ge(S["elu_ready"], i + 1)
                    link(nc.vector.scalar_tensor_tensor(x[:], elu[:], -1.0, x[:], ALU.add, ALU.add))
                    for j in range(TB):
                        dve.wait_ge(S["mixed"], i * TB + j + 1)
                        nc.vector.tensor_tensor(x[:, j, :], x[:, j, :], ps_o[j % 2][:, 0:D], ALU.add)\
                            .then_inc(S["mix_added"], 1)
                    dve.wait_ge(S["mix_added"], (i + 1) * TB)
                    row_moments(nc, link, x, stats, mv, S["passed"]).then_inc(S["moments_ready"], 1)
                    dve.wait_ge(S["std_ready"], i + 1)
                    link(nc.vector.reciprocal(rstd[:], std[:]))
                    for j in range(TB):
                        nc.vector.tensor_scalar(xn[:, j, :], x[:, j, :], mv[:, j, 0:1], rstd[:, j:j + 1],
                                                ALU.subtract, ALU.mult).then_inc(S["xn_ready"], 1)
                    dve.wait_ge(S["logits_made"], i + 1)
                    link(nc.vector.tensor_tensor(prob[:], ps_o[1][:, 0:TB * N_EXP].rearrange("p (j e) -> p j e", j=TB),
                                                 r_b2[:].unsqueeze(1).to_broadcast([P, TB, N_EXP]), ALU.add))
                    link(nc.vector.tensor_reduce(e_max[:], prob[:], AX.X, ALU.max))
                    nc.vector.tensor_tensor(prob[:], prob[:], cast(e_max[:], N_EXP), ALU.subtract)\
                        .then_inc(S["gates_shifted"], 1)
                    dve.wait_ge(S["probs_exp"], i + 1)
                    link(nc.vector.tensor_reduce(e_sum[:], prob[:], AX.X, ALU.add))
                    link(nc.vector.reciprocal(e_sum[:], e_sum[:]))
                    link(nc.vector.tensor_tensor(prob[:], prob[:], cast(e_sum[:], N_EXP), ALU.mult))
                    of = prob[:].unsqueeze(3).to_broadcast([P, TB, N_EXP, N_EXP])
                    other = prob[:].unsqueeze(2).to_broadcast([P, TB, N_EXP, N_EXP])
                    g4, e4 = (a[:].rearrange("p j (e f) -> p j e f", e=N_EXP) for a in (greater, equal))
                    nc.vector.tensor_tensor(g4, of, other, ALU.is_lt)
                    link(nc.vector.tensor_tensor(e4, of, other, ALU.is_equal))
                    link(nc.vector.tensor_tensor(equal[:], equal[:], col(keep, "earlier").unsqueeze(1)
                                                 .to_broadcast([P, TB, 36]), ALU.mult))
                    link(nc.vector.tensor_tensor(greater[:], greater[:], equal[:], ALU.add))
                    link(nc.vector.tensor_reduce(rank[:], g4, AX.X, ALU.add))
                    nc.vector.tensor_scalar(rank[:], rank[:], 1.5, None, ALU.is_lt)
                    link(nc.vector.tensor_reduce(e_max[:], prob[:], AX.X, ALU.max))
                    nc.vector.tensor_tensor(prob[:], prob[:], cast(e_max[:], N_EXP), ALU.subtract)\
                        .then_inc(S["top_shifted"], 1)
                    dve.wait_ge(S["top_exp"], i + 1)
                    link(nc.vector.tensor_tensor(gate[:], prob[:], rank[:], ALU.mult))
                    link(nc.vector.tensor_reduce(e_sum[:], gate[:], AX.X, ALU.add))
                    link(nc.vector.reciprocal(e_sum[:], e_sum[:]))
                    nc.vector.tensor_tensor(gate[:], gate[:], cast(e_sum[:], N_EXP), ALU.mult).then_inc(S["gate_ready"], 1)
                    dve.wait_ge(S["gate_ready"], i + 1)
                    for e in range(-1, N_EXP):
                        for j in range(TB):
                            n = (e + 1) * TB + j
                            dve.wait_ge(S["down_made"], i * (TB * (N_EXP + 1)) + n + 1)
                            if e >= 0:
                                nc.vector.scalar_tensor_tensor(x[:, j, :], ps_o[n % 2][:, 0:D], gate[:, j, e:e + 1], x[:, j, :],
                                                               ALU.mult, ALU.add).then_inc(S["down_added"], 1)
                            else:
                                nc.vector.tensor_tensor(x[:, j, :], x[:, j, :], ps_o[n % 2][:, 0:D], ALU.add)\
                                    .then_inc(S["down_added"], 1)
                        dve.wait_ge(S["down_added"], i * (TB * (N_EXP + 1)) + (e + 2) * TB)
                link.leave(NBLK)

            @block.scalar
            def _(act):
                act.wait_ge(S["weights_in"], 16 * len(W))
                with act.Fori(0, NBLK) as i:
                    for j in range(TB):
                        act.wait_ge(S["vq_made"], i * TB + j + 1)
                        nc.scalar.activation(vq_t[:].rearrange("p k n -> p (k n)"), ps_a[j % 2][:], ACT.Copy)\
                            .then_inc(S["vq_copied"], 1)
                        if j == 0:
                            act.wait_ge(S["neg_ready"], i + 1)
                            nc.scalar.activation(elu[:], elu[:], ACT.Exp).then_inc(S["elu_ready"], 1)
                    act.wait_ge(S["moments_ready"], i + 1)
                    nc.scalar.activation(std[:], mv[:, :, 1], ACT.Sqrt, bias=eps).then_inc(S["std_ready"], 1)
                    for j in range(TB):
                        act.wait_ge(S["xt_made"], i * TB + j + 1)
                        nc.scalar.activation(xt[:, :, j * P:(j + 1) * P],
                                             ps_a[j % 2][:, 0:D].rearrange("p (k n) -> p k n", k=DC), ACT.Copy)\
                            .then_inc(S["xt_copied"], 1)
                    for half in range(2):
                        act.wait_ge(S["rh_made"], i * 2 + half + 1)
                        nc.scalar.activation(rh[:, 0, half * HALF:(half + 1) * HALF], ps_h[half][:, 0:HALF], ACT.Relu,
                                             bias=r_b1[:, 0:1]).then_inc(S["rh_ready"], 1)
                    act.wait_ge(S["gates_shifted"], i + 1)
                    nc.scalar.activation(prob[:], prob[:], ACT.Exp).then_inc(S["probs_exp"], 1)
                    act.wait_ge(S["top_shifted"], i + 1)
                    nc.scalar.activation(prob[:], prob[:], ACT.Exp).then_inc(S["top_exp"], 1)
                    act.wait_ge(S["gate_t_made"], i + 1)
                    nc.scalar.activation(gate_t[:, 0:4 * P], ps_a[0][0:N_EXP, :], ACT.Copy)
                    nc.scalar.activation(gate_t[:, 4 * P:TB * P], ps_a[1][0:N_EXP, 0:(TB - 4) * P], ACT.Copy)\
                        .then_inc(S["gate_t_copied"], 1)
                    for e in range(N_EXP):
                        for which, (out, b, made, ready) in enumerate(((h1, b1, "up1_made", "h1_ready"),
                                                                       (h2, b2, "up2_made", "h2_ready"))):
                            for n in range(4):
                                o, half = n // 2, n % 2
                                act.wait_ge(S[made], i * (4 * N_EXP) + e * 4 + n + 1)
                                nc.scalar.activation(out[:, o, half * HALF:(half + 1) * HALF], ps_h[n][:, 0:HALF],
                                                     ACT.Relu, bias=b[:, e, o:o + 1]).then_inc(S[ready], 1)

            @block.tensor
            def _(pe):
                pe.wait_ge(S["weights_in"], 16 * len(W))
                with pe.Fori(0, NBLK) as i:
                    pe.wait_ge(S["inputs_in"], (i + 1) * 64)
                    for j in range(TB):
                        if j >= 2:
                            pe.wait_ge(S["vq_copied"], i * TB + j - 1)
                        for c in range(DC):
                            nc.tensor.transpose(ps_a[j % 2][:, c * P:(c + 1) * P], v[:, j, c * P:(c + 1) * P], ident)
                        for c in range(DC):
                            last = nc.tensor.transpose(ps_a[j % 2][:, (DC + c) * P:(DC + c + 1) * P],
                                                       q2[:, j, c * P:(c + 1) * P], ident)
                        last.then_inc(S["vq_made"], 1)
                        pe.wait_ge(S["vq_copied"], i * TB + j + 1)
                        if j >= 2:
                            pe.wait_ge(S["mix_added"], i * TB + j - 1)
                        for c in range(2 * DC):
                            w = (w_out if c < DC else keep["kw"])[:, c % DC, :]
                            last = nc.tensor.matmul(ps_o[j % 2][:, 0:D], vq_t[:, c], w, start=c == 0, stop=c == 2 * DC - 1)
                        last.then_inc(S["mixed"], 1)
                    for j in range(TB):
                        pe.wait_ge(S["xn_ready"], i * TB + j + 1)
                        if j >= 2:
                            pe.wait_ge(S["xt_copied"], i * TB + j - 1)
                        for c in range(DC):
                            last = nc.tensor.transpose(ps_a[j % 2][:, c * P:(c + 1) * P], xn[:, j, c * P:(c + 1) * P], ident)
                        last.then_inc(S["xt_made"], 1)
                    pe.wait_ge(S["xt_copied"], (i + 1) * TB)
                    for half in range(2):
                        for c in range(DC):
                            last = nc.tensor.matmul(ps_h[half][:, 0:HALF], r_w1[:, c, :],
                                                    xt[:, c, half * HALF:(half + 1) * HALF], start=c == 0, stop=c == DC - 1)
                        last.then_inc(S["rh_made"], 1)
                    pe.wait_ge(S["rh_ready"], (i + 1) * 2)
                    for j in range(TB):
                        last = nc.tensor.matmul(ps_o[1][:, j * N_EXP:(j + 1) * N_EXP], rh[:, 0, j * P:(j + 1) * P],
                                                r_w2[:], start=True, stop=True)
                    last.then_inc(S["logits_made"], 1)

                    def up(e, src, w, ready, made, before):
                        for n in range(4):
                            o, half = n // 2, n % 2
                            if before is not None:
                                pe.wait_ge(S[before[0]], before[1] + n + 1)
                            if ready is not None and n == 0:
                                pe.wait_ge(S[ready], i * (4 * N_EXP) + e * 4 + 4)
                            for c in range(DC):
                                last = nc.tensor.matmul(ps_h[n][:, 0:HALF], w[:, e, c, o * P:(o + 1) * P],
                                                        src[:, c, half * HALF:(half + 1) * HALF],
                                                        start=c == 0, stop=c == DC - 1)
                            last.then_inc(S[made], 1)

                    def down(n, lhs_rhs):
                        if n >= 2:
                            pe.wait_ge(S["down_added"], i * (TB * (N_EXP + 1)) + n - 1)
                        for c, (a, b) in enumerate(lhs_rhs):
                            last = nc.tensor.matmul(ps_o[n % 2][:, 0:D], a, b, start=c == 0, stop=c == len(lhs_rhs) - 1)
                        last.then_inc(S["down_made"], 1)

                    up(0, xt, w1, None, "up1_made", None)
                    pe.wait_ge(S["gate_ready"], i + 1)
                    for j in range(TB):
                        last = nc.tensor.transpose(ps_a[j // 4][0:N_EXP, (j % 4) * P:(j % 4 + 1) * P], gate[:, j, :], ident)
                    last.then_inc(S["gate_t_made"], 1)
                    pe.wait_ge(S["gate_t_copied"], i + 1)
                    for j in range(TB):
                        down(j, [(gate_t[:, j * P:(j + 1) * P], b3[:])])
                    for e in range(N_EXP):
                        at = i * (4 * N_EXP) + e * 4
                        if e:
                            up(e, xt, w1, None, "up1_made", ("h2_ready", at - 4))
                        up(e, h1, w2, "h1_ready", "up2_made", ("h1_ready", at))
                        pe.wait_ge(S["h2_ready"], at + 4)
                        for j in range(TB):
                            down((e + 1) * TB + j, [(h2[:, c, j * P:(j + 1) * P], w3[:, e, c, :]) for c in range(DC)])


def context_stage(nc, keep, io):
    with Stage(nc, "context") as st:
        k = st.sb("k", [P, 2, TB, D])
        v = st.sb("v", [P, 2, TB, D])
        expk = st.sb("expk", [P, TB, D])
        zeros = st.sb("zeros", [P, D])
        w_out = st.sb("w_out", [P, DC, D])
        context_t = st.sb("context_t", [P, DC, P])
        inv = st.sb("inv", [P, DC])
        ps_c = st.banks("ps_c", 1)[0]
        ps_s = st.banks("ps_s", 1)[0]
        ps_w = st.banks("ps_w", 1)[0]
        S = {n: st.sem(n) for n in ("weights_in k_in v_in chain zeros_ready shifted exp_ready used done "
                                    "context_ready product_made passed").split()}
        with nc.Block() as block:
            @block.sync
            def _(sp):
                sp.dma_start(w_out[:], io["l1_w_out"]).then_inc(S["weights_in"], 16)
                with sp.Fori(0, NBLK) as i:
                    sp.wait_ge(S["used"], i + 1)
                    sp.dma_start(k[:, 0], block_of(io["k"], i)).then_inc(S["k_in"], 16)
                    sp.dma_start(v[:, 0], block_of(io["v"], i)).then_inc(S["v_in"], 16)
                sp.wait_ge(S["weights_in"], 16)

            @block.vector
            def _(dve):
                link = Link(dve, S["chain"])
                nc.vector.memset(zeros[:], 0.0).then_inc(S["zeros_ready"], 1)
                with dve.Fori(0, NBLK) as i:
                    dve.wait_ge(S["k_in"], (i + 1) * 16)
                    nc.vector.tensor_tensor(expk[:], k[:, 0], keep["k_max"][:].unsqueeze(1).to_broadcast([P, TB, D]),
                                            ALU.subtract).then_inc(S["shifted"], 1)
                    dve.wait_ge(S["used"], i + 2)
                    dve.sem_inc(S["passed"], 1)
                dve.wait_ge(S["done"], 1)
                for c in range(DC):
                    last = nc.vector.tensor_tensor(context_t[:, c], ps_c[:, c * P:(c + 1) * P], col(keep, "blockmask"), ALU.mult)
                last.then_inc(S["context_ready"], 1)
                link(nc.vector.reciprocal(inv[:], ps_s[:, 0:DC]))
                link(nc.vector.tensor_scalar(inv[:], inv[:], float(32) ** -0.5, None, ALU.mult))
                dve.wait_ge(S["product_made"], 1)
                for c in range(DC):
                    last = nc.vector.tensor_scalar(keep["kw"][:, c, :], ps_w[:, c * D:(c + 1) * D], inv[:, c:c + 1], None,
                                                   ALU.mult)
                link(last)

            @block.scalar
            def _(act):
                with act.Fori(0, NBLK) as i:
                    act.wait_ge(S["shifted"], i + 1)
                    nc.scalar.activation(expk[:], expk[:], ACT.Exp).then_inc(S["exp_ready"], 1)

            @block.tensor
            def _(pe):
                pe.wait_ge(S["zeros_ready"], 1)
                nc.tensor.matmul(ps_c[:, 0:D], zeros[:, 0:P], zeros[:], start=True, stop=False, skip_group_check=True)
                nc.tensor.matmul(ps_s[:, 0:DC], zeros[:, 0:P], zeros[:, 0:DC], start=True, stop=False, skip_group_check=True)
                pe.sem_inc(S["used"], 1)
                with pe.Fori(0, NBLK) as i:
                    pe.wait_ge(S["exp_ready"], i + 1)
                    pe.wait_ge(S["v_in"], (i + 1) * 16)
                    for j in range(TB):
                        for c in range(DC):
                            nc.tensor.matmul(ps_c[:, c * P:(c + 1) * P], v[:, 0, j, c * P:(c + 1) * P],
                                             expk[:, j, c * P:(c + 1) * P], start=False, stop=False, skip_group_check=True)
                            last = nc.tensor.matmul(ps_s[:, c:c + 1], expk[:, j, c * P:(c + 1) * P],
                                                    col(keep, "ones")[:, 0:1], start=False, stop=False, skip_group_check=True)
                    last.then_inc(S["used"], 1)
                nc.tensor.matmul(ps_s[:, 0:DC], zeros[:, 0:P], zeros[:, 0:DC], start=False, stop=True, skip_group_check=True)
                nc.tensor.matmul(ps_c[:, 0:D], zeros[:, 0:P], zeros[:], start=False, stop=True, skip_group_check=True)\
                    .then_inc(S["done"], 1)
                pe.wait_ge(S["weights_in"], 16)
                pe.wait_ge(S["context_ready"], 1)
                for c in range(DC):
                    last = nc.tensor.matmul(ps_w[:, c * D:(c + 1) * D], context_t[:, c], w_out[:, c, :], start=True, stop=True)
                last.then_inc(S["product_made"], 1)


def mlp_stage(nc, keep, io):
    H, ROW = 8, D + 8
    HID = 4 * D
    HC = HID // P
    acc = keep["acc"]
    with Stage(nc, "mlp") as st:
        x = st.sb("x", [P, TB, D])
        q = st.sb("q", [P, TB, D])
        gat = st.sb("gat", [P, TB, D])
        mix = st.sb("mix", [P, TB, D])
        xn = st.sb("xn", [P, TB, D])
        stats = st.sb("stats", [P, TB, 6])
        mv = st.sb("mv", [P, 3, TB, 2])
        std = st.sb("std", [P, 3, TB])
        rstd = st.sb("rstd", [P, 3, TB])
        den = st.sb("den", [P, TB, H])
        q_t = st.sb("q_t", [P, 2, D])
        gat_bias = st.sb("gat_bias", [P, D])
        gamma = st.sb("gamma", [P, D])
        beta = st.sb("beta", [P, D])
        mix_gamma = st.sb("mix_gamma", [P, D])
        wr = st.sb("wr", [P, D])
        br = st.sb("br", [P, 1])
        w1 = st.sb("w1", [P, DC, HID])
        b1 = st.sb("b1", [P, HC])
        w2 = st.sb("w2", [P, HC, D])
        b2 = st.sb("b2", [P, D])
        xt = st.sb("xt", [P, DC, TB * P])
        hid = st.sb("hid", [P, HC, TB * P])
        weight = st.sb("weight", [P, TB])
        ps_a = st.banks("ps_a", 2)
        ps_h = st.banks("ps_h", 4)
        ps_o = st.banks("ps_o", 2)
        S = {n: st.sem(n) for n in (
            "weights_in inputs_in passed passed_sp chain q_t_made q_t_copied mixed mix_copied moments_ready std_ready "
            "xn_ready xt_made xt_copied up_made hid_ready down_made down_added base_ready stored").split()}
        ident, eps = col(keep, "ident"), col(keep, "eps")
        W = [(gat_bias, "l1_gat_bias"), (gamma, "l1_gamma"), (beta, "l1_beta"), (mix_gamma, "l1_mix_gamma"),
             (wr, "f_wr"), (br, "f_br"), (w1, "f_w1"), (b1, "f_b1"), (w2, "f_w2"), (b2, "f_b2")]
        rows = lambda a: a[:].unsqueeze(1).to_broadcast([P, TB, D])
        with nc.Block() as block:
            @block.sync
            def _(sp):
                for tile, name in W:
                    sp.dma_start(tile[:], io[name]).then_inc(S["weights_in"], 16)
                with sp.Fori(0, NBLK) as i:
                    for tile, name in ((x, "x2"), (q, "q")):
                        sp.dma_start(tile[:], block_of(io[name], i)).then_inc(S["inputs_in"], 16)
                    sp.wait_ge(S["base_ready"], i + 1)
                    sp.dma_start(block_of(io["base"], i), x[:]).then_inc(S["stored"], 16)
                    sp.wait_ge(S["stored"], (i + 1) * 16)
                    sp.sem_inc(S["passed_sp"], 1)
                sp.wait_ge(S["weights_in"], 16 * len(W))

            @block.vector
            def _(dve):
                link = Link(dve, S["chain"])
                dve.wait_ge(S["weights_in"], 16 * len(W))
                with dve.Fori(0, NBLK) as i:
                    link.loop(i, 19)

                    def normed(n, a, out):
                        row_moments(nc, link, a, stats, mv[:, n], S["passed"]).then_inc(S["moments_ready"], 1)
                        dve.wait_ge(S["std_ready"], i * 3 + n + 1)
                        link(nc.vector.reciprocal(rstd[:, n, :], std[:, n, :]))
                        for j in range(TB):
                            last = nc.vector.tensor_scalar(out[:, j, :], a[:, j, :], mv[:, n, j, 0:1], rstd[:, n, j:j + 1],
                                                           ALU.subtract, ALU.mult)
                        return last

                    mine = acc[:, bass.ds(i * TB, TB), :]
                    link(nc.vector.tensor_scalar(den[:], mine[:, :, D:ROW], 1e-30, None, ALU.max))
                    link(nc.vector.reciprocal(den[:], den[:]))
                    for h in range(H):
                        last = nc.vector.tensor_tensor(gat[:, :, h * 32:(h + 1) * 32], mine[:, :, h * 32:(h + 1) * 32],
                                                       cast(den[:, :, h], 32), ALU.mult)
                    link(last)
                    link(nc.vector.tensor_tensor(gat[:], gat[:], rows(gat_bias), ALU.add))
                    link(normed(0, gat, gat))
                    link(nc.vector.tensor_tensor(gat[:], gat[:], rows(gamma), ALU.mult))
                    link(nc.vector.tensor_tensor(gat[:], gat[:], rows(beta), ALU.add))
                    dve.wait_ge(S["inputs_in"], (i + 1) * 32)
                    link(nc.vector.tensor_tensor(x[:], x[:], gat[:], ALU.add))
                    dve.wait_ge(S["mix_copied"], (i + 1) * TB)
                    link(normed(1, mix, mix))
                    link(nc.vector.tensor_tensor(mix[:], mix[:], rows(mix_gamma), ALU.mult))
                    link(nc.vector.tensor_tensor(x[:], x[:], mix[:], ALU.add))
                    normed(2, x, xn).then_inc(S["xn_ready"], 1)
                    dve.wait_ge(S["xn_ready"], i + 1)
                    nc.vector.tensor_tensor(x[:], x[:], xn[:], ALU.add).then_inc(S["base_ready"], 1)
                    link(nc.vector.tensor_tensor(gat[:], xn[:], rows(wr), ALU.mult))
                    link(nc.vector.tensor_reduce(weight[:], gat[:], AX.X, ALU.add))
                    nc.vector.tensor_scalar(keep["score"][:, bass.ds(i * TB, TB)], weight[:], br[:, 0:1], None, ALU.add)
                    for j in range(TB):
                        dve.wait_ge(S["down_made"], i * TB + j + 1)
                        nc.vector.tensor_tensor(acc[:, bass.ds(i * TB + j, 1), 0:D].rearrange("p a d -> p (a d)"),
                                                ps_o[j % 2][:, 0:D], b2[:], ALU.add).then_inc(S["down_added"], 1)
                link.leave(NBLK)

            @block.scalar
            def _(act):
                act.wait_ge(S["weights_in"], 16 * len(W))
                with act.Fori(0, NBLK) as i:
                    def root(n):
                        act.wait_ge(S["moments_ready"], i * 3 + n + 1)
                        nc.scalar.activation(std[:, n, :], mv[:, n, :, 1], ACT.Sqrt, bias=eps).then_inc(S["std_ready"], 1)

                    for j in range(TB):
                        act.wait_ge(S["q_t_made"], i * TB + j + 1)
                        nc.scalar.activation(q_t[:, j % 2], ps_a[j % 2][:, 0:D], ACT.Copy).then_inc(S["q_t_copied"], 1)
                        act.wait_ge(S["mixed"], i * TB + j + 1)
                        nc.scalar.activation(mix[:, j, :], ps_h[j % 2][:, 0:D], ACT.Copy).then_inc(S["mix_copied"], 1)
                    for n in range(3):
                        root(n)
                    for j in range(TB):
                        act.wait_ge(S["xt_made"], i * TB + j + 1)
                        nc.scalar.activation(xt[:, :, j * P:(j + 1) * P],
                                             ps_a[j % 2][:, 0:D].rearrange("p (k n) -> p k n", k=DC), ACT.Copy)\
                            .then_inc(S["xt_copied"], 1)
                    for n in range(2 * HC):
                        o, half = n // 2, n % 2
                        act.wait_ge(S["up_made"], i * (2 * HC) + n + 1)
                        nc.scalar.activation(hid[:, o, half * HALF:(half + 1) * HALF], ps_h[n % 4][:, 0:HALF],
                                             ACT.Gelu_apprx_tanh, bias=b1[:, o:o + 1]).then_inc(S["hid_ready"], 1)

            @block.tensor
            def _(pe):
                pe.wait_ge(S["weights_in"], 16 * len(W))
                with pe.Fori(0, NBLK) as i:
                    pe.wait_ge(S["inputs_in"], (i + 1) * 32)
                    for j in range(TB):
                        if j >= 2:
                            pe.wait_ge(S["q_t_copied"], i * TB + j - 1)
                        for c in range(DC):
                            last = nc.tensor.transpose(ps_a[j % 2][:, c * P:(c + 1) * P], q[:, j, c * P:(c + 1) * P], ident)
                        last.then_inc(S["q_t_made"], 1)
                        pe.wait_ge(S["q_t_copied"], i * TB + j + 1)
                        if j >= 2:
                            pe.wait_ge(S["mix_copied"], i * TB + j - 1)
                        for c in range(DC):
                            last = nc.tensor.matmul(ps_h[j % 2][:, 0:D], q_t[:, j % 2, c * P:(c + 1) * P], keep["kw"][:, c, :],
                                                    start=c == 0, stop=c == DC - 1)
                        last.then_inc(S["mixed"], 1)
                    pe.wait_ge(S["xn_ready"], i + 1)
                    for j in range(TB):
                        if j >= 2:
                            pe.wait_ge(S["xt_copied"], i * TB + j - 1)
                        for c in range(DC):
                            last = nc.tensor.transpose(ps_a[j % 2][:, c * P:(c + 1) * P], xn[:, j, c * P:(c + 1) * P], ident)
                        last.then_inc(S["xt_made"], 1)
                    pe.wait_ge(S["xt_copied"], (i + 1) * TB)
                    for n in range(2 * HC):
                        o, half = n // 2, n % 2
                        if n >= 4:
                            pe.wait_ge(S["hid_ready"], i * (2 * HC) + n - 3)
                        for c in range(DC):
                            last = nc.tensor.matmul(ps_h[n % 4][:, 0:HALF], w1[:, c, o * P:(o + 1) * P],
                                                    xt[:, c, half * HALF:(half + 1) * HALF], start=c == 0, stop=c == DC - 1)
                        last.then_inc(S["up_made"], 1)
                    pe.wait_ge(S["hid_ready"], (i + 1) * (2 * HC))
                    for j in range(TB):
                        if j >= 2:
                            pe.wait_ge(S["down_added"], i * TB + j - 1)
                        for c in range(HC):
                            last = nc.tensor.matmul(ps_o[j % 2][:, 0:D], hid[:, c, j * P:(j + 1) * P], w2[:, c, :],
                                                    start=c == 0, stop=c == HC - 1)
                        last.then_inc(S["down_made"], 1)


def select_stage(nc, keep, io):
    with Stage(nc, "select") as st:
        bits = st.sb("bits", [P, 34], I32)
        key = st.sb("key", [P, 1], I32)
        cand = st.sb("cand", [P, 1], I32)
        flip = st.sb("flip", [P, 1], I32)
        value = st.sb("value", [P, 1], I32)
        took = st.sb("took", [P, 1], I32)
        count = st.sb("count", [P, 1])
        above = st.sb("above", [P, NT])
        equal = st.sb("equal", [P, NT])
        before = st.sb("before", [P, NT])
        tiles = st.sb("tiles", [P, NT])
        ones_row = st.sb("ones_row", [P, NT])
        scale = st.sb("scale", [P, NT])
        base = st.sb("base", [P, 2, TB, D])
        ps_n = st.banks("ps_n", 1)[0]
        ps_p = st.banks("ps_p", 1)[0]
        S = {n: st.sem(n) for n in ("bits_in chain counted totalled equal_ready prefixes_made base_in scaled stored "
                                    "passed free").split()}
        score, acc = keep["score"], keep["acc"]
        with nc.Block() as block:
            @block.sync
            def _(sp):
                sp.dma_start(bits[:], io["bits"]).then_inc(S["bits_in"], 16)
                with sp.Fori(0, NBLK) as i:
                    sp.dma_start(base[:, 0], block_of(io["base"], i)).then_inc(S["base_in"], 16)
                    sp.wait_ge(S["scaled"], i + 1)
                    sp.dma_start(block_of(io["out"], i), base[:, 0]).then_inc(S["stored"], 16)
                    sp.wait_ge(S["stored"], (i + 1) * 16)
                    sp.sem_inc(S["passed"], 1)

            @block.vector
            def _(dve):
                link = Link(dve, S["chain"])
                valid = keep["valid"]

                def as_float():
                    link(nc.vector.tensor_single_scalar(flip[:], cand[:], 31, ALU.arith_shift_right))
                    link(nc.vector.tensor_tensor(flip[:], flip[:], bits[:, 33:34], ALU.bitwise_xor))
                    link(nc.vector.tensor_tensor(flip[:], flip[:], bits[:, 32:33], ALU.bitwise_or))
                    link(nc.vector.tensor_tensor(value[:], cand[:], flip[:], ALU.bitwise_xor))

                nc.vector.memset(ones_row[:], 1.0)
                link(nc.vector.memset(key[:], 0))
                dve.wait_ge(S["bits_in"], 16)
                with dve.Fori(0, 32) as b:
                    link.loop(b, 8)
                    bit = bits[:, bass.ds(b, 1)]
                    link(nc.vector.tensor_tensor(cand[:], key[:], bit, ALU.bitwise_or))
                    as_float()
                    nc.vector.scalar_tensor_tensor(above[:], score[:], value[:].bitcast(F32)[:, 0:1], valid, ALU.is_ge,
                                                   ALU.mult, accum_out=count[:]).then_inc(S["counted"], 1)
                    dve.wait_ge(S["totalled"], b + 1)
                    link(nc.vector.tensor_scalar(took[:], ps_n[:, 0:1], TOPK_KEEP - 0.5, -1.0, ALU.is_ge, ALU.mult))
                    link(nc.vector.tensor_tensor(took[:], took[:], bit, ALU.bitwise_and))
                    link(nc.vector.tensor_tensor(key[:], key[:], took[:], ALU.bitwise_or))
                link.leave(32)
                link(nc.vector.tensor_tensor(cand[:], key[:], key[:], ALU.bitwise_or))
                as_float()
                threshold = value[:].bitcast(F32)[:, 0:1]
                link(nc.vector.scalar_tensor_tensor(above[:], score[:], threshold, valid, ALU.is_gt, ALU.mult,
                                                    accum_out=count[:]))
                nc.vector.scalar_tensor_tensor(equal[:], score[:], threshold, valid, ALU.is_equal, ALU.mult)\
                    .then_inc(S["equal_ready"], 1)
                dve.wait_ge(S["prefixes_made"], 1)
                nc.vector.tensor_copy(before[:], ps_p[:, 0:NT])
                link(nc.vector.tensor_copy(tiles[:], ps_p[:, 64:64 + NT]))
                nc.vector.tensor_copy(count[:], ps_p[:, 128:129])
                link(nc.vector.tensor_tensor(before[:], before[:], tiles[:], ALU.subtract))
                link(nc.vector.tensor_tensor_scan(tiles[:], ones_row[:], tiles[:], 0.0, ALU.mult, ALU.add))
                link(nc.vector.tensor_tensor(before[:], before[:], tiles[:], ALU.add))
                link(nc.vector.tensor_scalar(before[:], before[:], count[:, 0:1], TOPK_KEEP - 0.5, ALU.add, ALU.is_lt))
                link(nc.vector.tensor_tensor(equal[:], equal[:], before[:], ALU.mult))
                link(nc.vector.tensor_tensor(above[:], above[:], equal[:], ALU.add))
                link(nc.vector.tensor_tensor(scale[:], above[:], score[:], ALU.mult))
                with dve.Fori(0, NBLK) as i:
                    dve.wait_ge(S["base_in"], (i + 1) * 16)
                    for j in range(TB):
                        last = nc.vector.scalar_tensor_tensor(
                            base[:, 0, j, :], acc[:, bass.ds(i * TB + j, 1), 0:D].rearrange("p a d -> p (a d)"),
                            scale[:, bass.ds(i * TB + j, 1)], base[:, 0, j, :], ALU.mult, ALU.add)
                    last.then_inc(S["scaled"], 1)

            @block.tensor
            def _(pe):
                with pe.Fori(0, 32) as b:
                    pe.wait_ge(S["counted"], b + 1)
                    nc.tensor.matmul(ps_n[:, 0:1], col(keep, "ones"), count[:], start=True, stop=True)\
                        .then_inc(S["totalled"], 1)
                pe.wait_ge(S["equal_ready"], 1)
                nc.tensor.matmul(ps_p[:, 0:NT], col(keep, "below"), equal[:], start=True, stop=True)
                nc.tensor.matmul(ps_p[:, 64:64 + NT], col(keep, "ones"), equal[:], start=True, stop=True)
                nc.tensor.matmul(ps_p[:, 128:129], col(keep, "ones"), count[:], start=True, stop=True)\
                    .then_inc(S["prefixes_made"], 1)


def build(nc, io):
    for name, width in (("table0", D + 4), ("table1", D + 8), ("q", D), ("k", D), ("v", D), ("xn", D), ("x2", D),
                        ("base", D)):
        io[name] = nc.dram_tensor(name, (NPAD, width), F32).ap()
    with ExitStack() as stack:
        def sb(name, shape, dt=F32):
            return stack.enter_context(nc.sbuf_tensor(name, shape, dt))
        keep = {
            "const": sb("const", [P, CONST_W]),
            "acc": sb("acc", [P, NTA, D + 8]),
            "left_max": sb("left_max", [P, NTA, 8]),
            "right": sb("right", [P, NTA, 8]),
            "macro_of": sb("macro_of", [P, NSTEP], I32),
            "tile_of": sb("tile_of", [P, NSTEP], I32),
            "node0": sb("node0", [P, NSTEP]),
            "last_step": sb("last_step", [P, NM], I32),
            "kw": sb("kw", [P, DC, D]),
            "k_max": sb("k_max", [P, D]),
            "iota_b": sb("iota_b", [P, P], mybir.dt.bfloat16),
            "score": sb("score", [P, NT]),
        }
        keep["valid"], keep["negpad"] = col(keep, "valid"), col(keep, "negpad")
        schedule_stage(nc, keep, io)
        pre_stage(nc, keep, io, 0)
        edge_stage(nc, keep, io, 0)
        moe_stage(nc, keep, io)
        pre_stage(nc, keep, io, 1)
        edge_stage(nc, keep, io, 1)
        context_stage(nc, keep, io)
        mlp_stage(nc, keep, io)
        select_stage(nc, keep, io)


def _constants():
    import numpy as np
    c = np.zeros((P, CONST_W), np.float32)

    def put(name, a):
        c[:, slice(*CONST[name])] = a
    p = np.arange(P)
    node = np.arange(NT)[None, :] * P + p[:, None]
    put("ident", np.eye(P))
    put("ones", 1.0)
    put("iota", p[None, :])
    put("valid", node < N)
    put("negpad", np.where(node < N, 0.0, -BIG))
    put("blockmask", p[:, None] // 32 == p[None, :] // 32)
    put("steps", np.arange(NSTEP)[None, :])
    put("macros", np.arange(NM)[None, :])
    put("index", node)
    for heads in (4, 8):
        channel = np.arange(DC)[None, :, None] * P + p[:, None, None]
        put(f"head{heads}", (channel // (D // heads) == np.arange(heads)[None, None, :]).reshape(P, -1))
    put("earlier", np.array([f < e for e in range(N_EXP) for f in range(N_EXP)])[None, :])
    put("eps", LN_EPS)
    put("below", p[:, None] < p[None, :])
    return c


def _layout(inputs):
    import numpy as np
    g = {k: np.asarray(a) for k, a in inputs.items()}

    def chunks(w):
        return np.ascontiguousarray(w.reshape(-1, P, w.shape[-1]).transpose(1, 0, 2))

    def each(w):
        return np.ascontiguousarray(w.reshape(w.shape[0], -1, P, w.shape[-1]).transpose(2, 0, 1, 3))

    def down(b):
        return np.ascontiguousarray(np.moveaxis(b.reshape(*b.shape[:-1], -1, P), -1, 0))

    def rep(b):
        return np.ascontiguousarray(np.broadcast_to(b.reshape(1, -1), (P, b.size)))

    x = np.zeros((NPAD, D), np.float32)
    x[:N] = g["x"]
    edges = {}
    for name, fill in (("src", 0), ("dst", 8191)):
        a = np.full(NM * ME, fill, np.int32)
        a[:E] = g[name]
        edges[name] = a
    ends = edges["dst"][ME - 1::ME]
    ends_col = np.full((P, 1), 8191 * 4, np.int32)
    ends_col[:NM, 0] = ends
    bits = np.array([1 << b for b in range(31, -1, -1)] + [1 << 31, 0xFFFFFFFF], np.uint32).view(np.int32)
    out = {
        "const": _constants(), "bits": rep(bits), "x0": x, "ends_row": rep(ends), "ends_col": ends_col,
        "src": np.ascontiguousarray(edges["src"].reshape(-1, P).T), "dst": np.ascontiguousarray(edges["dst"].reshape(-1, P).T),
        "l0_w_gat": chunks(g["L0_gnn_W"]), "l1_w_gat": chunks(g["L1_gnn_W"]),
        "l0_attn": np.stack([down(g["L0_gnn_attn_l"].reshape(-1)), down(g["L0_gnn_attn_r"].reshape(-1))], axis=2),
        "l1_attn": np.stack([down(g["L1_gnn_att_src"].reshape(-1)), down(g["L1_gnn_att_dst"].reshape(-1))], axis=2),
        "l0_gat_bias": rep(g["L0_gnn_bias"]), "l0_w_qkv": chunks(g["L0_mix_W_qkv"]), "l0_b_qkv": rep(g["L0_mix_b_qkv"]),
        "l0_w_out": chunks(g["L0_mix_W_out"]), "l0_b_out": rep(g["L0_mix_b_out"]),
        "r_w1": chunks(g["L0_ffn_router_w1"]), "r_b1": down(g["L0_ffn_router_b1"]),
        "r_w2": g["L0_ffn_router_w2"], "r_b2": rep(g["L0_ffn_router_b2"]),
        "e_w1": each(g["L0_ffn_expert_w1"]), "e_b1": down(g["L0_ffn_expert_b1"]),
        "e_w2": each(g["L0_ffn_expert_w2"]), "e_b2": down(g["L0_ffn_expert_b2"]),
        "e_w3": each(g["L0_ffn_expert_w3"]), "e_b3": g["L0_ffn_expert_b3"],
        "l1_gat_bias": rep(g["L1_gnn_bias"]), "l1_gamma": rep(g["L1_gnn_gamma"]), "l1_beta": rep(g["L1_gnn_beta"]),
        "l1_w_qkv": chunks(g["L1_mix_Wqkv"]), "l1_w_out": chunks(g["L1_mix_Wout"]), "l1_mix_gamma": rep(g["L1_mix_gamma"]),
        "f_wr": rep(g["L1_ffn_wr"]), "f_br": rep(g["L1_ffn_br"]), "f_w1": chunks(g["L1_ffn_w1"]), "f_b1": down(g["L1_ffn_b1"]),
        "f_w2": chunks(g["L1_ffn_w2"]), "f_b2": rep(g["L1_ffn_b2"]),
    }
    return {k: np.ascontiguousarray(a) for k, a in out.items()}


def kernel(**inputs):
    import concourse.bacc as bacc
    from concourse.bass_utils import run_bass_kernel_spmd

    nc = bacc.Bacc("TRN2", target_bir_lowering=False, num_devices=1)
    arrays = {f"in_{name}": a for name, a in _layout(inputs).items()}
    io = {name[3:]: nc.dram_tensor(name, a.shape, mybir.dt.from_np(a.dtype), kind="ExternalInput").ap()
          for name, a in arrays.items()}
    io["out"] = nc.dram_tensor("out", (NPAD, D), F32, kind="ExternalOutput").ap()
    build(nc, io)
    result = run_bass_kernel_spmd(nc, [arrays], core_ids=[0])
    return result.results[0]["out"][:N]
```

```python
from contextlib import ExitStack

import concourse.bass as bass
from concourse import mybir

F32 = mybir.dt.float32
I32 = mybir.dt.int32
ALU = mybir.AluOpType
ACT = mybir.ActivationFunctionType
AX = mybir.AxisListType

P = 128
N = 6250
D = 256
DC = D // P
NT = -(-N // P)
TB = 7
NBLK = NT // TB
NPAD = NT * P
HALF = TB * P // 2
assert N < 2 ** 15
E = 206250
G = 16
ME = G * P
NM = -(-E // ME)
NSTEP = NM + NT
NSTEP += NSTEP % 2
NTA = NT + 1
BIG = 2.0 ** 100
NEG_SLOPE = 0.2
LN_EPS = 1e-5
N_EXP = 6
TOPK_KEEP = 3124

assert NT == TB * NBLK and HALF <= 512 and NM % 2 == 1

CONST = {}
_at = 0
for _name, _width in (("ident", P), ("ones", P), ("iota", P), ("valid", NT), ("negpad", NT),
                      ("blockmask", P), ("steps", NSTEP), ("macros", NM), ("below", P), ("index", NT),
                      ("head4", DC * 4), ("head8", DC * 8), ("earlier", 36), ("eps", 1)):
    CONST[_name] = (_at, _at + _width)
    _at += _width
CONST_W = _at


class Link:

    def __init__(self, eng, sem):
        self.eng, self.sem, self.before, self.n, self.i, self.per = eng, sem, 0, 0, None, 0

    def loop(self, i, per):
        self.before, self.n, self.i, self.per = self.before + self.n, 0, i, per

    def leave(self, rounds):
        assert self.n == self.per, f"the loop's body has {self.n} links"
        self.before, self.n, self.i = self.before + rounds * self.per, 0, None

    def mark(self, ins):
        ins.then_inc(self.sem, 1)
        self.n += 1

    def settle(self):
        value = self.before + self.n
        self.eng.wait_ge(self.sem, value if self.i is None else self.i * self.per + value)

    def __call__(self, ins):
        self.mark(ins)
        self.settle()


class Stage:

    def __init__(self, nc, name):
        self.nc, self.name, self.stack, self.sems = nc, name, ExitStack(), []

    def __enter__(self):
        return self

    def sb(self, name, shape, dt=F32):
        return self.stack.enter_context(self.nc.sbuf_tensor(f"{self.name}_{name}", shape, dt))

    def banks(self, name, n):
        return [self.stack.enter_context(self.nc.psum_tensor(f"{self.name}_{name}{i}", [P, 512], F32))
                for i in range(n)]

    def sem(self, name):
        self.sems.append(self.nc.alloc_semaphore(f"{self.name}_{name}"))
        return self.sems[-1]

    def __exit__(self, *exc):
        if exc[0] is None:
            self.nc.clear_and_free_semaphores(self.sems)
            self.nc.all_engine_barrier()
            self.stack.close()
        return False


def col(keep, name):
    a, b = CONST[name]
    return keep["const"][:, a:b]


def blocks(dram):
    return dram.rearrange("(b j p) c -> b p j c", p=P, j=TB)


def cast(ap, n):
    return ap.unsqueeze(2).to_broadcast([ap.shape[0], ap.shape[1], n])


def block_of(dram, i):
    return blocks(dram)[bass.ds(i, 1), :, :, :].rearrange("b p j c -> p (b j) c")


def row_moments(nc, link, x, stats, mv, passed):
    for j in range(TB):
        last = nc.vector.bn_stats(stats[:, j, :], x[:, j, :])
    link(last)
    nc.vector.sem_inc(passed, 1)
    for j in range(TB):
        last = nc.vector.bn_aggr(mv[:, j, :], stats[:, j, :])
    return last


def schedule_stage(nc, keep, io):
    with Stage(nc, "sched") as st:
        ends_row = st.sb("ends_row", [P, NM], I32)
        ends_col = st.sb("ends_col", [P, 1], I32)
        tile_row = st.sb("tile_row", [P, NM], I32)
        tile_col = st.sb("tile_col", [P, 1], I32)
        key_row = st.sb("key_row", [P, NM])
        key_col = st.sb("key_col", [P, 1])
        after = st.sb("after", [P, NSTEP])
        psum = st.banks("macro", 1)[0]
        loaded, chain, compared, summed = (st.sem(n) for n in ("loaded", "chain", "compared", "summed"))
        with nc.Block() as block:
            @block.sync
            def _(sp):
                sp.dma_start(keep["const"][:], io["const"]).then_inc(loaded, 16)
                sp.dma_start(ends_row[:], io["ends_row"]).then_inc(loaded, 16)
                sp.dma_start(ends_col[:], io["ends_col"]).then_inc(loaded, 16)
                sp.wait_ge(loaded, 48)

            @block.vector
            def _(dve):
                link = Link(dve, chain)
                link(nc.vector.memset(keep["right"][:], 0.0))
                dve.wait_ge(loaded, 48)
                nc.vector.tensor_copy(keep["iota_b"][:], cast(col(keep, "iota"), G))
                nc.vector.tensor_single_scalar(tile_row[:], ends_row[:], 7, ALU.logical_shift_right)
                link(nc.vector.tensor_single_scalar(tile_col[:], ends_col[:], 7, ALU.logical_shift_right))
                nc.vector.tensor_tensor(key_row[:], tile_row[:], col(keep, "macros"), ALU.add)
                link(nc.vector.tensor_tensor(key_col[:], tile_col[:], col(keep, "index")[:, 0:1], ALU.add))
                nc.vector.tensor_copy(keep["last_step"][:], key_row[:])
                nc.vector.tensor_scalar(after[:], col(keep, "steps"), key_col[:, 0:1], None,
                                        ALU.is_gt).then_inc(compared, 1)
                dve.wait_ge(summed, 1)
                nc.vector.tensor_copy(keep["macro_of"][:], psum[:, 0:NSTEP])
                link(nc.vector.tensor_tensor(keep["node0"][:], col(keep, "steps"), psum[:, 0:NSTEP], ALU.subtract))
                nc.vector.tensor_scalar(keep["node0"][:], keep["node0"][:], float(P), None, ALU.mult)
                macros = [keep["macro_of"][:, n:NSTEP - 3 + n:2] for n in range(4)]
                packed = keep["packed"]
                link(nc.vector.tensor_single_scalar(packed[:], macros[3], 8, ALU.logical_shift_left))
                for n in (2, 1, 0):
                    link(nc.vector.tensor_tensor(packed[:], packed[:], macros[n], ALU.bitwise_or))
                    if n:
                        link(nc.vector.tensor_single_scalar(packed[:], packed[:], 8, ALU.logical_shift_left))

            @block.tensor
            def _(pe):
                pe.wait_ge(compared, 1)
                nc.tensor.matmul(psum[:, 0:NSTEP], col(keep, "ones"), after[:], start=True, stop=True)\
                    .then_inc(summed, 1)


def pre_stage(nc, keep, io, layer):
    H = 4 if layer == 0 else 8
    ROW = D + H
    L = f"l{layer}_"
    first = layer == 0
    src, table = io["x0" if first else "x2"], io[f"table{layer}"]
    with Stage(nc, f"pre{layer}") as st:
        x = st.sb("x", [P, TB, D])
        xn = st.sb("xn", [P, TB, D])
        stats = st.sb("stats", [P, TB, 6])
        mv = st.sb("mv", [P, TB, 2])
        std = st.sb("std", [P, TB])
        rstd = st.sb("rstd", [P, TB])
        w_gat = st.sb("w_gat", [P, DC, D + 2 * H])
        w_gat_t = st.sb("w_gat_t", [P, DC, D])
        attn = st.sb("attn", [P, DC, 2])
        attn_heads = st.sb("attn_heads", [P, DC, 2, H])
        w_qkv = st.sb("w_qkv", [P, DC, 3 * D])
        xt = st.sb("xt", [P, 2, DC, P])
        row = st.sb("row", [P, TB, ROW])
        q = st.sb("q", [P, TB, D])
        k = st.sb("k", [P, TB, D])
        v = st.sb("v", [P, TB, D])
        rights = st.sb("rights", [P, TB, H])
        if first:
            mean = st.sb("mean", [P, DC, 2])
            bias = st.sb("bias", [P, 3 * D])
            bias_mean = st.sb("bias_mean", [P, 2])
            q2 = st.sb("q2", [P, TB, D])
            k2 = st.sb("k2", [P, TB, D])
            junk = st.sb("junk", [P, D])
            k_square = st.sb("k_square", [P, TB, D])
            sums = st.sb("sums", [P, 3, TB])
            q_root = st.sb("q_root", [P, TB])
            scale = st.sb("scale", [P, 2, TB])
            zeros = st.sb("zeros", [P, 512])
            kv_t = st.sb("kv_t", [P, DC, D])
            w_out = st.sb("w_out", [P, DC, D])
            col_norm = st.sb("col_norm", [P, DC])
            norm_root = st.sb("norm_root", [P, DC])
        else:
            q_max = st.sb("q_max", [P, TB, H])
            q_sum = st.sb("q_sum", [P, TB, H])
            block_max = st.sb("block_max", [P, D])
            run_max = st.sb("run_max", [P, D])
            col_max = st.sb("col_max", [P, DC])
            diag = st.sb("diag", [P, DC, P])
        ps_xt = st.banks("ps_xt", 2)
        ps_qk = st.banks("ps_qk", 2)
        ps_gv = st.banks("ps_gv", 1)[0]
        ps_lr = st.banks("ps_lr", 1)[0]
        ps_kv = st.banks("ps_kv", 1)[0]
        ps_norm = st.banks("ps_norm", 1)[0]
        S = {n: st.sem(n) for n in (
            "weights_in x_in passed passed_sp chain act_chain moments_ready std_ready xn_ready xt_made xt_copied projected row_ready "
            "qkv_ready squares_ready q_root_ready stored out_free q_ready k_ready k_square_ready kv_done "
            "w_t_made w_t_copied heads_ready wa_made weights_ready kv_copied kw_made norm_root_ready zeros_ready "
            "q_shifted q_exp max_ready max_t_made diag_ready max_row_made v_ready").split()}
        n_weights = 6 if first else 4
        ident = col(keep, "ident")
        eps = col(keep, "eps")
        with nc.Block() as block:
            @block.sync
            def _(sp):
                sp.dma_start(w_gat_t[:], io[L + "w_gat"]).then_inc(S["weights_in"], 16)
                sp.dma_start(attn[:], io[L + "attn"]).then_inc(S["weights_in"], 16)
                sp.dma_start(w_gat[:, :, 0:D], io[L + "w_gat"]).then_inc(S["weights_in"], 16)
                sp.dma_start(w_qkv[:], io[L + "w_qkv"]).then_inc(S["weights_in"], 16)
                if first:
                    sp.dma_start(bias[:], io["l0_b_qkv"]).then_inc(S["weights_in"], 16)
                    sp.dma_start(w_out[:], io["l0_w_out"]).then_inc(S["weights_in"], 16)
                sp.sem_inc(S["out_free"], 1)
                sp.dma_start(x[:], block_of(src, 0)).then_inc(S["x_in"], 16)

                def move(i, more):
                    if more:
                        sp.wait_ge(S["xn_ready"], (i + 1) * TB)
                        sp.sem_inc(S["passed_sp"], 1)
                        sp.dma_start(x[:], block_of(src, i + 1)).then_inc(S["x_in"], 16)
                    sp.wait_ge(S["row_ready"], (i + 1) * TB)
                    sp.sem_inc(S["passed_sp"], 1)
                    sp.dma_start(block_of(table, i), row[:]).then_inc(S["stored"], 16)
                    if first:
                        sp.wait_ge(S["v_ready"], i + 1)
                    sp.dma_start(block_of(io["v"], i), v[:]).then_inc(S["stored"], 16)
                    sp.wait_ge(S["q_ready"], i + 1)
                    sp.dma_start(block_of(io["q"], i), (q2 if first else q)[:]).then_inc(S["stored"], 16)
                    if first:
                        sp.dma_start(block_of(io["xn"], i), xn[:]).then_inc(S["stored"], 16)
                    else:
                        sp.dma_start(block_of(io["k"], i), k[:]).then_inc(S["stored"], 16)
                    sp.wait_ge(S["stored"], (i + 1) * 64)
                    sp.sem_inc(S["out_free"], 1)

                with sp.Fori(0, NBLK - 1) as i:
                    move(i, True)
                move(NBLK - 1, False)

            @block.vector
            def _(dve):
                link = Link(dve, S["chain"])
                dve.wait_ge(S["weights_in"], 16 * n_weights)
                heads = col(keep, f"head{H}").rearrange("p (k h) -> p k h", k=DC)
                for side in range(2):
                    last = nc.vector.tensor_tensor(attn_heads[:, :, side, :], heads, cast(attn[:, :, side], H), ALU.mult)
                last.then_inc(S["heads_ready"], 1)
                if first:
                    for a in range(2):
                        nc.vector.tensor_reduce(mean[:, :, a], w_qkv[:, :, a * D:(a + 1) * D], AX.X, ALU.add)
                        last = nc.vector.tensor_reduce(bias_mean[:, a:a + 1], bias[:, a * D:(a + 1) * D], AX.X, ALU.add)
                    link(last)
                    nc.vector.tensor_scalar(mean[:], mean[:], 1.0 / D, None, ALU.mult)
                    link(nc.vector.tensor_scalar(bias_mean[:], bias_mean[:], 1.0 / D, None, ALU.mult))
                    for a in range(2):
                        nc.vector.tensor_tensor(w_qkv[:, :, a * D:(a + 1) * D], w_qkv[:, :, a * D:(a + 1) * D],
                                                cast(mean[:, :, a], D), ALU.subtract)
                        nc.vector.tensor_scalar(bias[:, a * D:(a + 1) * D], bias[:, a * D:(a + 1) * D],
                                                bias_mean[:, a:a + 1], None, ALU.subtract)
                    nc.vector.memset(zeros[:], 0.0).then_inc(S["zeros_ready"], 1)
                else:
                    nc.vector.memset(run_max[:], -BIG).then_inc(S["zeros_ready"], 1)
                dve.wait_ge(S["zeros_ready"], 1)
                dve.wait_ge(S["wa_made"], 1)
                nc.vector.tensor_copy(w_gat[:, :, D:D + 2 * H],
                                      ps_lr[:, 0:DC * 2 * H].rearrange("p (k h) -> p k h", k=DC))\
                    .then_inc(S["weights_ready"], 1)
                with dve.Fori(0, NBLK) as i:
                    link.loop(i, 7)
                    dve.wait_ge(S["x_in"], (i + 1) * 16)
                    row_moments(nc, link, x, stats, mv, S["passed"]).then_inc(S["moments_ready"], 1)
                    dve.wait_ge(S["std_ready"], i + 1)
                    link(nc.vector.reciprocal(rstd[:], std[:]))
                    dve.wait_ge(S["out_free"], i + 1)
                    for j in range(TB):
                        nc.vector.tensor_scalar(xn[:, j, :], x[:, j, :], mv[:, j, 0:1], rstd[:, j:j + 1],
                                                ALU.subtract, ALU.mult).then_inc(S["xn_ready"], 1)
                    for j in range(TB):
                        t1 = i * TB + j + 1
                        dve.wait_ge(S["projected"], t1)
                        if first:
                            nc.vector.tensor_tensor(q[:, j, :], ps_qk[j % 2][:, 0:D], bias[:, 0:D], ALU.add)
                            nc.vector.tensor_tensor(k[:, j, :], ps_qk[j % 2][:, D:2 * D], bias[:, D:2 * D],
                                                    ALU.add).then_inc(S["qkv_ready"], 1)
                        else:
                            nc.vector.tensor_scalar(k[:, j, :], ps_qk[j % 2][:, D:2 * D],
                                                    keep["negpad"][:, bass.ds(i * TB + j, 1)], None, ALU.add)
                            nc.vector.tensor_copy(q[:, j, :], ps_qk[j % 2][:, 0:D]).then_inc(S["qkv_ready"], 1)
                    dve.wait_ge(S["qkv_ready"], (i + 1) * TB)
                    dve.wait_ge(S["row_ready"], (i + 1) * TB)
                    nc.vector.tensor_scalar(keep["right"][:, bass.ds(i * TB, TB), 0:H], rights[:], 1.0, None, ALU.mult)
                    if first:
                        nc.vector.tensor_tensor(v[:], v[:], bias[:, 2 * D:3 * D].unsqueeze(1).to_broadcast([P, TB, D]),
                                                ALU.add).then_inc(S["v_ready"], 1)
                    else:
                        here = bass.ds(i * TB, TB)
                        nc.vector.tensor_scalar(keep["acc"][:, here, 0:D], row[:, :, 0:D], 1.0, None, ALU.mult)
                        nc.vector.tensor_scalar(keep["acc"][:, here, D:ROW], row[:, :, D:ROW], 0.0, 1.0, ALU.mult, ALU.add)
                        nc.vector.tensor_scalar(keep["left_max"][:, here, 0:H], row[:, :, D:ROW], 1.0, None, ALU.mult)
                    if first:
                        dve.wait_ge(S["squares_ready"], i + 1)
                        dve.wait_ge(S["q_root_ready"], i + 1)
                        link(nc.vector.tensor_scalar(sums[:, 0:2, :], sums[:, 0:2, :], 1e-7, None, ALU.add))
                        link(nc.vector.reciprocal(scale[:], sums[:, 0:2, :]))
                        nc.vector.tensor_tensor(scale[:, 1, :], scale[:, 1, :], keep["valid"][:, bass.ds(i * TB, TB)],
                                                ALU.mult)
                        link(nc.vector.tensor_tensor(q_root[:], q_root[:], scale[:, 0, :], ALU.mult))
                        link(nc.vector.tensor_scalar(q_root[:], q_root[:], 1e-12, None, ALU.max))
                        link(nc.vector.reciprocal(q_root[:], q_root[:]))
                        nc.vector.tensor_tensor(k2[:], k2[:], cast(scale[:, 1, :], D), ALU.mult).then_inc(S["k_ready"], 1)
                        dve.wait_ge(S["k_ready"], i + 1)
                        for j in range(TB):
                            last = nc.vector.tensor_scalar(q2[:, j, :], q2[:, j, :], scale[:, 0, j:j + 1],
                                                           q_root[:, j:j + 1], ALU.mult, ALU.mult)
                        last.then_inc(S["q_ready"], 1)
                    else:
                        qh = q[:].rearrange("p j (h d) -> p (j h) d", h=H)
                        m, s = (a[:].rearrange("p j h -> p (j h)") for a in (q_max, q_sum))
                        link(nc.vector.tensor_reduce(m, qh, AX.X, ALU.max))
                        nc.vector.tensor_tensor(qh, qh, cast(m, D // H), ALU.subtract).then_inc(S["q_shifted"], 1)
                        link(nc.vector.tensor_reduce(block_max[:], k[:].rearrange("p j c -> p c j"), AX.X, ALU.max))
                        link(nc.vector.tensor_tensor(run_max[:], run_max[:], block_max[:], ALU.max))
                        dve.wait_ge(S["q_exp"], i + 1)
                        link(nc.vector.tensor_reduce(s, qh, AX.X, ALU.add))
                        link(nc.vector.reciprocal(s, s))
                        nc.vector.tensor_tensor(qh, qh, cast(s, D // H), ALU.mult).then_inc(S["q_ready"], 1)
                link.leave(NBLK)
                if first:
                    dve.wait_ge(S["kv_done"], 1)
                    nc.vector.tensor_copy(kv_t[:].rearrange("p k c -> p (k c)"), ps_kv[:]).then_inc(S["kv_copied"], 1)
                    dve.wait_ge(S["norm_root_ready"], 1)
                    link(nc.vector.tensor_scalar(norm_root[:], norm_root[:], 1e-12, float(N) ** 0.5, ALU.max, ALU.mult))
                    link(nc.vector.reciprocal(col_norm[:], norm_root[:]))
                    dve.wait_ge(S["kw_made"], 1)
                    for c in range(DC):
                        last = nc.vector.tensor_scalar(keep["kw"][:, c, :], ps_qk[0][:, c * D:(c + 1) * D],
                                                       col_norm[:, c:c + 1], None, ALU.mult)
                    link(last)
                else:
                    nc.vector.tensor_copy(block_max[:], run_max[:]).then_inc(S["max_ready"], 1)
                    dve.wait_ge(S["max_t_made"], 1)
                    link(nc.vector.tensor_reduce(col_max[:], ps_kv[:, 0:D].rearrange("p (k n) -> p k n", k=DC), AX.X, ALU.max))
                    for c in range(DC):
                        last = nc.vector.tensor_scalar(diag[:, c, :], ident, col_max[:, c:c + 1], None, ALU.mult)
                    last.then_inc(S["diag_ready"], 1)
                    dve.wait_ge(S["max_row_made"], 1)
                    link(nc.vector.tensor_copy(keep["k_max"][:], ps_norm[:, 0:D]))

            @block.scalar
            def _(act):
                act.wait_ge(S["w_t_made"], 1)
                nc.scalar.activation(w_gat_t[:].rearrange("p k n -> p (k n)"), ps_kv[:], ACT.Copy).then_inc(S["w_t_copied"], 1)
                with act.Fori(0, NBLK) as i:
                    act.wait_ge(S["moments_ready"], i + 1)
                    nc.scalar.activation(std[:], mv[:, :, 1], ACT.Sqrt, bias=eps).then_inc(S["std_ready"], 1)
                    for j in range(TB):
                        t1 = i * TB + j + 1
                        act.wait_ge(S["xt_made"], t1)
                        nc.scalar.activation(xt[:, j % 2].rearrange("p k n -> p (k n)"), ps_xt[j % 2][:, 0:D], ACT.Copy)\
                            .then_inc(S["xt_copied"], 1)
                        act.wait_ge(S["projected"], t1)
                        nc.scalar.activation(v[:, j, :], ps_gv[:, D:2 * D], ACT.Copy)
                        nc.scalar.activation(row[:, j, 0:D], ps_gv[:, 0:D], ACT.Copy)
                        nc.scalar.activation(rights[:, j, :], ps_lr[:, H:2 * H], ACT.Copy)
                        nc.scalar.activation(row[:, j, D:ROW], ps_lr[:, 0:H], ACT.Copy).then_inc(S["row_ready"], 1)
                        if first:
                            act.wait_ge(S["qkv_ready"], t1)
                            nc.scalar.activation(k2[:, j, :], k[:, j, :], ACT.Square, accum_out=sums[:, 1, j:j + 1])
                            nc.scalar.activation(q2[:, j, :], q[:, j, :], ACT.Square,
                                                 accum_out=sums[:, 0, j:j + 1]).then_inc(S["act_chain"], 1)
                            act.wait_ge(S["act_chain"], t1)
                            last = nc.scalar.activation(junk[:], q2[:, j, :], ACT.Square, accum_out=sums[:, 2, j:j + 1])
                    if first:
                        last.then_inc(S["squares_ready"], 1)
                        act.wait_ge(S["squares_ready"], i + 1)
                        nc.scalar.activation(q_root[:], sums[:, 2, :], ACT.Sqrt).then_inc(S["q_root_ready"], 1)
                        act.wait_ge(S["k_ready"], i + 1)
                        nc.scalar.activation(k_square[:], k2[:], ACT.Square).then_inc(S["k_square_ready"], 1)
                    else:
                        act.wait_ge(S["q_shifted"], i + 1)
                        nc.scalar.activation(q[:], q[:], ACT.Exp).then_inc(S["q_exp"], 1)
                if first:
                    act.wait_ge(S["kv_done"], 1)
                    nc.scalar.activation(norm_root[:], ps_norm[:, 0:DC], ACT.Sqrt).then_inc(S["norm_root_ready"], 1)

            @block.tensor
            def _(pe):
                pe.wait_ge(S["weights_in"], 16 * n_weights)
                for k_ in range(DC):
                    for n_ in range(DC):
                        last = nc.tensor.transpose(ps_kv[:, n_ * D + k_ * P:n_ * D + (k_ + 1) * P],
                                                   w_gat[:, k_, n_ * P:(n_ + 1) * P], ident)
                last.then_inc(S["w_t_made"], 1)
                pe.wait_ge(S["w_t_copied"], 1)
                pe.wait_ge(S["heads_ready"], 1)
                for k_ in range(DC):
                    for n_ in range(DC):
                        last = nc.tensor.matmul(ps_lr[:, k_ * 2 * H:(k_ + 1) * 2 * H],
                                                w_gat_t[:, n_, k_ * P:(k_ + 1) * P],
                                                attn_heads[:, n_].rearrange("p a h -> p (a h)"),
                                                start=n_ == 0, stop=n_ == DC - 1)
                last.then_inc(S["wa_made"], 1)
                pe.wait_ge(S["weights_ready"], 1)
                if first:
                    nc.tensor.matmul(ps_kv[:], zeros[:, 0:P], zeros[:], start=True, stop=False, skip_group_check=True)
                    nc.tensor.matmul(ps_norm[:, 0:DC], zeros[:, 0:P], zeros[:, 0:DC], start=True, stop=False,
                                     skip_group_check=True)

                def transposes(i, j):
                    pe.wait_ge(S["xn_ready"], i * TB + j + 1)
                    for c in range(DC):
                        last = nc.tensor.transpose(ps_xt[j % 2][:, c * P:(c + 1) * P], xn[:, j, c * P:(c + 1) * P], ident)
                    last.then_inc(S["xt_made"], 1)

                with pe.Fori(0, NBLK) as i:
                    transposes(i, 0)
                    for j in range(TB):
                        if j + 1 < TB:
                            transposes(i, j + 1)
                        pe.wait_ge(S["xt_copied"], i * TB + j + 1)
                        if j >= 2:
                            pe.wait_ge(S["qkv_ready"], i * TB + j - 1)
                        for c in range(DC):
                            a, o = xt[:, j % 2, c], dict(start=c == 0, stop=c == DC - 1)
                            nc.tensor.matmul(ps_qk[j % 2][:], a, w_qkv[:, c, 0:2 * D], **o)
                        if j:
                            pe.wait_ge(S["row_ready"], i * TB + j)
                        for c in range(DC):
                            a, o = xt[:, j % 2, c], dict(start=c == 0, stop=c == DC - 1)
                            nc.tensor.matmul(ps_gv[:, 0:D], a, w_gat[:, c, 0:D], **o)
                        for c in range(DC):
                            a, o = xt[:, j % 2, c], dict(start=c == 0, stop=c == DC - 1)
                            nc.tensor.matmul(ps_gv[:, D:2 * D], a, w_qkv[:, c, 2 * D:3 * D], **o)
                        for c in range(DC):
                            a, o = xt[:, j % 2, c], dict(start=c == 0, stop=c == DC - 1)
                            last = nc.tensor.matmul(ps_lr[:, 0:2 * H], a, w_gat[:, c, D:D + 2 * H], **o)
                        last.then_inc(S["projected"], 1)
                    if first:
                        pe.wait_ge(S["k_ready"], i + 1)
                        for j in range(TB):
                            for c in range(DC):
                                nc.tensor.matmul(ps_kv[:, c * D:(c + 1) * D], v[:, j, c * P:(c + 1) * P], k2[:, j, :],
                                                 start=False, stop=False, skip_group_check=True)
                        pe.wait_ge(S["k_square_ready"], i + 1)
                        for j in range(TB):
                            for c in range(DC):
                                last = nc.tensor.matmul(ps_norm[:, c:c + 1], k_square[:, j, c * P:(c + 1) * P],
                                                        col(keep, "ones")[:, 0:1], start=False, stop=False,
                                                        skip_group_check=True)
                if first:
                    nc.tensor.matmul(ps_norm[:, 0:DC], zeros[:, 0:P], zeros[:, 0:DC], start=False, stop=True,
                                     skip_group_check=True)
                    nc.tensor.matmul(ps_kv[:], zeros[:, 0:P], zeros[:], start=False, stop=True,
                                     skip_group_check=True).then_inc(S["kv_done"], 1)
                    pe.wait_ge(S["kv_copied"], 1)
                    for c in range(DC):
                        for d in range(DC):
                            last = nc.tensor.matmul(ps_qk[0][:, c * D:(c + 1) * D], kv_t[:, d, c * P:(c + 1) * P],
                                                    w_out[:, d, :], start=d == 0, stop=d == DC - 1)
                    last.then_inc(S["kw_made"], 1)
                else:
                    pe.wait_ge(S["max_ready"], 1)
                    for c in range(DC):
                        last = nc.tensor.transpose(ps_kv[:, c * P:(c + 1) * P], block_max[:, c * P:(c + 1) * P], ident)
                    last.then_inc(S["max_t_made"], 1)
                    pe.wait_ge(S["diag_ready"], 1)
                    for c in range(DC):
                        last = nc.tensor.matmul(ps_norm[:, c * P:(c + 1) * P], col(keep, "ones"), diag[:, c],
                                                start=True, stop=True)
                    last.then_inc(S["max_row_made"], 1)


def head(a):
    a = a[:].bitcast(mybir.dt.bfloat16)
    return a[(slice(None),) * (len(a.shape) - 1) + (slice(1, None, 2),)]


def edge_stage(nc, keep, io, layer):
    H = 4 if layer == 0 else 8
    ROW = D + H
    GH = G * H
    BF16 = mybir.dt.bfloat16
    NROWS = 4
    table = io[f"table{layer}"]
    acc, left_max, right = keep["acc"], keep["left_max"], keep["right"]
    with Stage(nc, f"edge{layer}") as st:
        dst = st.sb("dst", [P, NM * G])
        srcs = st.sb("srcs", [P, NM * G], mybir.dt.int16)
        index = st.sb("index", [P, NROWS, G], I32)
        rows = st.sb("rows", [P, NROWS, G * ROW])
        local = st.sb("local", [P, G], BF16)
        onehot = st.sb("onehot", [P, 2, G, P])
        onehot_b = st.sb("onehot_b", [P, P, G], BF16)
        onehot_t = st.sb("onehot_t", [P, G, P], BF16)
        flat = st.sb("flat", [P, 2, G, H])
        dst_t = st.sb("dst_t", [P, P])
        drop = st.sb("drop", [P, P + 1])
        reset = st.sb("reset", [P, P + 1])
        running = st.sb("running", [P, P])
        at_last = st.sb("at_last", [P, P])
        values = st.sb("values", [P, G, 4, H])
        bigs = st.sb("bigs", [P, GH], BF16)
        new_max = st.sb("new_max", [P, H])
        z = st.sb("z", [P, 2, H])
        shifts = st.sb("shifts", [P, 2, H])
        node_side = st.sb("node_side", [P, 3, 2, H])
        fade = st.sb("fade", [P, H])
        logit = st.sb("logit", [P, G, H])
        weighted = st.sb("weighted", [P, 2, G, ROW])
        ident_b = st.sb("ident_b", [P, P], BF16)
        ps_t = st.banks("ps_t", 1)[0]
        ps_o = [st.stack.enter_context(nc.psum_tensor(f"{st.name}_ps_o{n}", [P, 1024], BF16)) for n in range(2)]
        ps_b = ps_t[:, 2 * P:4 * P]
        ps_m = st.banks("ps_m", 1)[0]
        ps_e = st.banks("ps_e", 1)[0]
        ps_acc = st.banks("ps_acc", 2)
        S = {n: st.sem(n) for n in (
            "edges_in srcs_ready passed chain prepared index_ready gather0 gather1 gather2 gather3 macro_ready onehot_b_ready onehot_ready flat_ready "
            "ident_ready t_made dst_t_ready at_last_ready back_made values_copied values_ready onehot_t_made onehot_t_copied locals_made "
            "node_side_ready fade_ready expanded logit_ready exp_ready rows_weighted summed").split()}
        ident = col(keep, "ident")
        gather = [S[f"gather{n}"] for n in range(NROWS)]
        dst_int, src_int = (weighted[:].rearrange("p a g r -> p (a g r)")[:, a * NM * G:(a + 1) * NM * G].bitcast(I32)
                            for a in range(2))
        with nc.Block() as block:
            @block.sync
            def _(sp):
                sp.dma_start(src_int, io["src"]).then_inc(S["edges_in"], 16)
                sp.dma_start(dst_int, io["dst"]).then_inc(S["edges_in"], 16)
                sp.wait_ge(S["edges_in"], 32)

            @block.gpsimd
            def _(pool):
                pool.wait_ge(S["srcs_ready"], 1)

                def issue(m, buf, release, landed):
                    if release:
                        last = pool.value_load(keep["last_step"][0:1, bass.ds(m - NROWS, 1)], min_val=0, max_val=NSTEP)
                        pool.wait_ge(S["rows_weighted"], last * 4 + 4)
                        pool.sem_inc(S["passed"], 1)
                    nc.gpsimd.tensor_copy(index[:, buf, :], srcs[:, bass.ds(m * G, G)]).then_inc(S["index_ready"], 1)
                    pool.wait_ge(S["index_ready"], m + 1)
                    pool.sem_inc(S["passed"], 1)
                    for c in range(G):
                        pool.indirect_dma_start(
                            out=rows[:, buf, c * ROW:(c + 1) * ROW], out_offset=None, in_=table,
                            in_offset=bass.IndirectOffsetOnAxis(ap=index[:, buf, c:c + 1], axis=0)
                        ).then_inc(gather[buf], 16)
                        if c == 2 and landed is not None:
                            confirm(*landed)

                def confirm(turn, buf):
                    pool.wait_ge(gather[buf], (turn + 1) * (16 * G))
                    pool.sem_inc(S["macro_ready"], 1)

                for m in range(NROWS):
                    issue(m, m, False, (0, m - 1) if m else None)
                with pool.Fori(1, NM // NROWS) as i:
                    for buf in range(NROWS):
                        issue(i * NROWS + buf, buf, True, (i, buf - 1) if buf else (i - 1, NROWS - 1))
                for m in range(NM // NROWS * NROWS, NM):
                    issue(m, m % NROWS, True, ((m - 1) // NROWS, (m - 1) % NROWS))
                confirm((NM - 1) // NROWS, (NM - 1) % NROWS)

            @block.vector
            def _(dve):
                link = Link(dve, S["chain"])
                one = lambda a: a.rearrange("p a h -> p (a h)")

                def macros(i):
                    word = dve.value_load(keep["packed"][0:1, bass.ds(i, 1)], min_val=0, max_val=2 ** 31 - 1)
                    return [nc.s_assert_within((word >> (8 * n)) & 255, 0, NM - 1, skip_runtime_bounds_check_because=
                                               "a macro's number was packed there") for n in range(4)]

                def got(m):
                    return rows[:, bass.ds(m % NROWS, 1), :].rearrange("p a (g r) -> p (a g) r", r=ROW)

                def tile(s, m):
                    return nc.s_assert_within(s - m, 0, NTA - 1, skip_runtime_bounds_check_because=
                                              "a step's macro is the number of macros whose last step is before it")

                def sums_of(s, m):
                    return one(acc[:, bass.ds(tile(s, m), 1), :])

                def spread(s, m, again=True):
                    node0 = keep["node0"][:, bass.ds(s, 1)]
                    link.mark(nc.vector.tensor_scalar(local[:], dst[:, bass.ds(m * G, G)], node0, None, ALU.subtract))
                    nc.vector.tensor_scalar(flat[:, 1], cast(dst[:, bass.ds(m * G, G)], H), node0, None, ALU.subtract)
                    dve.wait_ge(S["macro_ready"], m + 1)
                    nc.vector.tensor_scalar(flat[:, 0], got(m)[:, :, D:ROW], 1.0, None, ALU.mult).then_inc(S["flat_ready"], 1)
                    if again:
                        dve.wait_ge(S["onehot_ready"], s)
                    link.settle()
                    nc.vector.tensor_tensor(onehot_b[:], keep["iota_b"][:], local[:].unsqueeze(1).to_broadcast([P, P, G]),
                                            ALU.is_equal).then_inc(S["onehot_b_ready"], 1)

                def local_maxima(s):
                    dve.wait_ge(S["dst_t_ready"], s + 1)
                    link(nc.vector.tensor_tensor(drop[0:GH, 1:P], dst_t[0:GH, 0:P - 1], dst_t[0:GH, 1:P], ALU.subtract))
                    nc.vector.tensor_scalar(reset[0:GH], drop[0:GH], -BIG, None, ALU.max)
                    link(nc.vector.tensor_tensor_scan(running[0:GH], drop[0:GH, 0:P], ps_t[0:GH, 0:P], -BIG, ALU.add, ALU.max))
                    nc.vector.scalar_tensor_tensor(at_last[0:GH], reset[0:GH, 1:P + 1], 1.0 / BIG, running[0:GH], ALU.mult,
                                                   ALU.mult).then_inc(S["at_last_ready"], 1)

                def split_values(s):
                    dve.wait_ge(S["values_copied"], s + 1)
                    link(nc.vector.tensor_tensor(values[:, :, 2], values[:, :, 1], head(values)[:, :, 1], ALU.subtract))
                    nc.vector.tensor_tensor(values[:, :, 3], values[:, :, 2], head(values)[:, :, 2], ALU.subtract)\
                        .then_inc(S["values_ready"], 1)

                def maxima(s, m):
                    t = tile(s, m)
                    er, old_max = one(right[:, bass.ds(t, 1), 0:H]), one(left_max[:, bass.ds(t, 1), 0:H])
                    dve.wait_ge(S["locals_made"], s + 1)
                    link.mark(nc.vector.tensor_reduce(new_max[:], ps_m[:, 0:GH].rearrange("p (g h) -> p h g", g=G),
                                                        AX.X, ALU.min))
                    nc.vector.tensor_tensor(z[:, 0], old_max, er, ALU.add)
                    nc.vector.tensor_scalar(node_side[:, 0, 0], er, 1.0, None, ALU.mult)
                    link.settle()
                    link(nc.vector.scalar_tensor_tensor(old_max, new_max[:], -1.0, old_max, ALU.mult, ALU.max))
                    link(nc.vector.tensor_tensor(z[:, 1], old_max, er, ALU.add))
                    nc.vector.scalar_tensor_tensor(shifts[:], z[:], NEG_SLOPE, z[:], ALU.mult, ALU.max)
                    link(nc.vector.scalar_tensor_tensor(node_side[:, 0, 1], z[:, 1], NEG_SLOPE, z[:, 1], ALU.mult, ALU.max))
                    nc.vector.tensor_tensor(fade[:], shifts[:, 0], shifts[:, 1], ALU.subtract).then_inc(S["prepared"], 1)
                    link(nc.vector.tensor_tensor(node_side[:, 1], node_side[:, 0], head(node_side)[:, 0], ALU.subtract))
                    nc.vector.tensor_tensor(node_side[:, 2], node_side[:, 1], head(node_side)[:, 1], ALU.subtract)\
                        .then_inc(S["node_side_ready"], 1)

                def logits(s):
                    dve.wait_ge(S["expanded"], s + 1)
                    node = ps_e[:, 0:2 * GH].rearrange("p (g a h) -> p g a h", g=G, a=2)
                    link(nc.vector.tensor_tensor(logit[:], node[:, :, 0, :], flat[:, 0], ALU.add))
                    link(nc.vector.scalar_tensor_tensor(logit[:], logit[:], NEG_SLOPE, logit[:], ALU.mult, ALU.max))
                    link(nc.vector.tensor_tensor(logit[:], logit[:], node[:, :, 1, :], ALU.subtract))
                    nc.vector.tensor_scalar(logit[:], logit[:], 0.0, None, ALU.min).then_inc(S["logit_ready"], 1)

                def let_fade(s, m):
                    mine = sums_of(s, m)
                    dve.wait_ge(S["fade_ready"], s + 1)
                    nc.vector.tensor_tensor(mine[:, 0:D].rearrange("p (h d) -> p h d", h=H),
                                            mine[:, 0:D].rearrange("p (h d) -> p h d", h=H), cast(fade[:], D // H), ALU.mult)
                    link(nc.vector.tensor_tensor(mine[:, D:ROW], mine[:, D:ROW], fade[:], ALU.mult))

                def weigh(s, m, par, part):
                    a, b = part * G // 4, (part + 1) * G // 4
                    if part == 0:
                        dve.wait_ge(S["exp_ready"], s + 1)
                        dve.sem_inc(S["passed"], 1)
                    nc.vector.tensor_tensor(weighted[:, par, a:b, 0:D].rearrange("p g (h d) -> p g h d", h=H),
                                            got(m)[:, a:b, 0:D].rearrange("p g (h d) -> p g h d", h=H),
                                            weighted[:, par, a:b, D:ROW].unsqueeze(3).to_broadcast([P, G // 4, H, D // H]),
                                            ALU.mult).then_inc(S["rows_weighted"], 1)

                def add(s, m, par):
                    mine = sums_of(s, m)
                    dve.wait_ge(S["summed"], s + 1)
                    link(nc.vector.tensor_tensor(mine[:, 0:ROW], mine[:, 0:ROW], ps_acc[par][:, 0:ROW], ALU.add))

                def round_of(s, par, before, now, after):
                    spread(s + 1, after)
                    weigh(s, now, par, 0)
                    local_maxima(s + 1)
                    weigh(s, now, par, 1)
                    split_values(s + 1)
                    weigh(s, now, par, 2)
                    if before is not None:
                        add(s - 1, before, 1 - par)
                    let_fade(s, now)
                    maxima(s + 1, after)
                    weigh(s, now, par, 3)
                    logits(s + 1)

                dve.wait_ge(S["edges_in"], 32)
                nc.vector.tensor_copy(srcs[:], src_int).then_inc(S["srcs_ready"], 1)
                nc.vector.tensor_copy(dst[:], dst_int)
                first_tile = 0 if layer == 0 else NT
                nc.vector.memset(acc[:, first_tile:NTA, :], 0.0)
                nc.vector.memset(left_max[:, first_tile:NTA, :], -BIG)
                nc.vector.memset(bigs[:], BIG)
                nc.vector.tensor_copy(ident_b[:], ident).then_inc(S["ident_ready"], 1)
                link(nc.vector.memset(drop[:], -BIG))
                dve.sem_inc(S["passed"], 1)
                m0, m1, *_ = macros(0)
                spread(0, m0, False)
                local_maxima(0)
                split_values(0)
                maxima(0, m0)
                logits(0)
                round_of(0, 0, None, m0, m1)
                with dve.Fori(0, (NSTEP - 2) // 2) as i:
                    link.loop(i, 28)
                    m0, m1, m2, m3 = macros(i)
                    round_of(i * 2 + 1, 1, m0, m1, m2)
                    round_of(i * 2 + 2, 0, m1, m2, m3)
                link.leave((NSTEP - 2) // 2)
                *_, m0, m1 = macros((NSTEP - 2) // 2 - 1)
                add(NSTEP - 2, m0, 0)
                for part in range(4):
                    weigh(NSTEP - 1, m1, 1, part)
                let_fade(NSTEP - 1, m1)
                add(NSTEP - 1, m1, 1)

            @block.scalar
            def _(act):
                def front(s, par, again):
                    def transposed(k):
                        act.wait_ge(S["onehot_t_made"], s * 2 + k + 1)
                        nc.scalar.activation(onehot_t[:, 8 * k:8 * k + 8, :].rearrange("p g n -> p (g n)"), ps_o[k][:],
                                             ACT.Copy).then_inc(S["onehot_t_copied"], 1)

                    act.wait_ge(S["t_made"], s + 1)
                    nc.scalar.activation(dst_t[0:GH], ps_t[0:GH, P:2 * P], ACT.Copy, scale=BIG).then_inc(S["dst_t_ready"], 1)
                    transposed(0)
                    act.wait_ge(S["back_made"], s + 1)
                    nc.scalar.activation(values[:, :, 0:2].rearrange("p g a h -> p a g h"),
                                         ps_b[:, 0:2 * GH].rearrange("p (a g h) -> p a g h", a=2, g=G),
                                         ACT.Copy).then_inc(S["values_copied"], 1)
                    transposed(1)
                    if again:
                        act.wait_ge(S["summed"], s - 1)
                    act.wait_ge(S["onehot_b_ready"], s + 1)
                    nc.scalar.activation(onehot[:, par], onehot_b[:].rearrange("p n g -> p g n"), ACT.Copy)\
                        .then_inc(S["onehot_ready"], 1)
                    act.wait_ge(S["prepared"], s + 1)
                    nc.scalar.activation(fade[:], fade[:], ACT.Exp).then_inc(S["fade_ready"], 1)
                    act.wait_ge(S["logit_ready"], s + 1)
                    nc.scalar.activation(weighted[:, par, :, D:ROW], logit[:], ACT.Exp).then_inc(S["exp_ready"], 1)

                front(0, 0, False)
                front(1, 1, False)
                with act.Fori(1, NSTEP // 2) as i:
                    for par in range(2):
                        front(i * 2 + par, par, True)

            @block.tensor
            def _(pe):
                def transposes(s, between=lambda half: None):
                    pe.wait_ge(S["flat_ready"], s + 1)
                    pe.sem_inc(S["passed"], 1)
                    for a in range(2):
                        last = nc.tensor.transpose(ps_t[0:GH, a * P:(a + 1) * P],
                                                   flat[:, a].rearrange("p g h -> p (g h)"), ident)
                    last.then_inc(S["t_made"], 1)
                    between(0)
                    pe.wait_ge(S["onehot_b_ready"], s + 1)
                    for k in range(2):
                        for c in range(8):
                            last = nc.tensor.transpose(ps_o[k][:, c * P:(c + 1) * P], onehot_b[:, :, 8 * k + c], ident_b[:])
                        last.then_inc(S["onehot_t_made"], 1)
                    between(1)

                def back(s):
                    pe.wait_ge(S["at_last_ready"], s + 1)
                    pe.sem_inc(S["passed"], 1)
                    nc.tensor.transpose(ps_b[:, 0:GH], reset[0:GH, 1:P + 1], ident[0:GH, 0:GH])
                    nc.tensor.transpose(ps_b[:, GH:2 * GH], at_last[0:GH], ident[0:GH, 0:GH])\
                        .then_inc(S["back_made"], 1)

                def locals_of(s):
                    pe.wait_ge(S["values_ready"], s + 1)
                    nc.tensor.matmul(ps_m[:, 0:GH], ident_b[:], bigs[:], start=True, stop=False, skip_group_check=True)
                    for c in range(G):
                        for k in range(4):
                            last = nc.tensor.matmul(ps_m[:, c * H:(c + 1) * H], onehot_b[:, :, c], head(values)[:, c, k],
                                                    start=False, stop=k == 3, skip_group_check=True)
                    last.then_inc(S["locals_made"], 1)

                def expand(s):
                    pe.wait_ge(S["node_side_ready"], s + 1)
                    pe.wait_ge(S["onehot_t_copied"], (s + 1) * 2)
                    for c in range(G):
                        for k in range(3):
                            last = nc.tensor.matmul(ps_e[:, c * 2 * H:(c + 1) * 2 * H], onehot_t[:, c, :],
                                                    head(node_side)[:, k].rearrange("p a h -> p (a h)"),
                                                    start=k == 0, stop=k == 2)
                    last.then_inc(S["expanded"], 1)

                def sum_up(s, par, chunks):
                    if 0 in chunks:
                        pe.wait_ge(S["onehot_ready"], s + 1)
                    for c in chunks:
                        if c % (G // 4) == 0:
                            pe.wait_ge(S["rows_weighted"], s * 4 + c // (G // 4) + 1)
                        last = nc.tensor.matmul(ps_acc[par][:, 0:ROW], onehot[:, par, c, :], weighted[:, par, c, :],
                                                start=c == 0, stop=c == G - 1)
                    if c == G - 1:
                        last.then_inc(S["summed"], 1)

                def both(front, s, par, started):
                    def rest(half):
                        if started:
                            sum_up(s - 1, 1 - par, range(12 + 2 * half, 14 + 2 * half))
                    transposes(front, rest)
                    back(front)
                    sum_up(s, par, range(0, 4))
                    locals_of(front)
                    sum_up(s, par, range(4, 8))
                    expand(front)
                    sum_up(s, par, range(8, 12))

                pe.wait_ge(S["ident_ready"], 1)
                transposes(0)
                back(0)
                locals_of(0)
                expand(0)
                both(1, 0, 0, False)
                with pe.Fori(0, (NSTEP - 2) // 2) as i:
                    for par in (1, 0):
                        s = i * 2 + (2 - par)
                        both(s + 1, s, par, True)
                sum_up(NSTEP - 2, 0, range(12, G))
                sum_up(NSTEP - 1, 1, range(G))


def moe_stage(nc, keep, io):
    H, ROW = 4, D + 4
    acc = keep["acc"]
    with Stage(nc, "moe") as st:
        x_in = st.sb("x_in", [P, TB, D])
        xn_in = st.sb("xn_in", [P, TB, D])
        x = st.sb("x", [P, TB, D])
        xn = st.sb("xn", [P, TB, D])
        v = st.sb("v", [P, TB, D])
        q2 = st.sb("q2", [P, TB, D])
        elu = st.sb("elu", [P, TB, D])
        stats = st.sb("stats", [P, TB, 6])
        mv = st.sb("mv", [P, TB, 2])
        std = st.sb("std", [P, TB])
        rstd = st.sb("rstd", [P, TB])
        den = st.sb("den", [P, TB, H])
        vq_t = st.sb("vq_t", [P, 2 * DC, P])
        w_out = st.sb("w_out", [P, DC, D])
        b_out = st.sb("b_out", [P, D])
        gat_bias = st.sb("gat_bias", [P, D])
        r_w1 = st.sb("r_w1", [P, DC, P])
        r_b1 = st.sb("r_b1", [P, 1])
        r_w2 = st.sb("r_w2", [P, N_EXP])
        r_b2 = st.sb("r_b2", [P, N_EXP])
        w1 = st.sb("w1", [P, N_EXP, DC, D])
        b1 = st.sb("b1", [P, N_EXP, DC])
        w2 = st.sb("w2", [P, N_EXP, DC, D])
        b2 = st.sb("b2", [P, N_EXP, DC])
        w3 = st.sb("w3", [P, N_EXP, DC, D])
        b3 = st.sb("b3", [N_EXP, D])
        xt = st.sb("xt", [P, DC, TB * P])
        h1 = st.sb("h1", [P, DC, TB * P])
        h2 = st.sb("h2", [P, DC, TB * P])
        rh = h1
        prob = st.sb("prob", [P, TB, N_EXP])
        e_max = st.sb("e_max", [P, TB])
        e_sum = st.sb("e_sum", [P, TB])
        rank = st.sb("rank", [P, TB, N_EXP])
        greater = st.sb("greater", [P, TB, 36])
        equal = st.sb("equal", [P, TB, 36])
        gate = st.sb("gate", [P, TB, N_EXP])
        gate_t = st.sb("gate_t", [N_EXP, TB * P])
        ps_a = st.banks("ps_a", 2)
        ps_h = st.banks("ps_h", 4)
        ps_o = st.banks("ps_o", 2)
        S = {n: st.sem(n) for n in (
            "weights_in inputs_in passed passed_sp x_free chain elu_ready vq_made vq_copied mixed mix_added moments_ready std_ready "
            "xn_ready xt_made xt_copied rh_made rh_ready logits_made gates_shifted probs_exp top_shifted top_exp gate_ready "
            "gate_t_made gate_t_copied up1_made h1_ready up2_made h2_ready down_made down_added stored "
            "neg_ready").split()}
        ident, eps = col(keep, "ident"), col(keep, "eps")
        W = [(w_out, "l0_w_out"), (b_out, "l0_b_out"), (gat_bias, "l0_gat_bias"), (r_w1, "r_w1"), (r_b1, "r_b1"),
             (r_w2, "r_w2"), (r_b2, "r_b2"), (w1, "e_w1"), (b1, "e_b1"), (w2, "e_w2"), (b2, "e_b2"), (w3, "e_w3"),
             (b3, "e_b3")]
        with nc.Block() as block:
            @block.sync
            def _(sp):
                for tile, name in W:
                    sp.dma_start(tile[:], io[name]).then_inc(S["weights_in"], 16)
                def load(i):
                    for tile, name in ((x_in, "x0"), (xn_in, "xn"), (v, "v"), (q2, "q")):
                        sp.dma_start(tile[:], block_of(io[name], i)).then_inc(S["inputs_in"], 16)

                def move(i, more):
                    if more:
                        sp.wait_ge(S["neg_ready"], i + 1)
                        sp.sem_inc(S["passed_sp"], 1)
                        sp.wait_ge(S["vq_made"], (i + 1) * TB)
                        sp.sem_inc(S["passed_sp"], 1)
                        load(i + 1)
                    sp.wait_ge(S["down_added"], (i + 1) * (TB * (N_EXP + 1)))
                    sp.sem_inc(S["passed_sp"], 1)
                    sp.dma_start(block_of(io["x2"], i), x[:]).then_inc(S["stored"], 16)
                    sp.wait_ge(S["stored"], (i + 1) * 16)
                    sp.sem_inc(S["x_free"], 1)

                load(0)
                sp.sem_inc(S["x_free"], 1)
                with sp.Fori(0, NBLK - 1) as i:
                    move(i, True)
                move(NBLK - 1, False)
                sp.wait_ge(S["weights_in"], 16 * len(W))

            @block.vector
            def _(dve):
                link = Link(dve, S["chain"])
                dve.wait_ge(S["weights_in"], 16 * len(W))
                with dve.Fori(0, NBLK) as i:
                    link.loop(i, 23)
                    mine = acc[:, bass.ds(i * TB, TB), :]
                    link(nc.vector.tensor_scalar(den[:], mine[:, :, D:ROW], 1e-30, None, ALU.max))
                    link(nc.vector.reciprocal(den[:], den[:]))
                    for h in range(H):
                        last = nc.vector.tensor_tensor(elu[:, :, h * 64:(h + 1) * 64], mine[:, :, h * 64:(h + 1) * 64],
                                                       cast(den[:, :, h], 64), ALU.mult)
                    link(last)
                    link(nc.vector.tensor_tensor(elu[:], elu[:], gat_bias[:].unsqueeze(1).to_broadcast([P, TB, D]), ALU.add))
                    dve.wait_ge(S["inputs_in"], (i + 1) * 64)
                    dve.wait_ge(S["x_free"], i + 1)
                    dve.sem_inc(S["passed"], 1)
                    link(nc.vector.tensor_tensor(x[:], x_in[:], xn_in[:], ALU.add))
                    link(nc.vector.scalar_tensor_tensor(x[:], elu[:], 0.0, x[:], ALU.max, ALU.add))
                    nc.vector.tensor_scalar(elu[:], elu[:], 0.0, None, ALU.min).then_inc(S["neg_ready"], 1)
                    link(nc.vector.tensor_tensor(x[:], x[:], b_out[:].unsqueeze(1).to_broadcast([P, TB, D]), ALU.add))
                    dve.wait_ge(S["elu_ready"], i + 1)
                    link(nc.vector.scalar_tensor_tensor(x[:], elu[:], -1.0, x[:], ALU.add, ALU.add))
                    for j in range(TB):
                        dve.wait_ge(S["mixed"], i * TB + j + 1)
                        nc.vector.tensor_tensor(x[:, j, :], x[:, j, :], ps_o[j % 2][:, 0:D], ALU.add)\
                            .then_inc(S["mix_added"], 1)
                    dve.wait_ge(S["mix_added"], (i + 1) * TB)
                    row_moments(nc, link, x, stats, mv, S["passed"]).then_inc(S["moments_ready"], 1)
                    dve.wait_ge(S["std_ready"], i + 1)
                    link(nc.vector.reciprocal(rstd[:], std[:]))
                    for j in range(TB):
                        nc.vector.tensor_scalar(xn[:, j, :], x[:, j, :], mv[:, j, 0:1], rstd[:, j:j + 1],
                                                ALU.subtract, ALU.mult).then_inc(S["xn_ready"], 1)
                    dve.wait_ge(S["logits_made"], i + 1)
                    link(nc.vector.tensor_tensor(prob[:], ps_o[1][:, 0:TB * N_EXP].rearrange("p (j e) -> p j e", j=TB),
                                                 r_b2[:].unsqueeze(1).to_broadcast([P, TB, N_EXP]), ALU.add))
                    link(nc.vector.tensor_reduce(e_max[:], prob[:], AX.X, ALU.max))
                    nc.vector.tensor_tensor(prob[:], prob[:], cast(e_max[:], N_EXP), ALU.subtract)\
                        .then_inc(S["gates_shifted"], 1)
                    dve.wait_ge(S["probs_exp"], i + 1)
                    link(nc.vector.tensor_reduce(e_sum[:], prob[:], AX.X, ALU.add))
                    link(nc.vector.reciprocal(e_sum[:], e_sum[:]))
                    link(nc.vector.tensor_tensor(prob[:], prob[:], cast(e_sum[:], N_EXP), ALU.mult))
                    of = prob[:].unsqueeze(3).to_broadcast([P, TB, N_EXP, N_EXP])
                    other = prob[:].unsqueeze(2).to_broadcast([P, TB, N_EXP, N_EXP])
                    g4, e4 = (a[:].rearrange("p j (e f) -> p j e f", e=N_EXP) for a in (greater, equal))
                    nc.vector.tensor_tensor(g4, of, other, ALU.is_lt)
                    link(nc.vector.tensor_tensor(e4, of, other, ALU.is_equal))
                    link(nc.vector.tensor_tensor(equal[:], equal[:], col(keep, "earlier").unsqueeze(1)
                                                 .to_broadcast([P, TB, 36]), ALU.mult))
                    link(nc.vector.tensor_tensor(greater[:], greater[:], equal[:], ALU.add))
                    link(nc.vector.tensor_reduce(rank[:], g4, AX.X, ALU.add))
                    nc.vector.tensor_scalar(rank[:], rank[:], 1.5, None, ALU.is_lt)
                    link(nc.vector.tensor_reduce(e_max[:], prob[:], AX.X, ALU.max))
                    nc.vector.tensor_tensor(prob[:], prob[:], cast(e_max[:], N_EXP), ALU.subtract)\
                        .then_inc(S["top_shifted"], 1)
                    dve.wait_ge(S["top_exp"], i + 1)
                    link(nc.vector.tensor_tensor(gate[:], prob[:], rank[:], ALU.mult))
                    link(nc.vector.tensor_reduce(e_sum[:], gate[:], AX.X, ALU.add))
                    link(nc.vector.reciprocal(e_sum[:], e_sum[:]))
                    nc.vector.tensor_tensor(gate[:], gate[:], cast(e_sum[:], N_EXP), ALU.mult).then_inc(S["gate_ready"], 1)
                    dve.wait_ge(S["gate_ready"], i + 1)
                    for e in range(-1, N_EXP):
                        for j in range(TB):
                            n = (e + 1) * TB + j
                            dve.wait_ge(S["down_made"], i * (TB * (N_EXP + 1)) + n + 1)
                            if e >= 0:
                                nc.vector.scalar_tensor_tensor(x[:, j, :], ps_o[n % 2][:, 0:D], gate[:, j, e:e + 1], x[:, j, :],
                                                               ALU.mult, ALU.add).then_inc(S["down_added"], 1)
                            else:
                                nc.vector.tensor_tensor(x[:, j, :], x[:, j, :], ps_o[n % 2][:, 0:D], ALU.add)\
                                    .then_inc(S["down_added"], 1)
                        dve.wait_ge(S["down_added"], i * (TB * (N_EXP + 1)) + (e + 2) * TB)
                link.leave(NBLK)

            @block.scalar
            def _(act):
                act.wait_ge(S["weights_in"], 16 * len(W))
                with act.Fori(0, NBLK) as i:
                    for j in range(TB):
                        act.wait_ge(S["vq_made"], i * TB + j + 1)
                        nc.scalar.activation(vq_t[:].rearrange("p k n -> p (k n)"), ps_a[j % 2][:], ACT.Copy)\
                            .then_inc(S["vq_copied"], 1)
                        if j == 0:
                            act.wait_ge(S["neg_ready"], i + 1)
                            nc.scalar.activation(elu[:], elu[:], ACT.Exp).then_inc(S["elu_ready"], 1)
                    act.wait_ge(S["moments_ready"], i + 1)
                    nc.scalar.activation(std[:], mv[:, :, 1], ACT.Sqrt, bias=eps).then_inc(S["std_ready"], 1)
                    for j in range(TB):
                        act.wait_ge(S["xt_made"], i * TB + j + 1)
                        nc.scalar.activation(xt[:, :, j * P:(j + 1) * P],
                                             ps_a[j % 2][:, 0:D].rearrange("p (k n) -> p k n", k=DC), ACT.Copy)\
                            .then_inc(S["xt_copied"], 1)
                    for half in range(2):
                        act.wait_ge(S["rh_made"], i * 2 + half + 1)
                        nc.scalar.activation(rh[:, 0, half * HALF:(half + 1) * HALF], ps_h[half][:, 0:HALF], ACT.Relu,
                                             bias=r_b1[:, 0:1]).then_inc(S["rh_ready"], 1)
                    act.wait_ge(S["gates_shifted"], i + 1)
                    nc.scalar.activation(prob[:], prob[:], ACT.Exp).then_inc(S["probs_exp"], 1)
                    act.wait_ge(S["top_shifted"], i + 1)
                    nc.scalar.activation(prob[:], prob[:], ACT.Exp).then_inc(S["top_exp"], 1)
                    act.wait_ge(S["gate_t_made"], i + 1)
                    nc.scalar.activation(gate_t[:, 0:4 * P], ps_a[0][0:N_EXP, :], ACT.Copy)
                    nc.scalar.activation(gate_t[:, 4 * P:TB * P], ps_a[1][0:N_EXP, 0:(TB - 4) * P], ACT.Copy)\
                        .then_inc(S["gate_t_copied"], 1)
                    for e in range(N_EXP):
                        for which, (out, b, made, ready) in enumerate(((h1, b1, "up1_made", "h1_ready"),
                                                                       (h2, b2, "up2_made", "h2_ready"))):
                            for n in range(4):
                                o, half = n // 2, n % 2
                                act.wait_ge(S[made], i * (4 * N_EXP) + e * 4 + n + 1)
                                nc.scalar.activation(out[:, o, half * HALF:(half + 1) * HALF], ps_h[n][:, 0:HALF],
                                                     ACT.Relu, bias=b[:, e, o:o + 1]).then_inc(S[ready], 1)

            @block.tensor
            def _(pe):
                pe.wait_ge(S["weights_in"], 16 * len(W))
                with pe.Fori(0, NBLK) as i:
                    pe.wait_ge(S["inputs_in"], (i + 1) * 64)
                    for j in range(TB):
                        if j >= 2:
                            pe.wait_ge(S["vq_copied"], i * TB + j - 1)
                        for c in range(DC):
                            nc.tensor.transpose(ps_a[j % 2][:, c * P:(c + 1) * P], v[:, j, c * P:(c + 1) * P], ident)
                        for c in range(DC):
                            last = nc.tensor.transpose(ps_a[j % 2][:, (DC + c) * P:(DC + c + 1) * P],
                                                       q2[:, j, c * P:(c + 1) * P], ident)
                        last.then_inc(S["vq_made"], 1)
                        pe.wait_ge(S["vq_copied"], i * TB + j + 1)
                        if j >= 2:
                            pe.wait_ge(S["mix_added"], i * TB + j - 1)
                        for c in range(2 * DC):
                            w = (w_out if c < DC else keep["kw"])[:, c % DC, :]
                            last = nc.tensor.matmul(ps_o[j % 2][:, 0:D], vq_t[:, c], w, start=c == 0, stop=c == 2 * DC - 1)
                        last.then_inc(S["mixed"], 1)
                    for j in range(TB):
                        pe.wait_ge(S["xn_ready"], i * TB + j + 1)
                        if j >= 2:
                            pe.wait_ge(S["xt_copied"], i * TB + j - 1)
                        for c in range(DC):
                            last = nc.tensor.transpose(ps_a[j % 2][:, c * P:(c + 1) * P], xn[:, j, c * P:(c + 1) * P], ident)
                        last.then_inc(S["xt_made"], 1)
                    pe.wait_ge(S["xt_copied"], (i + 1) * TB)
                    for half in range(2):
                        for c in range(DC):
                            last = nc.tensor.matmul(ps_h[half][:, 0:HALF], r_w1[:, c, :],
                                                    xt[:, c, half * HALF:(half + 1) * HALF], start=c == 0, stop=c == DC - 1)
                        last.then_inc(S["rh_made"], 1)
                    pe.wait_ge(S["rh_ready"], (i + 1) * 2)
                    for j in range(TB):
                        last = nc.tensor.matmul(ps_o[1][:, j * N_EXP:(j + 1) * N_EXP], rh[:, 0, j * P:(j + 1) * P],
                                                r_w2[:], start=True, stop=True)
                    last.then_inc(S["logits_made"], 1)

                    def up(e, src, w, ready, made, before):
                        for n in range(4):
                            o, half = n // 2, n % 2
                            if before is not None:
                                pe.wait_ge(S[before[0]], before[1] + n + 1)
                            if ready is not None and n == 0:
                                pe.wait_ge(S[ready], i * (4 * N_EXP) + e * 4 + 4)
                            for c in range(DC):
                                last = nc.tensor.matmul(ps_h[n][:, 0:HALF], w[:, e, c, o * P:(o + 1) * P],
                                                        src[:, c, half * HALF:(half + 1) * HALF],
                                                        start=c == 0, stop=c == DC - 1)
                            last.then_inc(S[made], 1)

                    def down(n, lhs_rhs):
                        if n >= 2:
                            pe.wait_ge(S["down_added"], i * (TB * (N_EXP + 1)) + n - 1)
                        for c, (a, b) in enumerate(lhs_rhs):
                            last = nc.tensor.matmul(ps_o[n % 2][:, 0:D], a, b, start=c == 0, stop=c == len(lhs_rhs) - 1)
                        last.then_inc(S["down_made"], 1)

                    up(0, xt, w1, None, "up1_made", None)
                    pe.wait_ge(S["gate_ready"], i + 1)
                    for j in range(TB):
                        last = nc.tensor.transpose(ps_a[j // 4][0:N_EXP, (j % 4) * P:(j % 4 + 1) * P], gate[:, j, :], ident)
                    last.then_inc(S["gate_t_made"], 1)
                    pe.wait_ge(S["gate_t_copied"], i + 1)
                    for j in range(TB):
                        down(j, [(gate_t[:, j * P:(j + 1) * P], b3[:])])
                    for e in range(N_EXP):
                        at = i * (4 * N_EXP) + e * 4
                        if e:
                            up(e, xt, w1, None, "up1_made", ("h2_ready", at - 4))
                        up(e, h1, w2, "h1_ready", "up2_made", ("h1_ready", at))
                        pe.wait_ge(S["h2_ready"], at + 4)
                        for j in range(TB):
                            down((e + 1) * TB + j, [(h2[:, c, j * P:(j + 1) * P], w3[:, e, c, :]) for c in range(DC)])
                    pe.wait_ge(S["down_added"], (i + 1) * (TB * (N_EXP + 1)))
                    pe.sem_inc(S["passed"], 1)


def context_stage(nc, keep, io):
    with Stage(nc, "context") as st:
        k = st.sb("k", [P, TB, D])
        v = st.sb("v", [P, TB, D])
        expk = st.sb("expk", [P, TB, D])
        zeros = st.sb("zeros", [P, D])
        w_out = st.sb("w_out", [P, DC, D])
        context_t = st.sb("context_t", [P, DC, P])
        inv = st.sb("inv", [P, DC])
        ps_c = st.banks("ps_c", 1)[0]
        ps_s = st.banks("ps_s", 1)[0]
        ps_w = st.banks("ps_w", 1)[0]
        S = {n: st.sem(n) for n in ("weights_in k_in v_in chain zeros_ready shifted exp_ready used done "
                                    "context_ready product_made passed").split()}
        with nc.Block() as block:
            @block.sync
            def _(sp):
                sp.dma_start(w_out[:], io["l1_w_out"]).then_inc(S["weights_in"], 16)
                with sp.Fori(0, NBLK) as i:
                    sp.wait_ge(S["used"], i + 1)
                    sp.dma_start(k[:], block_of(io["k"], i)).then_inc(S["k_in"], 16)
                    sp.dma_start(v[:], block_of(io["v"], i)).then_inc(S["v_in"], 16)
                sp.wait_ge(S["weights_in"], 16)

            @block.vector
            def _(dve):
                link = Link(dve, S["chain"])
                nc.vector.memset(zeros[:], 0.0).then_inc(S["zeros_ready"], 1)
                with dve.Fori(0, NBLK) as i:
                    dve.wait_ge(S["k_in"], (i + 1) * 16)
                    nc.vector.tensor_tensor(expk[:], k[:], keep["k_max"][:].unsqueeze(1).to_broadcast([P, TB, D]),
                                            ALU.subtract).then_inc(S["shifted"], 1)
                    dve.wait_ge(S["used"], i + 2)
                    dve.sem_inc(S["passed"], 1)
                dve.wait_ge(S["done"], 1)
                for c in range(DC):
                    last = nc.vector.tensor_tensor(context_t[:, c], ps_c[:, c * P:(c + 1) * P], col(keep, "blockmask"), ALU.mult)
                last.then_inc(S["context_ready"], 1)
                link(nc.vector.reciprocal(inv[:], ps_s[:, 0:DC]))
                link(nc.vector.tensor_scalar(inv[:], inv[:], float(32) ** -0.5, None, ALU.mult))
                dve.wait_ge(S["product_made"], 1)
                for c in range(DC):
                    last = nc.vector.tensor_scalar(keep["kw"][:, c, :], ps_w[:, c * D:(c + 1) * D], inv[:, c:c + 1], None,
                                                   ALU.mult)
                link(last)

            @block.scalar
            def _(act):
                with act.Fori(0, NBLK) as i:
                    act.wait_ge(S["shifted"], i + 1)
                    nc.scalar.activation(expk[:], expk[:], ACT.Exp).then_inc(S["exp_ready"], 1)

            @block.tensor
            def _(pe):
                pe.wait_ge(S["zeros_ready"], 1)
                nc.tensor.matmul(ps_c[:, 0:D], zeros[:, 0:P], zeros[:], start=True, stop=False, skip_group_check=True)
                nc.tensor.matmul(ps_s[:, 0:DC], zeros[:, 0:P], zeros[:, 0:DC], start=True, stop=False, skip_group_check=True)
                pe.sem_inc(S["used"], 1)
                with pe.Fori(0, NBLK) as i:
                    pe.wait_ge(S["exp_ready"], i + 1)
                    pe.wait_ge(S["v_in"], (i + 1) * 16)
                    for j in range(TB):
                        for c in range(DC):
                            nc.tensor.matmul(ps_c[:, c * P:(c + 1) * P], v[:, j, c * P:(c + 1) * P],
                                             expk[:, j, c * P:(c + 1) * P], start=False, stop=False, skip_group_check=True)
                            last = nc.tensor.matmul(ps_s[:, c:c + 1], expk[:, j, c * P:(c + 1) * P],
                                                    col(keep, "ones")[:, 0:1], start=False, stop=False, skip_group_check=True)
                    last.then_inc(S["used"], 1)
                nc.tensor.matmul(ps_s[:, 0:DC], zeros[:, 0:P], zeros[:, 0:DC], start=False, stop=True, skip_group_check=True)
                nc.tensor.matmul(ps_c[:, 0:D], zeros[:, 0:P], zeros[:], start=False, stop=True, skip_group_check=True)\
                    .then_inc(S["done"], 1)
                pe.wait_ge(S["weights_in"], 16)
                pe.wait_ge(S["context_ready"], 1)
                for c in range(DC):
                    last = nc.tensor.matmul(ps_w[:, c * D:(c + 1) * D], context_t[:, c], w_out[:, c, :], start=True, stop=True)
                last.then_inc(S["product_made"], 1)


def mlp_stage(nc, keep, io):
    H, ROW = 8, D + 8
    HID = 4 * D
    HC = HID // P
    acc = keep["acc"]
    with Stage(nc, "mlp") as st:
        x = st.sb("x", [P, TB, D])
        q = st.sb("q", [P, TB, D])
        gat = st.sb("gat", [P, TB, D])
        mix = st.sb("mix", [P, TB, D])
        xn = st.sb("xn", [P, TB, D])
        stats = st.sb("stats", [P, TB, 6])
        mv = st.sb("mv", [P, 3, TB, 2])
        std = st.sb("std", [P, 3, TB])
        rstd = st.sb("rstd", [P, 3, TB])
        den = st.sb("den", [P, TB, H])
        q_t = st.sb("q_t", [P, 2, D])
        gat_bias = st.sb("gat_bias", [P, D])
        gamma = st.sb("gamma", [P, D])
        beta = st.sb("beta", [P, D])
        mix_gamma = st.sb("mix_gamma", [P, D])
        wr = st.sb("wr", [P, D])
        br = st.sb("br", [P, 1])
        w1 = st.sb("w1", [P, DC, HID])
        b1 = st.sb("b1", [P, HC])
        w2 = st.sb("w2", [P, HC, D])
        b2 = st.sb("b2", [P, D])
        xt = st.sb("xt", [P, DC, TB * P])
        hid = st.sb("hid", [P, HC, TB * P])
        weight = st.sb("weight", [P, TB])
        ps_a = st.banks("ps_a", 2)
        ps_h = st.banks("ps_h", 4)
        ps_o = st.banks("ps_o", 2)
        S = {n: st.sem(n) for n in (
            "weights_in x_in q_in passed passed_sp chain q_t_made q_t_copied mixed mix_copied moments_ready std_ready "
            "xn_ready xt_made xt_copied up_made hid_ready down_made down_added base_ready stored").split()}
        ident, eps = col(keep, "ident"), col(keep, "eps")
        W = [(gat_bias, "l1_gat_bias"), (gamma, "l1_gamma"), (beta, "l1_beta"), (mix_gamma, "l1_mix_gamma"),
             (wr, "f_wr"), (br, "f_br"), (w1, "f_w1"), (b1, "f_b1"), (w2, "f_w2"), (b2, "f_b2")]
        rows = lambda a: a[:].unsqueeze(1).to_broadcast([P, TB, D])
        with nc.Block() as block:
            @block.sync
            def _(sp):
                for tile, name in W:
                    sp.dma_start(tile[:], io[name]).then_inc(S["weights_in"], 16)
                def move(i, more):
                    sp.dma_start(x[:], block_of(io["x2"], i)).then_inc(S["x_in"], 16)
                    if more:
                        sp.wait_ge(S["q_t_made"], (i + 1) * TB)
                        sp.sem_inc(S["passed_sp"], 1)
                        sp.dma_start(q[:], block_of(io["q"], i + 1)).then_inc(S["q_in"], 16)
                    sp.wait_ge(S["base_ready"], i + 1)
                    sp.dma_start(block_of(io["base"], i), x[:]).then_inc(S["stored"], 16)
                    sp.wait_ge(S["stored"], (i + 1) * 16)
                    sp.sem_inc(S["passed_sp"], 1)

                sp.dma_start(q[:], block_of(io["q"], 0)).then_inc(S["q_in"], 16)
                with sp.Fori(0, NBLK - 1) as i:
                    move(i, True)
                move(NBLK - 1, False)
                sp.wait_ge(S["weights_in"], 16 * len(W))

            @block.vector
            def _(dve):
                link = Link(dve, S["chain"])
                dve.wait_ge(S["weights_in"], 16 * len(W))
                with dve.Fori(0, NBLK) as i:
                    link.loop(i, 19)

                    def normed(n, a, out):
                        row_moments(nc, link, a, stats, mv[:, n], S["passed"]).then_inc(S["moments_ready"], 1)
                        dve.wait_ge(S["std_ready"], i * 3 + n + 1)
                        link(nc.vector.reciprocal(rstd[:, n, :], std[:, n, :]))
                        for j in range(TB):
                            last = nc.vector.tensor_scalar(out[:, j, :], a[:, j, :], mv[:, n, j, 0:1], rstd[:, n, j:j + 1],
                                                           ALU.subtract, ALU.mult)
                        return last

                    mine = acc[:, bass.ds(i * TB, TB), :]
                    link(nc.vector.tensor_scalar(den[:], mine[:, :, D:ROW], 1e-30, None, ALU.max))
                    link(nc.vector.reciprocal(den[:], den[:]))
                    for h in range(H):
                        last = nc.vector.tensor_tensor(gat[:, :, h * 32:(h + 1) * 32], mine[:, :, h * 32:(h + 1) * 32],
                                                       cast(den[:, :, h], 32), ALU.mult)
                    link(last)
                    link(nc.vector.tensor_tensor(gat[:], gat[:], rows(gat_bias), ALU.add))
                    link(normed(0, gat, gat))
                    link(nc.vector.tensor_tensor(gat[:], gat[:], rows(gamma), ALU.mult))
                    link(nc.vector.tensor_tensor(gat[:], gat[:], rows(beta), ALU.add))
                    dve.wait_ge(S["x_in"], (i + 1) * 16)
                    link(nc.vector.tensor_tensor(x[:], x[:], gat[:], ALU.add))
                    dve.wait_ge(S["mix_copied"], (i + 1) * TB)
                    link(normed(1, mix, mix))
                    link(nc.vector.tensor_tensor(mix[:], mix[:], rows(mix_gamma), ALU.mult))
                    link(nc.vector.tensor_tensor(x[:], x[:], mix[:], ALU.add))
                    normed(2, x, xn).then_inc(S["xn_ready"], 1)
                    dve.wait_ge(S["xn_ready"], i + 1)
                    nc.vector.tensor_tensor(x[:], x[:], xn[:], ALU.add).then_inc(S["base_ready"], 1)
                    link(nc.vector.tensor_tensor(gat[:], xn[:], rows(wr), ALU.mult))
                    link(nc.vector.tensor_reduce(weight[:], gat[:], AX.X, ALU.add))
                    nc.vector.tensor_scalar(keep["score"][:, bass.ds(i * TB, TB)], weight[:], br[:, 0:1], None, ALU.add)
                    for j in range(TB):
                        dve.wait_ge(S["down_made"], i * TB + j + 1)
                        nc.vector.tensor_tensor(acc[:, bass.ds(i * TB + j, 1), 0:D].rearrange("p a d -> p (a d)"),
                                                ps_o[j % 2][:, 0:D], b2[:], ALU.add).then_inc(S["down_added"], 1)
                link.leave(NBLK)

            @block.scalar
            def _(act):
                act.wait_ge(S["weights_in"], 16 * len(W))
                with act.Fori(0, NBLK) as i:
                    def root(n):
                        act.wait_ge(S["moments_ready"], i * 3 + n + 1)
                        nc.scalar.activation(std[:, n, :], mv[:, n, :, 1], ACT.Sqrt, bias=eps).then_inc(S["std_ready"], 1)

                    for j in range(TB):
                        act.wait_ge(S["q_t_made"], i * TB + j + 1)
                        nc.scalar.activation(q_t[:, j % 2], ps_a[j % 2][:, 0:D], ACT.Copy).then_inc(S["q_t_copied"], 1)
                        act.wait_ge(S["mixed"], i * TB + j + 1)
                        nc.scalar.activation(mix[:, j, :], ps_h[j % 2][:, 0:D], ACT.Copy).then_inc(S["mix_copied"], 1)
                    for n in range(3):
                        root(n)
                    for j in range(TB):
                        act.wait_ge(S["xt_made"], i * TB + j + 1)
                        nc.scalar.activation(xt[:, :, j * P:(j + 1) * P],
                                             ps_a[j % 2][:, 0:D].rearrange("p (k n) -> p k n", k=DC), ACT.Copy)\
                            .then_inc(S["xt_copied"], 1)
                    for n in range(2 * HC):
                        o, half = n // 2, n % 2
                        act.wait_ge(S["up_made"], i * (2 * HC) + n + 1)
                        nc.scalar.activation(hid[:, o, half * HALF:(half + 1) * HALF], ps_h[n % 4][:, 0:HALF],
                                             ACT.Gelu_apprx_tanh, bias=b1[:, o:o + 1]).then_inc(S["hid_ready"], 1)

            @block.tensor
            def _(pe):
                pe.wait_ge(S["weights_in"], 16 * len(W))
                with pe.Fori(0, NBLK) as i:
                    pe.wait_ge(S["q_in"], (i + 1) * 16)
                    for j in range(TB):
                        if j >= 2:
                            pe.wait_ge(S["q_t_copied"], i * TB + j - 1)
                        for c in range(DC):
                            last = nc.tensor.transpose(ps_a[j % 2][:, c * P:(c + 1) * P], q[:, j, c * P:(c + 1) * P], ident)
                        last.then_inc(S["q_t_made"], 1)
                        pe.wait_ge(S["q_t_copied"], i * TB + j + 1)
                        if j >= 2:
                            pe.wait_ge(S["mix_copied"], i * TB + j - 1)
                        for c in range(DC):
                            last = nc.tensor.matmul(ps_h[j % 2][:, 0:D], q_t[:, j % 2, c * P:(c + 1) * P], keep["kw"][:, c, :],
                                                    start=c == 0, stop=c == DC - 1)
                        last.then_inc(S["mixed"], 1)
                    pe.wait_ge(S["xn_ready"], i + 1)
                    for j in range(TB):
                        if j >= 2:
                            pe.wait_ge(S["xt_copied"], i * TB + j - 1)
                        for c in range(DC):
                            last = nc.tensor.transpose(ps_a[j % 2][:, c * P:(c + 1) * P], xn[:, j, c * P:(c + 1) * P], ident)
                        last.then_inc(S["xt_made"], 1)
                    pe.wait_ge(S["xt_copied"], (i + 1) * TB)
                    for n in range(2 * HC):
                        o, half = n // 2, n % 2
                        if n >= 4:
                            pe.wait_ge(S["hid_ready"], i * (2 * HC) + n - 3)
                        for c in range(DC):
                            last = nc.tensor.matmul(ps_h[n % 4][:, 0:HALF], w1[:, c, o * P:(o + 1) * P],
                                                    xt[:, c, half * HALF:(half + 1) * HALF], start=c == 0, stop=c == DC - 1)
                        last.then_inc(S["up_made"], 1)
                    pe.wait_ge(S["hid_ready"], (i + 1) * (2 * HC))
                    for j in range(TB):
                        if j >= 2:
                            pe.wait_ge(S["down_added"], i * TB + j - 1)
                        for c in range(HC):
                            last = nc.tensor.matmul(ps_o[j % 2][:, 0:D], hid[:, c, j * P:(j + 1) * P], w2[:, c, :],
                                                    start=c == 0, stop=c == HC - 1)
                        last.then_inc(S["down_made"], 1)


def select_stage(nc, keep, io):
    with Stage(nc, "select") as st:
        bits = st.sb("bits", [P, 34], I32)
        key = st.sb("key", [P, 1], I32)
        cand = st.sb("cand", [P, 1], I32)
        flip = st.sb("flip", [P, 1], I32)
        value = st.sb("value", [P, 1], I32)
        took = st.sb("took", [P, 1], I32)
        count = st.sb("count", [P, 1])
        above = st.sb("above", [P, NT])
        equal = st.sb("equal", [P, NT])
        before = st.sb("before", [P, NT])
        tiles = st.sb("tiles", [P, NT])
        ones_row = st.sb("ones_row", [P, NT])
        scale = st.sb("scale", [P, NT])
        base = st.sb("base", [P, TB, D])
        ps_n = st.banks("ps_n", 1)[0]
        ps_p = st.banks("ps_p", 1)[0]
        S = {n: st.sem(n) for n in ("bits_in chain counted totalled equal_ready prefixes_made base_in scaled stored "
                                    "passed ").split()}
        score, acc = keep["score"], keep["acc"]
        with nc.Block() as block:
            @block.sync
            def _(sp):
                sp.dma_start(bits[:], io["bits"]).then_inc(S["bits_in"], 16)
                with sp.Fori(0, NBLK) as i:
                    sp.dma_start(base[:], block_of(io["base"], i)).then_inc(S["base_in"], 16)
                    sp.wait_ge(S["scaled"], i + 1)
                    sp.dma_start(block_of(io["out"], i), base[:]).then_inc(S["stored"], 16)
                    sp.wait_ge(S["stored"], (i + 1) * 16)
                    sp.sem_inc(S["passed"], 1)

            @block.vector
            def _(dve):
                link = Link(dve, S["chain"])
                valid = keep["valid"]

                def as_float():
                    link(nc.vector.tensor_single_scalar(flip[:], cand[:], 31, ALU.arith_shift_right))
                    link(nc.vector.tensor_tensor(flip[:], flip[:], bits[:, 33:34], ALU.bitwise_xor))
                    link(nc.vector.tensor_tensor(flip[:], flip[:], bits[:, 32:33], ALU.bitwise_or))
                    link(nc.vector.tensor_tensor(value[:], cand[:], flip[:], ALU.bitwise_xor))

                nc.vector.memset(ones_row[:], 1.0)
                link(nc.vector.memset(key[:], 0))
                dve.wait_ge(S["bits_in"], 16)
                with dve.Fori(0, 32) as b:
                    link.loop(b, 8)
                    bit = bits[:, bass.ds(b, 1)]
                    link(nc.vector.tensor_tensor(cand[:], key[:], bit, ALU.bitwise_or))
                    as_float()
                    nc.vector.scalar_tensor_tensor(above[:], score[:], value[:].bitcast(F32)[:, 0:1], valid, ALU.is_ge,
                                                   ALU.mult, accum_out=count[:]).then_inc(S["counted"], 1)
                    dve.wait_ge(S["totalled"], b + 1)
                    link(nc.vector.tensor_scalar(took[:], ps_n[:, 0:1], TOPK_KEEP - 0.5, -1.0, ALU.is_ge, ALU.mult))
                    link(nc.vector.tensor_tensor(took[:], took[:], bit, ALU.bitwise_and))
                    link(nc.vector.tensor_tensor(key[:], key[:], took[:], ALU.bitwise_or))
                link.leave(32)
                link(nc.vector.tensor_tensor(cand[:], key[:], key[:], ALU.bitwise_or))
                as_float()
                threshold = value[:].bitcast(F32)[:, 0:1]
                link(nc.vector.scalar_tensor_tensor(above[:], score[:], threshold, valid, ALU.is_gt, ALU.mult,
                                                    accum_out=count[:]))
                nc.vector.scalar_tensor_tensor(equal[:], score[:], threshold, valid, ALU.is_equal, ALU.mult)\
                    .then_inc(S["equal_ready"], 1)
                dve.wait_ge(S["prefixes_made"], 1)
                nc.vector.tensor_copy(before[:], ps_p[:, 0:NT])
                link(nc.vector.tensor_copy(tiles[:], ps_p[:, 64:64 + NT]))
                nc.vector.tensor_copy(count[:], ps_p[:, 128:129])
                link(nc.vector.tensor_tensor(before[:], before[:], tiles[:], ALU.subtract))
                link(nc.vector.tensor_tensor_scan(tiles[:], ones_row[:], tiles[:], 0.0, ALU.mult, ALU.add))
                link(nc.vector.tensor_tensor(before[:], before[:], tiles[:], ALU.add))
                link(nc.vector.tensor_scalar(before[:], before[:], count[:, 0:1], TOPK_KEEP - 0.5, ALU.add, ALU.is_lt))
                link(nc.vector.tensor_tensor(equal[:], equal[:], before[:], ALU.mult))
                link(nc.vector.tensor_tensor(above[:], above[:], equal[:], ALU.add))
                link(nc.vector.tensor_tensor(scale[:], above[:], score[:], ALU.mult))
                with dve.Fori(0, NBLK) as i:
                    dve.wait_ge(S["base_in"], (i + 1) * 16)
                    for j in range(TB):
                        last = nc.vector.scalar_tensor_tensor(
                            base[:, j, :], acc[:, bass.ds(i * TB + j, 1), 0:D].rearrange("p a d -> p (a d)"),
                            scale[:, bass.ds(i * TB + j, 1)], base[:, j, :], ALU.mult, ALU.add)
                    last.then_inc(S["scaled"], 1)

            @block.tensor
            def _(pe):
                with pe.Fori(0, 32) as b:
                    pe.wait_ge(S["counted"], b + 1)
                    nc.tensor.matmul(ps_n[:, 0:1], col(keep, "ones"), count[:], start=True, stop=True)\
                        .then_inc(S["totalled"], 1)
                pe.wait_ge(S["equal_ready"], 1)
                nc.tensor.matmul(ps_p[:, 0:NT], col(keep, "below"), equal[:], start=True, stop=True)
                nc.tensor.matmul(ps_p[:, 64:64 + NT], col(keep, "ones"), equal[:], start=True, stop=True)
                nc.tensor.matmul(ps_p[:, 128:129], col(keep, "ones"), count[:], start=True, stop=True)\
                    .then_inc(S["prefixes_made"], 1)


def build(nc, io):
    for name, width in (("table0", D + 4), ("table1", D + 8), ("q", D), ("k", D), ("v", D), ("xn", D), ("x2", D),
                        ("base", D)):
        io[name] = nc.dram_tensor(name, (NPAD, width), F32).ap()
    with ExitStack() as stack:
        def sb(name, shape, dt=F32):
            return stack.enter_context(nc.sbuf_tensor(name, shape, dt))
        keep = {
            "const": sb("const", [P, CONST_W]),
            "acc": sb("acc", [P, NTA, D + 8]),
            "left_max": sb("left_max", [P, NTA, 8]),
            "right": sb("right", [P, NTA, 8]),
            "macro_of": sb("macro_of", [P, NSTEP], I32),
            "packed": sb("packed", [P, (NSTEP - 2) // 2], I32),
            "node0": sb("node0", [P, NSTEP]),
            "last_step": sb("last_step", [P, NM], I32),
            "kw": sb("kw", [P, DC, D]),
            "k_max": sb("k_max", [P, D]),
            "iota_b": sb("iota_b", [P, P, G], mybir.dt.bfloat16),
            "score": sb("score", [P, NT]),
        }
        keep["valid"], keep["negpad"] = col(keep, "valid"), col(keep, "negpad")
        schedule_stage(nc, keep, io)
        pre_stage(nc, keep, io, 0)
        edge_stage(nc, keep, io, 0)
        moe_stage(nc, keep, io)
        pre_stage(nc, keep, io, 1)
        edge_stage(nc, keep, io, 1)
        context_stage(nc, keep, io)
        mlp_stage(nc, keep, io)
        select_stage(nc, keep, io)


def _constants():
    import numpy as np
    c = np.zeros((P, CONST_W), np.float32)

    def put(name, a):
        c[:, slice(*CONST[name])] = a
    p = np.arange(P)
    node = np.arange(NT)[None, :] * P + p[:, None]
    put("ident", np.eye(P))
    put("ones", 1.0)
    put("iota", p[None, :])
    put("valid", node < N)
    put("negpad", np.where(node < N, 0.0, -BIG))
    put("blockmask", p[:, None] // 32 == p[None, :] // 32)
    put("steps", np.arange(NSTEP)[None, :])
    put("macros", np.arange(NM)[None, :])
    put("index", node)
    for heads in (4, 8):
        channel = np.arange(DC)[None, :, None] * P + p[:, None, None]
        put(f"head{heads}", (channel // (D // heads) == np.arange(heads)[None, None, :]).reshape(P, -1))
    put("earlier", np.array([f < e for e in range(N_EXP) for f in range(N_EXP)])[None, :])
    put("eps", LN_EPS)
    put("below", p[:, None] < p[None, :])
    return c


def _layout(inputs):
    import numpy as np
    g = {k: np.asarray(a) for k, a in inputs.items()}

    def chunks(w):
        return np.ascontiguousarray(w.reshape(-1, P, w.shape[-1]).transpose(1, 0, 2))

    def each(w):
        return np.ascontiguousarray(w.reshape(w.shape[0], -1, P, w.shape[-1]).transpose(2, 0, 1, 3))

    def down(b):
        return np.ascontiguousarray(np.moveaxis(b.reshape(*b.shape[:-1], -1, P), -1, 0))

    def rep(b):
        return np.ascontiguousarray(np.broadcast_to(b.reshape(1, -1), (P, b.size)))

    x = np.zeros((NPAD, D), np.float32)
    x[:N] = g["x"]
    edges = {}
    for name, fill in (("src", 0), ("dst", 8191)):
        a = np.full(NM * ME, fill, np.int32)
        a[:E] = g[name]
        edges[name] = a
    ends = edges["dst"][ME - 1::ME]
    ends_col = np.full((P, 1), 8191 * 4, np.int32)
    ends_col[:NM, 0] = ends
    bits = np.array([1 << b for b in range(31, -1, -1)] + [1 << 31, 0xFFFFFFFF], np.uint32).view(np.int32)
    out = {
        "const": _constants(), "bits": rep(bits), "x0": x, "ends_row": rep(ends), "ends_col": ends_col,
        "src": np.ascontiguousarray(edges["src"].reshape(-1, P).T), "dst": np.ascontiguousarray(edges["dst"].reshape(-1, P).T),
        "l0_w_gat": chunks(g["L0_gnn_W"]), "l1_w_gat": chunks(g["L1_gnn_W"]),
        "l0_attn": np.stack([down(g["L0_gnn_attn_l"].reshape(-1)), down(g["L0_gnn_attn_r"].reshape(-1))], axis=2),
        "l1_attn": np.stack([down(g["L1_gnn_att_src"].reshape(-1)), down(g["L1_gnn_att_dst"].reshape(-1))], axis=2),
        "l0_gat_bias": rep(g["L0_gnn_bias"]), "l0_w_qkv": chunks(g["L0_mix_W_qkv"]), "l0_b_qkv": rep(g["L0_mix_b_qkv"]),
        "l0_w_out": chunks(g["L0_mix_W_out"]), "l0_b_out": rep(g["L0_mix_b_out"]),
        "r_w1": chunks(g["L0_ffn_router_w1"]), "r_b1": down(g["L0_ffn_router_b1"]),
        "r_w2": g["L0_ffn_router_w2"], "r_b2": rep(g["L0_ffn_router_b2"]),
        "e_w1": each(g["L0_ffn_expert_w1"]), "e_b1": down(g["L0_ffn_expert_b1"]),
        "e_w2": each(g["L0_ffn_expert_w2"]), "e_b2": down(g["L0_ffn_expert_b2"]),
        "e_w3": each(g["L0_ffn_expert_w3"]), "e_b3": g["L0_ffn_expert_b3"],
        "l1_gat_bias": rep(g["L1_gnn_bias"]), "l1_gamma": rep(g["L1_gnn_gamma"]), "l1_beta": rep(g["L1_gnn_beta"]),
        "l1_w_qkv": chunks(g["L1_mix_Wqkv"]), "l1_w_out": chunks(g["L1_mix_Wout"]), "l1_mix_gamma": rep(g["L1_mix_gamma"]),
        "f_wr": rep(g["L1_ffn_wr"]), "f_br": rep(g["L1_ffn_br"]), "f_w1": chunks(g["L1_ffn_w1"]), "f_b1": down(g["L1_ffn_b1"]),
        "f_w2": chunks(g["L1_ffn_w2"]), "f_b2": rep(g["L1_ffn_b2"]),
    }
    return {k: np.ascontiguousarray(a) for k, a in out.items()}


def kernel(**inputs):
    import concourse.bacc as bacc
    from concourse.bass_utils import run_bass_kernel_spmd

    nc = bacc.Bacc("TRN2", target_bir_lowering=False, num_devices=1)
    arrays = {f"in_{name}": a for name, a in _layout(inputs).items()}
    io = {name[3:]: nc.dram_tensor(name, a.shape, mybir.dt.from_np(a.dtype), kind="ExternalInput").ap()
          for name, a in arrays.items()}
    io["out"] = nc.dram_tensor("out", (NPAD, D), F32, kind="ExternalOutput").ap()
    build(nc, io)
    result = run_bass_kernel_spmd(nc, [arrays], core_ids=[0])
    return result.results[0]["out"][:N]
```
